# Optimizing a Trainium2 kernel written in Bass

```python
import numpy as np
import jax
import jax.numpy as jnp

def _softmax(x, axis=-1):
    return jax.nn.softmax(x, axis=axis)

def _gelu(x):
    return jax.nn.gelu(x, approximate=True)

def _silu(x):
    return jax.nn.silu(x)

def _sigmoid(x):
    return jax.nn.sigmoid(x)

def _layernorm(x, axis=-1, eps=1e-05):
    m = jnp.mean(x, axis=axis, keepdims=True)
    v = jnp.var(x, axis=axis, keepdims=True)
    return (x - m) / jnp.sqrt(v + eps)

def _scatter_add(tgt, idx, src, axis=0):
    return tgt.at[idx].add(src)

def _segment_sum(src, seg, n):
    return jax.ops.segment_sum(src, seg, n)
kernel_name = 'mk_gnn_preln_d4_gnn_r32_c3e357'

def setup_inputs(seed: int=0):
    np.random.seed(seed)
    _w = jnp.asarray

    def _rec_inputs():
        import jax
        import jax.numpy as jnp
        _gk = jax.random.key(seed)
        x = -0.000202 + 1 * jax.random.normal(jax.random.fold_in(_gk, 1), (50000, 64), jnp.float32)
        src = jax.random.randint(jax.random.fold_in(_gk, 2), (50000,), 0, 50000, jnp.int32)
        dst = jax.random.randint(jax.random.fold_in(_gk, 3), (50000,), 0, 50000, jnp.int32)
        _o = jnp.argsort(dst, stable=True)
        src = src[_o]
        dst = dst[_o]
        edge_attr_64 = -8.16379e-05 + 0.999858 * jax.random.normal(jax.random.fold_in(_gk, 12), (50000, 64), jnp.float32)
        return (x, src, dst, edge_attr_64)
    x, src, dst, edge_attr_64 = _rec_inputs()

    def _L0_gnn_setup():
        import jax, jax.numpy as jnp
        import numpy as np
        N_NODES = 3125
        N_EDGES = 50000
        IN_CH = 64
        OUT_CH = 64
        key = jax.random.key(seed)
        ks = jax.random.split(key, 6)
        x = jax.random.normal(ks[0], (N_NODES, IN_CH), dtype=jnp.float32)
        edge_index = jax.random.randint(ks[1], (2, N_EDGES), 0, N_NODES, dtype=jnp.int64)
        W1 = jax.random.normal(ks[2], (2 * IN_CH, OUT_CH), dtype=jnp.float32) * (1.0 / np.sqrt(2 * IN_CH))
        b1 = jnp.zeros((OUT_CH,), dtype=jnp.float32)
        W2 = jax.random.normal(ks[3], (OUT_CH, OUT_CH), dtype=jnp.float32) * (1.0 / np.sqrt(OUT_CH))
        b2 = jnp.zeros((OUT_CH,), dtype=jnp.float32)
        return {'x': x, 'edge_index': edge_index, 'W1': W1, 'b1': b1, 'W2': W2, 'b2': b2}
    _L0_gnn_all = _L0_gnn_setup()
    _L0_gnn_in = {k: v for k, v in _L0_gnn_all.items() if k in ('W1', 'b1', 'W2', 'b2')}
    del _L0_gnn_all

    def _L1_gnn_setup():
        import jax, jax.numpy as jnp
        import numpy as np
        N = 3125
        E = 50000
        D = 64
        BN_EPS = 1e-05
        LEAKY_SLOPE = 0.01
        key = jax.random.key(seed)
        ks = jax.random.split(key, 8)
        s = 1.0 / np.sqrt(D)
        return {'x': jax.random.normal(ks[0], (N, D), jnp.float32), 'edge_index': jax.random.randint(ks[1], (2, E), 0, N, dtype=jnp.int32), 'W1': jax.random.uniform(ks[2], (D, D), jnp.float32, -s, s), 'b1': jnp.zeros((D,), jnp.float32), 'gamma': jnp.ones((D,), jnp.float32), 'beta': jnp.zeros((D,), jnp.float32), 'W2': jax.random.uniform(ks[3], (D, D), jnp.float32, -s, s), 'b2': jnp.zeros((D,), jnp.float32)}
    _L1_gnn_all = _L1_gnn_setup()
    _L1_gnn_in = {k: v for k, v in _L1_gnn_all.items() if k in ('W1', 'b1', 'gamma', 'beta', 'W2', 'b2')}
    del _L1_gnn_all

    def _L2_gnn_setup():
        import jax, jax.numpy as jnp
        import numpy as np
        N_NODES = 3125
        N_EDGES = 37500
        D_IN = 64
        D_OUT = 64
        key = jax.random.key(seed)
        k1, k2, k3, k4 = jax.random.split(key, 4)
        features = jax.random.normal(k1, (N_NODES, D_IN), dtype=jnp.float32)
        edge_index = jax.random.randint(k2, (2, N_EDGES), 0, N_NODES, dtype=jnp.int64)
        W = jax.random.normal(k3, (2 * D_IN, D_OUT), dtype=jnp.float32) * (1.0 / np.sqrt(2 * D_IN))
        b = jax.random.normal(k4, (D_OUT,), dtype=jnp.float32) * 0.01
        return {'features': features, 'edge_index': edge_index, 'W': W, 'b': b}
    _L2_gnn_all = _L2_gnn_setup()
    _L2_gnn_in = {k: v for k, v in _L2_gnn_all.items() if k in ('W', 'b')}
    del _L2_gnn_all

    def _L3_gnn_setup():
        import jax, jax.numpy as jnp
        import numpy as np
        N, D = (3125, 64)
        E, DE = (50000, 64)
        MSG_H, MSG_OUT = (128, 64)
        NODE_H = 128
        LN_EPS = 1e-05
        key = jax.random.key(seed)
        ks = jax.random.split(key, 10)

        def glorot(k, shape):
            fan_in = shape[0]
            return jax.random.normal(k, shape, jnp.float32) / jnp.sqrt(jnp.float32(fan_in))
        return {'nodes': jax.random.normal(ks[0], (N, D), jnp.float32), 'edges': jax.random.normal(ks[1], (E, DE), jnp.float32), 'senders': jax.random.randint(ks[2], (E,), 0, N, jnp.int32), 'receivers': jax.random.randint(ks[3], (E,), 0, N, jnp.int32), 'msg_W1': glorot(ks[4], (2 * D + DE, MSG_H)), 'msg_b1': jnp.zeros((MSG_H,), jnp.float32), 'msg_W2': glorot(ks[5], (MSG_H, MSG_OUT)), 'msg_b2': jnp.zeros((MSG_OUT,), jnp.float32), 'node_W1': glorot(ks[6], (D + MSG_OUT, NODE_H)), 'node_b1': jnp.zeros((NODE_H,), jnp.float32), 'node_W2': glorot(ks[7], (NODE_H, D)), 'node_b2': jnp.zeros((D,), jnp.float32), 'ln_scale': jnp.ones((D,), jnp.float32), 'ln_offset': jnp.zeros((D,), jnp.float32)}
    _L3_gnn_all = _L3_gnn_setup()
    _L3_gnn_in = {k: v for k, v in _L3_gnn_all.items() if k in ('msg_W1', 'msg_b1', 'msg_W2', 'msg_b2', 'node_W1', 'node_b1', 'node_W2', 'node_b2', 'ln_scale', 'ln_offset')}
    del _L3_gnn_all
    return {'x': x, 'src': src, 'dst': dst, 'edge_attr_64': edge_attr_64, 'L0_gnn_W1': _L0_gnn_in['W1'], 'L0_gnn_b1': _L0_gnn_in['b1'], 'L0_gnn_W2': _L0_gnn_in['W2'], 'L0_gnn_b2': _L0_gnn_in['b2'], 'L1_gnn_W1': _L1_gnn_in['W1'], 'L1_gnn_b1': _L1_gnn_in['b1'], 'L1_gnn_gamma': _L1_gnn_in['gamma'], 'L1_gnn_beta': _L1_gnn_in['beta'], 'L1_gnn_W2': _L1_gnn_in['W2'], 'L1_gnn_b2': _L1_gnn_in['b2'], 'L2_gnn_W': _L2_gnn_in['W'], 'L2_gnn_b': _L2_gnn_in['b'], 'L3_gnn_msg_W1': _L3_gnn_in['msg_W1'], 'L3_gnn_msg_b1': _L3_gnn_in['msg_b1'], 'L3_gnn_msg_W2': _L3_gnn_in['msg_W2'], 'L3_gnn_msg_b2': _L3_gnn_in['msg_b2'], 'L3_gnn_node_W1': _L3_gnn_in['node_W1'], 'L3_gnn_node_b1': _L3_gnn_in['node_b1'], 'L3_gnn_node_W2': _L3_gnn_in['node_W2'], 'L3_gnn_node_b2': _L3_gnn_in['node_b2'], 'L3_gnn_ln_scale': _L3_gnn_in['ln_scale'], 'L3_gnn_ln_offset': _L3_gnn_in['ln_offset']}

def reference(x, src, dst, edge_attr_64, L0_gnn_W1, L0_gnn_b1, L0_gnn_W2, L0_gnn_b2, L1_gnn_W1, L1_gnn_b1, L1_gnn_gamma, L1_gnn_beta, L1_gnn_W2, L1_gnn_b2, L2_gnn_W, L2_gnn_b, L3_gnn_msg_W1, L3_gnn_msg_b1, L3_gnn_msg_W2, L3_gnn_msg_b2, L3_gnn_node_W1, L3_gnn_node_b1, L3_gnn_node_W2, L3_gnn_node_b2, L3_gnn_ln_scale, L3_gnn_ln_offset):
    import jax
    import jax.numpy as jnp

    def _L0_gnn_ref(x, edge_index, W1, b1, W2, b2):
        import jax, jax.numpy as jnp
        import numpy as np
        N_NODES = 3125
        N_EDGES = 50000
        IN_CH = 64
        OUT_CH = 64
        src = edge_index[0]
        dst = edge_index[1]
        x_i = x[dst]
        x_j = x[src]
        edge_features = jnp.concatenate([x_i, x_j - x_i], axis=-1)
        h = jax.nn.relu(edge_features @ W1 + b1)
        edge_messages = h @ W2 + b2
        out = jax.ops.segment_max(edge_messages, dst, num_segments=x.shape[0])
        return jnp.where(jnp.isfinite(out), out, jnp.zeros_like(out))

    def _L1_gnn_ref(x, edge_index, W1, b1, gamma, beta, W2, b2):
        import jax, jax.numpy as jnp
        import numpy as np
        N = 3125
        E = 50000
        D = 64
        BN_EPS = 1e-05
        LEAKY_SLOPE = 0.01
        n = x.shape[0]
        loops = jnp.arange(n, dtype=edge_index.dtype)
        src = jnp.concatenate([edge_index[0], loops])
        dst = jnp.concatenate([edge_index[1], loops])
        deg = jax.ops.segment_sum(jnp.ones_like(dst, dtype=x.dtype), dst, num_segments=n)
        dinv = jnp.where(deg > 0, jax.lax.rsqrt(jnp.maximum(deg, 1.0)), 0.0)
        norm = dinv[src] * dinv[dst]

        def gcn(h, W, b):
            h = h @ W
            msg = h[src] * norm[:, None]
            return jax.ops.segment_sum(msg, dst, num_segments=n) + b
        h = gcn(x, W1, b1)
        mu = jnp.mean(h, axis=0)
        var = jnp.mean((h - mu) ** 2, axis=0)
        h = gamma * (h - mu) * jax.lax.rsqrt(var + BN_EPS) + beta
        h = jnp.where(h >= 0, h, LEAKY_SLOPE * h)
        return gcn(h, W2, b2)

    def _L2_gnn_ref(features, edge_index, W, b):
        import jax, jax.numpy as jnp
        import numpy as np
        N_NODES = 3125
        N_EDGES = 37500
        D_IN = 64
        D_OUT = 64
        n = features.shape[0]
        src, dst = (edge_index[0], edge_index[1])
        gathered = features[src]
        summed = jax.ops.segment_sum(gathered, dst, num_segments=n)
        deg = jax.ops.segment_sum(jnp.ones((src.shape[0],), dtype=features.dtype), dst, num_segments=n)
        neighbour = summed / jnp.maximum(deg, 1.0)[:, None]
        h = jnp.concatenate([features, neighbour], axis=1)
        return h @ W + b

    def _L3_gnn_ref(nodes, edges, senders, receivers, msg_W1, msg_b1, msg_W2, msg_b2, node_W1, node_b1, node_W2, node_b2, ln_scale, ln_offset):
        import jax, jax.numpy as jnp
        import numpy as np
        N, D = (3125, 64)
        E, DE = (50000, 64)
        MSG_H, MSG_OUT = (128, 64)
        NODE_H = 128
        LN_EPS = 1e-05
        x = jnp.concatenate([nodes[senders], nodes[receivers], edges], axis=-1)
        h = jax.nn.relu(x @ msg_W1 + msg_b1)
        messages = jax.nn.relu(h @ msg_W2 + msg_b2)
        agg = jax.ops.segment_sum(messages, receivers, num_segments=nodes.shape[0])
        y = jnp.concatenate([nodes, agg], axis=-1)
        y = jax.nn.relu(y @ node_W1 + node_b1)
        y = y @ node_W2 + node_b2
        mean = jnp.mean(y, axis=-1, keepdims=True)
        var = jnp.var(y, axis=-1, keepdims=True)
        y = (y - mean) * jax.lax.rsqrt(var + LN_EPS) * ln_scale + ln_offset
        return nodes + y
    edge_index = jnp.stack([src, dst])
    h = jnp.maximum(_layernorm(x, axis=-1), 0.0)
    x = x + _L0_gnn_ref(h, edge_index, L0_gnn_W1, L0_gnn_b1, L0_gnn_W2, L0_gnn_b2)
    h = jnp.maximum(_layernorm(x, axis=-1), 0.0)
    x = x + _L1_gnn_ref(h, edge_index, L1_gnn_W1, L1_gnn_b1, L1_gnn_gamma, L1_gnn_beta, L1_gnn_W2, L1_gnn_b2)
    h = jnp.maximum(_layernorm(x, axis=-1), 0.0)
    x = x + _L2_gnn_ref(h, edge_index, L2_gnn_W, L2_gnn_b)
    h = jnp.maximum(_layernorm(x, axis=-1), 0.0)
    x = x + _L3_gnn_ref(h, edge_attr_64, src, dst, L3_gnn_msg_W1, L3_gnn_msg_b1, L3_gnn_msg_W2, L3_gnn_msg_b2, L3_gnn_node_W1, L3_gnn_node_b1, L3_gnn_node_W2, L3_gnn_node_b2, L3_gnn_ln_scale, L3_gnn_ln_offset)
    return x

_drawn_inputs = setup_inputs


def setup_inputs(seed=0):
    import zlib

    import numpy as np

    out = dict(_drawn_inputs(seed))
    spreads = {'L0_gnn_b1': (0.0, 0.1),
     'L0_gnn_b2': (0.0, 0.1),
     'L1_gnn_b1': (0.0, 0.8),
     'L1_gnn_gamma': (1.0, 0.2),
     'L1_gnn_beta': (0.0, 0.1),
     'L1_gnn_b2': (0.0, 0.1),
     'L3_gnn_msg_b1': (0.0, 0.1),
     'L3_gnn_msg_b2': (0.0, 0.1),
     'L3_gnn_node_b1': (0.0, 0.1),
     'L3_gnn_node_b2': (0.0, 0.1),
     'L3_gnn_ln_scale': (1.0, 0.2),
     'L3_gnn_ln_offset': (0.0, 0.1)}
    factors = {'L2_gnn_b': 5.953}
    for name, (base, spread) in spreads.items():
        noise = np.random.default_rng([zlib.crc32(name.encode()), seed]).standard_normal(out[name].shape)
        drawn = base * np.exp(spread * noise) if base else spread * noise
        out[name] = jnp.asarray(drawn.astype(out[name].dtype))
    for name, factor in factors.items():
        out[name] = (out[name] * factor).astype(out[name].dtype)
    return out
```

```python
from contextlib import ExitStack

import concourse.bass as bass
from concourse import mybir

F32 = mybir.dt.float32
F16 = mybir.dt.float16
I32 = mybir.dt.int32
ALU = mybir.AluOpType
ACT = mybir.ActivationFunctionType
AX_X = mybir.AxisListType.X
RMAX = bass.bass_isa.ReduceOp.max

P = 128
D = 64
HID = 128
N_TRUE = 50000
TILES = 392
GT = 4
GROUPS = TILES // GT
GR = GT * P
N = TILES * P
WP, WK = 96, 2
WIN = WP * WK
MW = D + 2
UNROLL = 4
EPS = 1e-5
SLOPE = 0.01
FAR = -3.0e38


class Turn:

    def __init__(self, i, part, n):
        self.i, self.part, self.n = i, part, n
        self.known = isinstance(i, int)

    def at(self, lag):
        slot = (self.part - lag) % UNROLL
        turn = self.i + (self.part - lag - slot) // UNROLL
        g = self.i * UNROLL + (self.part - lag)
        if self.known and not 0 <= g < self.n:
            return None
        return Group(g, turn, slot, self.known)


class Group:

    def __init__(self, g, turn, slot, known):
        self.g, self.turn, self.slot, self.pair, self.known = g, turn, slot, slot % 2, known

    def from_(self, k):
        return not self.known or self.g >= k


class Tally:

    def __init__(self, sem):
        self.counter, self.base, self.used = sem, 0, False

    @property
    def sem(self):
        self.used = True
        return self.counter

    def wait(self, eng, t, back=0):
        if t.from_(back):
            eng.wait_ge(self.counter, t.g + (1 - back + self.base))


class Landing:

    def __init__(self, sems):
        self.sems, self.base = sems, [0] * len(sems)

    def wait(self, eng, t, dmas, back=0):
        if t.from_(back * UNROLL):
            eng.wait_ge(self.sems[t.slot], t.turn * (16 * dmas) + ((1 - back) * 16 * dmas + self.base[t.slot]))

    def held(self, slot, n):
        return (n - slot + UNROLL - 1) // UNROLL

    def wait_all(self, eng, dmas, n):
        for s in range(UNROLL):
            eng.wait_ge(self.sems[s], self.held(s, n) * 16 * dmas + self.base[s])

    def close(self, dmas, n):
        for s in range(UNROLL):
            self.base[s] += self.held(s, n) * 16 * dmas


def steps(eng, step, lag, n=GROUPS):
    head = -(-(lag + UNROLL) // UNROLL)
    loop = n // UNROLL
    for s in range(head * UNROLL):
        step(Turn(s // UNROLL, s % UNROLL, n))
    with eng.Fori(head, loop) as i:
        for part in range(UNROLL):
            step(Turn(i, part, n))
    for s in range(loop * UNROLL, n + lag):
        step(Turn(s // UNROLL, s % UNROLL, n))


def build(nc, mode, a, out):
    with ExitStack() as ctx:
        def sb(name, shape, dt=F32):
            return ctx.enter_context(nc.sbuf_tensor(name, shape, dt))[:]

        def sem(name):
            return ctx.enter_context(nc.semaphore(name))

        def dram(name, shape, dt=F32):
            return nc.dram_tensor(name, shape, dt).ap()

        tabP = dram("tabP", (N, D))
        tabQ = dram("tabQ", (N, D))
        msgs = dram("msgs", (N + P, MW))
        yT = dram("yT", (D, N))
        relrow = dram("relrow", (N,))
        farrow = dram("farrow", (N,))
        keeprow = dram("keeprow", (N,))
        firstnode = dram("firstnode", (TILES,), I32)
        fetchidx = dram("fetchidx", (GROUPS, P, GT), I32)

        xs = sb("xs", [P, TILES, D])
        deg = sb("deg", [P, TILES])
        dinv = sb("dinv", [P, TILES])
        invdeg = sb("invdeg", [P, TILES])
        blockf = sb("blockf", [P, TILES])
        starts = sb("starts", [1, TILES], I32)
        firsts = sb("firsts", [1, TILES], I32)
        flag = sb("flag", [1, 1], I32)
        ident = sb("ident", [P, P])
        iota = sb("iota", [P, P])
        pcol = sb("pcol", [P, WK])
        stats = sb("stats", [D, GROUPS, 6])
        bn = sb("bn", [D, 8])
        epsc = sb("epsc", [P, 1])

        w1raw = sb("w1raw", [D, 2, D])
        w1 = sb("w1", [D, 2, D])
        w2 = sb("w2", [D, D])
        wg1 = sb("wg1", [D, D])
        wg2 = sb("wg2", [D, D])
        wl2 = sb("wl2", [P, D])
        wmse = sb("wmse", [P, HID])
        wmt = sb("wmt", [D, HID])
        wm2 = sb("wm2", [HID, D])
        wn1 = sb("wn1", [P, HID])
        wn2 = sb("wn2", [HID, D])
        COLS = ["L0_gnn_b1", "L0_gnn_b2", "L1_gnn_b1", "L1_gnn_gamma", "L1_gnn_beta", "L3_gnn_msg_b1",
                "L3_gnn_msg_b2", "L3_gnn_node_b1"]
        ROWS = ["L1_gnn_b2", "L2_gnn_b", "L3_gnn_node_b2", "L3_gnn_ln_scale", "L3_gnn_ln_offset"]
        cols = sb("cols", [P, len(COLS)])
        rows = sb("rows", [P, len(ROWS), D])
        b2row = sb("b2row", [1, GT, D])
        ones1 = sb("ones1", [1, P])

        def col(name, k=D):
            return cols[0:k, COLS.index(name):COLS.index(name) + 1]

        def row(name):
            return rows[:, ROWS.index(name):ROWS.index(name) + 1, :].to_broadcast([P, GT, D])

        passed = {e: sem(f"passed_{e}") for e in ("pe", "pool", "dve")}

        def gate(eng, name):
            eng.sem_inc(passed[name], 1)

        def over4(v):
            return v.unsqueeze(2).to_broadcast([P, GT, D])

        def window_starts(eng, table, g):
            _, values = nc.values_load_multi_w_load_instructions(
                table[0:1, bass.ds(g * GT, GT)], engines=(eng.engine,), min_val=0, max_val=N - WIN,
                skip_runtime_bounds_check_because="VectorE limits every start to N - WIN, and none is negative")
            return values

        def setup():
            with ExitStack() as inner:
                def tmp(name, shape, dt=F32):
                    return inner.enter_context(nc.sbuf_tensor(name, shape, dt))[:]

                def sig(name):
                    return inner.enter_context(nc.semaphore(name))

                E98 = GROUPS
                cur, nxt, prv = (tmp(n, [E98, GR], I32) for n in ("cur", "nxt", "prv"))
                last, lastt, far, keep, rel = (tmp(n, [E98, GR]) for n in ("last", "lastt", "far", "keep", "rel"))
                tgts = tmp("tgts", [E98, GR, MW - D])
                first4 = tmp("first4", [E98, GT])
                first4i = tmp("first4i", [E98, GT], I32)
                relmax = tmp("relmax", [P, 1])
                relall = tmp("relall", [P, 1])
                dsti, loi, hii = (tmp(n, [P, TILES], I32) for n in ("dsti", "loi", "hii"))
                lo, hi = (tmp(n, [P, TILES]) for n in ("lo", "hi"))
                ioti = tmp("ioti", [P, TILES], I32)
                ioth = tmp("ioth", [P, TILES], F16)
                hotlo = tmp("hotlo", [P, UNROLL, P], F16)
                hothi = tmp("hothi", [P, UNROLL, TILES], F16)
                ones = tmp("ones", [P, P])
                below = tmp("below", [P, P])
                degp = tmp("degp", [P, TILES])
                tot, incl, excl, st, has = (tmp(n, [P, TILES]) for n in ("tot", "incl", "excl", "st", "has"))
                idxf = tmp("idxf", [P, TILES])
                idxi = tmp("idxi", [P, TILES], I32)
                sc = tmp("sc", [1, TILES])
                over = tmp("over", [1, 4])
                blocki = tmp("blocki", [P, TILES], I32)
                pcoli = tmp("pcoli", [P, WK], I32)
                zero = tmp("zero", [P, MW])
                hist = inner.enter_context(nc.psum_tensor("hist", [P, TILES], F32))
                prefix = inner.enter_context(nc.psum_tensor("prefix", [P, TILES], F32))
                totals = inner.enter_context(nc.psum_tensor("totals", [P, TILES], F32))

                weights_in, edges_in, dst_in = sig("weights_in"), sig("edges_in"), sig("dst_in")
                rows_out, first_out, first_in = sig("rows_out"), sig("first_out"), sig("first_in")
                made = sig("made")
                chain = sig("chain")
                hot, hot_used = Tally(sig("hot")), Tally(sig("hot_used"))
                sums = sig("sums")
                rooted = sig("rooted")
                start_ready, idx_ready, zero_out = sig("start_ready"), sig("idx_ready"), sig("zero_out")
                rel_ready, relall_ready = sig("rel_ready"), sig("relall_ready")
                rows_ready, firsts_ready = sig("rows_ready"), sig("firsts_ready")
                deg_ready = sig("deg_ready")
                zero_ready = sig("zero_ready")

                dstp = a["dst"]
                loads = [(w1raw[:], a["L0_gnn_W1"].rearrange("(h k) n -> k h n", h=2)),
                         (w2[:], a["L0_gnn_W2"]), (wg1[:], a["L1_gnn_W1"]), (wg2[:], a["L1_gnn_W2"]),
                         (wl2[:], a["L2_gnn_W"]),
                         (wmse[0:D, :], a["L3_gnn_msg_W1"][0:D, :]),
                         (wmt[:], a["L3_gnn_msg_W1"][D:2 * D, :]),
                         (wmse[D:P, :], a["L3_gnn_msg_W1"][2 * D:3 * D, :]),
                         (wm2[:], a["L3_gnn_msg_W2"]), (wn1[:], a["L3_gnn_node_W1"]), (wn2[:], a["L3_gnn_node_W2"])]
                for k, n in enumerate(COLS):
                    size = a[n].shape[0]
                    loads.append((cols[0:size, k:k + 1], a[n].rearrange("(n o) -> n o", o=1)))
                for k, n in enumerate(ROWS):
                    loads.append((rows[:, k, :], a[n].rearrange("(o n) -> o n", o=1).to_broadcast([P, D])))
                for j in range(GT):
                    loads.append((b2row[:, j, :], a["L3_gnn_msg_b2"].rearrange("(o n) -> o n", o=1)))

                with nc.Block() as block:
                    @block.sync
                    def _(sp):
                        sp.dma_start(dsti[:], dstp[1:1 + N].rearrange("(p c) -> p c", p=P)).then_inc(dst_in, 16)
                        for t, off in ((cur, 1), (nxt, 2), (prv, 0)):
                            sp.dma_start(t[:], dstp[off:off + N].rearrange("(q c) -> q c", q=E98)).then_inc(edges_in, 16)
                        sp.wait_ge(rows_ready, 5)
                        for t, to in ((rel, relrow), (far, farrow), (keep, keeprow)):
                            sp.dma_start(to.rearrange("(q c) -> q c", q=E98), t).then_inc(rows_out, 16)
                        sp.dma_start(msgs[0:N, D:MW].rearrange("(q c) f -> q c f", q=E98), tgts).then_inc(rows_out, 16)
                        sp.dma_start(firstnode.rearrange("(q j) -> q j", q=E98), first4i[:]).then_inc(first_out, 16)
                        sp.wait_ge(first_out, 16)
                        sp.dma_start(firsts[:], firstnode.rearrange("(o t) -> o t", o=1)).then_inc(first_in, 16)
                        sp.wait_ge(rows_out, 64)
                        sp.wait_ge(idx_ready, 1)
                        sp.dma_start(fetchidx.rearrange("g p j -> p g j"), idxi.rearrange("p (g j) -> p g j", j=GT)
                                     ).then_inc(rows_out, 16)
                        sp.wait_ge(zero_ready, 1)
                        sp.dma_start(msgs[N:N + P, :], zero[:]).then_inc(zero_out, 16)
                        sp.wait_ge(rows_out, 80)
                        sp.wait_ge(first_in, 16)
                        sp.wait_ge(zero_out, 16)

                    @block.scalar
                    def _(act):
                        for to, frm in loads:
                            act.dma_start(to, frm).then_inc(weights_in, 16)
                        act.wait_ge(weights_in, 16 * len(loads))
                        act.wait_ge(deg_ready, 1)
                        nc.scalar.activation(dinv[:], degp[:], ACT.Sqrt).then_inc(rooted, 1)

                    @block.gpsimd
                    def _(pool):
                        nc.gpsimd.iota(ioti[:], [[1, TILES]], base=0, channel_multiplier=0).then_inc(made, 1)
                        nc.gpsimd.iota(blocki[:], [[P, TILES]], base=0, channel_multiplier=0).then_inc(made, 1)
                        nc.gpsimd.iota(pcoli[:], [[1, WK]], base=0, channel_multiplier=WK).then_inc(made, 1)
                        nc.gpsimd.memset(ident[:], 0.0).then_inc(made, 1)
                        nc.gpsimd.memset(ones[:], 1.0).then_inc(made, 1)
                        nc.gpsimd.memset(ones1[:], 1.0).then_inc(made, 1)
                        nc.gpsimd.memset(relmax[:], 0.0).then_inc(made, 1)
                        nc.gpsimd.memset(zero[:], 0.0).then_inc(zero_ready, 1)
                        nc.gpsimd.memset(epsc[:], EPS).then_inc(made, 1)
                        pool.wait_ge(made, 8)
                        nc.gpsimd.affine_select(out=ident[:], in_=ident[:], compare_op=ALU.not_equal, fill=1.0, base=0,
                                                pattern=[[-1, P]], channel_multiplier=1).then_inc(made, 1)
                        nc.gpsimd.affine_select(out=below[:], in_=ones[:], compare_op=ALU.is_ge, fill=0.0, base=-1,
                                                pattern=[[1, P]], channel_multiplier=-1).then_inc(made, 1)
                        pool.wait_ge(rel_ready, 1)
                        nc.gpsimd.partition_all_reduce(relall[:], relmax[:], P, RMAX).then_inc(relall_ready, 1)

                    @block.tensor
                    def _(pe):
                        def count(t):
                            g = t.at(0)
                            if g is None:
                                return
                            hot.wait(pe, g)
                            gate(pe, "pe")
                            nc.tensor.matmul(hist[:], hotlo[:, g.slot, :], hothi[:, g.slot, :],
                                             start=g.known and g.g == 0, stop=g.known and g.g == TILES - 1,
                                             skip_group_check=True).then_inc(hot_used.sem, 1)
                        steps(pe, count, 0, TILES)
                        pe.wait_ge(sums, 1)
                        pe.wait_ge(made, 10)
                        nc.tensor.matmul(prefix[:], below[:], deg[:], start=True, stop=True)
                        nc.tensor.matmul(totals[:], ones[:], deg[:], start=True, stop=True).then_inc(sums, 1)

                    @block.vector
                    def _(dve):
                        n = [0]

                        def link(ins):
                            n[0] += 1
                            ins.then_inc(chain, 1)
                            dve.wait_ge(chain, n[0])

                        v = nc.vector
                        dve.wait_ge(made, 8)
                        v.tensor_copy(ioth[:], ioti[:]).then_inc(chain, 1)
                        v.tensor_copy(iota[:], ioti[:, 0:P]).then_inc(chain, 1)
                        v.tensor_copy(pcol[:], pcoli[:]).then_inc(chain, 1)
                        n[0] = 3
                        link(v.tensor_copy(blockf[:], blocki[:]))
                        dve.wait_ge(dst_in, 16)
                        link(v.tensor_scalar(loi[:], dsti[:], P - 1, None, ALU.bitwise_and))
                        link(v.tensor_scalar(hii[:], dsti[:], 7, None, ALU.logical_shift_right))
                        link(v.tensor_copy(lo[:], loi[:]))
                        link(v.tensor_copy(hi[:], hii[:]))

                        def onehot(t):
                            g = t.at(0)
                            if g is None:
                                return
                            hot_used.wait(dve, g, back=UNROLL)
                            v.tensor_scalar(hotlo[:, g.slot, :], ioth[:, 0:P], lo[:, bass.ds(g.g, 1)], None, ALU.is_equal)
                            v.tensor_scalar(hothi[:, g.slot, :], ioth[:], hi[:, bass.ds(g.g, 1)], None,
                                            ALU.is_equal).then_inc(hot.sem, 1)
                        steps(dve, onehot, 0, TILES)

                        dve.wait_ge(edges_in, 48)
                        link(v.tensor_tensor(last[:], cur[:], nxt[:], ALU.not_equal))
                        link(v.scalar_tensor_tensor(out=lastt[:], in0=cur[:], scalar=1.0, in1=last[:], op0=ALU.add, op1=ALU.mult))
                        v.tensor_scalar(tgts[:, :, 1], lastt[:], -1.0, None, ALU.add)
                        v.tensor_copy(tgts[:, :, 0], cur[:])
                        link(v.tensor_tensor(keep[:], cur[:], prv[:], ALU.is_equal))
                        v.tensor_scalar(far[:], keep[:], -FAR, FAR, ALU.mult, ALU.add).then_inc(rows_ready, 1)
                        link(v.tensor_scalar(first4[:], cur.rearrange("q (j c) -> q j c", j=GT)[:, :, 0], float(N - WIN), None, ALU.min))
                        v.tensor_copy(first4i[:], first4[:]).then_inc(rows_ready, 1)
                        link(v.tensor_tensor(rel.rearrange("q (j c) -> q j c", j=GT), cur.rearrange("q (j c) -> q j c", j=GT),
                                             first4.unsqueeze(2).to_broadcast([E98, GT, P]), ALU.subtract))
                        v.tensor_reduce(relmax[0:E98, :], rel[:], AX_X, ALU.max).then_inc(rel_ready, 1)
                        dve.sem_inc(rows_ready, 3)

                        dve.wait_ge(hot_used.sem, TILES)
                        v.tensor_copy(deg[:], hist[:]).then_inc(sums, 1)
                        dve.wait_ge(sums, 2)
                        v.tensor_scalar(degp[:], deg[:], 1.0, None, ALU.add).then_inc(deg_ready, 1)
                        link(v.tensor_scalar(invdeg[:], deg[:], 1.0, None, ALU.max))
                        link(v.reciprocal(invdeg[:], invdeg[:]))
                        link(v.tensor_copy(tot[:], totals[:]))
                        link(v.tensor_scalar(has[:], deg[:], 1.0, None, ALU.min))
                        link(v.tensor_tensor_scan(incl[:], iota[:, 0:1].to_broadcast([P, TILES]), tot[:], 0.0, ALU.add, ALU.add))
                        link(v.tensor_tensor(excl[:], incl[:], tot[:], ALU.subtract))
                        link(v.tensor_scalar(sc[:], excl[0:1, :], float(N - WIN), None, ALU.min))
                        v.tensor_copy(starts[:], sc[:]).then_inc(start_ready, 1)
                        link(v.tensor_tensor(st[:], excl[:], prefix[:], ALU.add))
                        link(v.scalar_tensor_tensor(out=idxf[:], in0=st[:], scalar=float(-1 - N), in1=deg[:], op0=ALU.add, op1=ALU.add))
                        link(v.tensor_tensor(idxf[:], idxf[:], has[:], ALU.mult))
                        link(v.tensor_scalar(idxf[:], idxf[:], float(N), None, ALU.add))
                        v.tensor_copy(idxi[:], idxf[:]).then_inc(idx_ready, 1)
                        link(v.tensor_tensor(sc[:], incl[0:1, :], sc[:], ALU.subtract))
                        link(v.tensor_reduce(over[:, 0:1], sc[:], AX_X, ALU.max))
                        link(v.tensor_scalar(over[:, 1:2], over[:, 0:1], float(WIN), None, ALU.is_gt))
                        dve.wait_ge(relall_ready, 1)
                        link(v.tensor_scalar(over[:, 2:3], relall[0:1, :], float(WIN - 1), None, ALU.is_gt))
                        link(v.tensor_tensor(over[:, 3:4], over[:, 1:2], over[:, 2:3], ALU.max))
                        link(v.tensor_copy(flag[:], over[:, 3:4]))
                        dve.wait_ge(rooted, 1)
                        link(v.reciprocal(dinv[:], dinv[:]))
                        dve.wait_ge(weights_in, 16 * len(loads))
                        link(v.tensor_tensor(w1[:, 0, :], w1raw[:, 0, :], w1raw[:, 1, :], ALU.subtract))
                        link(v.tensor_copy(w1[:, 1, :], w1raw[:, 1, :]))
        class Signals:

            def __init__(self, path):
                def tally(name):
                    self.tallies.append(Tally(sem(f"{path}_{name}")))
                    return self.tallies[-1]

                self.tallies = []
                self.landed = Landing([sem(f"{path}_landed{k}") for k in range(UNROLL)])
                self.fetched = Landing([sem(f"{path}_fetched{k}") for k in range(UNROLL)])
                self.stored = Landing([sem(f"{path}_stored{k}") for k in range(UNROLL)])
                self.rel = tally("rel")
                self.hot = tally("hot")
                self.joined = tally("joined")
                self.mixed = tally("mixed")
                self.biased = tally("biased")
                self.x_new = tally("x_new")
                self.summed = tally("summed")
                self.centred = tally("centred")
                self.squared = tally("squared")
                self.varied = tally("varied")
                self.inverted = tally("inverted")
                self.normed = tally("normed")
                self.scaled = tally("scaled")
                self.offset = tally("offset")
                self.with_h = tally("with_h")
                self.final = tally("final")
                self.shifted = tally("shifted")
                self.stat = tally("stat")
                self.agged = tally("agged")
                self.turned = tally("turned")
                self.multiplied = tally("multiplied")
                self.hid_sum = tally("hid_sum")
                self.rooted = tally("rooted")
                self.turned_sb = tally("turned_sb")
                self.hidden = tally("hidden")
                self.affined = tally("affined")
                self.rel_hot = tally("rel_hot")
                self.summed_e = tally("summed_e")
                self.hidden_e = tally("hidden_e")
                self.tgt_sb = tally("tgt_sb")
                self.hid_sb = tally("hid_sb")
                self.msg = tally("msg")
                self.msg_sb = tally("msg_sb")
                self.scanned = tally("scanned")
                self.turned_e = tally("turned_e")
                self.out_ready = tally("out_ready")

            def close(self, loads, gathers, stores):
                for t in self.tallies:
                    if t.used:
                        t.base, t.used = t.base + GROUPS, False
                self.landed.close(loads, GROUPS)
                self.fetched.close(gathers, GROUPS)
                self.stored.close(stores, GROUPS)

        def either(eng, fast, general):
            if mode != "both" or general is None:
                return (general if mode == "general" and general else fast)(eng)
            v = nc.values_load(flag[0:1, 0:1], engines=(eng.engine,), min_val=0, max_val=1)
            with eng.If(v > 0):
                general(eng)
            with eng.Else():
                fast(eng)

        def tabrows(tab, g):
            return tab.rearrange("(g j p) f -> g p j f", p=P, j=GT)[bass.ds(g, 1)].rearrange("o p j f -> (o p) j f")

        def edgerows(tab, g):
            return tab.rearrange("(g p j) f -> g p j f", p=P, j=GT)[bass.ds(g, 1)].rearrange("o p j f -> (o p) j f")

        def edgecols(vec, g, parts):
            return vec.rearrange("(g c) -> g c", c=GR)[bass.ds(g, 1)].to_broadcast([parts, GR])

        class NodePass:

            def __init__(self, kind, general, sg):
                self.kind, self.general, self.sg = kind, general, sg
                self.windowed = kind in (1, 2, 4, 5, 6) and not general
                self.gathered = kind in (1, 2, 4, 5, 6) and general
                self.norms = kind in (0, 1, 4, 5)
                self.own = kind in (2, 4, 5, 6)
                self.late = kind in (5, 6)
                self.loads = (4 if self.windowed else 0) + (1 if self.gathered else 0) + (1 if self.own else 0) + (kind in (0, 3))
                self.stores = 2 if kind == 0 else 1
                self.store_lag = {0: 3, 1: 4, 2: 3, 3: 2, 4: 3, 5: 5, 6: 5}[kind]
                self.mid = 3 if self.late else 1 if kind else 0
                self.fin = self.mid + 1

            def buffers(self, tmp, ps):
                k = self.kind
                if self.windowed:
                    self.win = tmp("win", [WP, UNROLL, GT, WK, MW])
                    self.hot = tmp("hot", [WP, 2, GT, WK, P])
                    self.relw = tmp("relw", [WP, 2, GT, WK])
                    self.agg = [ps(f"agg{b}", [P, GT, D]) for b in range(2)]
                if self.gathered:
                    self.fidx = tmp("fidx", [P, UNROLL, GT], I32)
                    self.aggs = tmp("aggs", [P, UNROLL, GT, MW])
                if self.own and not self.late:
                    self.ownb = tmp("ownb", [P, UNROLL, GT, D])
                if self.late:
                    self.hn = tmp("hn", [P, UNROLL, GT, P])
                if k == 3:
                    self.yin = tmp("yin", [D, UNROLL, GR])
                    self.zb = tmp("zb", [D, 2, GR])
                    self.zs = tmp("zs", [D, 2, GR])
                if k == 2:
                    self.mix = tmp("mix", [P, 2, GT, D])
                    self.yout = tmp("yout", [D, UNROLL, GR])
                if k == 4:
                    self.mix = tmp("mix", [P, 2, GT, D])
                    self.hout = tmp("hout", [P, UNROLL, GT, D])
                if k == 5:
                    self.hout = tmp("hout", [P, UNROLL, GT, D])
                if self.norms or k == 6:
                    self.s1, self.s2, self.sd, self.rs = (tmp(n, [P, 2, GT]) for n in ("s1", "s2", "sd", "rs"))
                    self.xc, self.sq = tmp("xc", [P, 2, GT, D]), tmp("sq", [P, 2, GT, D])
                if k in (0, 1):
                    self.hb = tmp("hb", [P, 2, GT, D])
                if k == 6:
                    self.yb, self.fb = tmp("yb", [P, 2, GT, D]), tmp("fb", [P, UNROLL, GT, D])
                    self.hidp = [ps(f"hidp{b}", [HID, GR]) for b in range(2)]
                    self.hids = tmp("hids", [HID, 2, GR])
                self.rowsT = P if self.late else D
                if k != 4 and k != 3:
                    self.tp = [ps(f"tp{b}", [self.rowsT, GR]) for b in range(2)]
                if k in (0, 1, 5, 6):
                    self.ts = tmp("ts", [self.rowsT, 2, GR])
                if k in (0, 1, 3, 5, 6):
                    self.width = 2 * D if k == 0 else D
                    self.mp = [ps(f"mp{b}", [P, GT, self.width]) for b in range(2)]
                if k in (0, 1, 3):
                    self.outb = tmp("outb", [P, UNROLL, GT, self.width])

            def sp(self, eng):
                sg, k = self.sg, self.kind

                def step(t):
                    g = t.at(0)
                    if g is not None:
                        land = sg.landed.sems[g.slot]
                        if k == 0:
                            eng.dma_start(xs[:, bass.ds(g.g * GT, GT), :], tabrows(a["x"], g.g)).then_inc(land, 16)
                        if k == 3:
                            sg.affined.wait(eng, g, back=UNROLL)
                            eng.dma_start(self.yin[:, g.slot, :], yT[:, bass.ds(g.g * GR, GR)]).then_inc(land, 16)
                        if self.own:
                            (sg.final if k == 6 else sg.turned if k == 5 else sg.mixed).wait(eng, g, back=UNROLL)
                            to = self.hn[:, g.slot, :, 0:D] if self.late else self.ownb[:, g.slot]
                            eng.dma_start(to, tabrows(tabQ, g.g)).then_inc(land, 16)
                        if self.gathered:
                            if g.from_(UNROLL):
                                sg.fetched.wait(eng, g, GT, back=1)
                            eng.dma_start(self.fidx[:, g.slot, :], fetchidx[bass.ds(g.g, 1)].rearrange("o p j -> (o p) j")).then_inc(land, 16)
                        if self.windowed:
                            sg.agged.wait(eng, g, back=UNROLL)
                            for j, s in enumerate(window_starts(eng, starts, g.g)):
                                eng.dma_start(self.win[:, g.slot, j, :, :],
                                              msgs[bass.ds(s, WIN), :].rearrange("(p k) f -> p k f", k=WK)).then_inc(land, 16)
                    g = t.at(self.store_lag)
                    if g is not None:
                        done = sg.stored.sems[g.slot]
                        if k == 0:
                            sg.scaled.wait(eng, g)
                            eng.dma_start(tabrows(tabP, g.g), self.outb[:, g.slot, :, 0:D]).then_inc(done, 16)
                            eng.dma_start(tabrows(tabQ, g.g), self.outb[:, g.slot, :, D:2 * D]).then_inc(done, 16)
                        elif k in (1, 3):
                            sg.scaled.wait(eng, g)
                            eng.dma_start(tabrows(tabQ, g.g), self.outb[:, g.slot]).then_inc(done, 16)
                        elif k == 2:
                            sg.turned_sb.wait(eng, g)
                            eng.dma_start(yT[:, bass.ds(g.g * GR, GR)], self.yout[:, g.slot, :]).then_inc(done, 16)
                        elif k in (4, 5):
                            sg.normed.wait(eng, g)
                            eng.dma_start(tabrows(tabQ, g.g), self.hout[:, g.slot]).then_inc(done, 16)
                        else:
                            sg.final.wait(eng, g)
                            eng.dma_start(tabrows(out, g.g), self.fb[:, g.slot]).then_inc(done, 16)
                steps(eng, step, self.store_lag)
                sg.stored.wait_all(eng, self.stores, GROUPS)

            def pool(self, eng):
                sg = self.sg
                if not self.gathered:
                    return

                def step(t):
                    g = t.at(0)
                    if g is None:
                        return
                    sg.landed.wait(eng, g, self.loads)
                    sg.mixed.wait(eng, g, back=UNROLL)
                    gate(eng, "pool")
                    for j in range(GT):
                        nc.gpsimd.indirect_dma_start(self.aggs[:, g.slot, j, :], None, msgs,
                                                     bass.IndirectOffsetOnAxis(ap=self.fidx[:, g.slot, j:j + 1], axis=0)
                                                     ).then_inc(sg.fetched.sems[g.slot], 16)
                steps(eng, step, 0)

            def pe(self, eng):
                sg, k = self.sg, self.kind
                T1 = {0: 1, 1: 2, 2: 1, 5: 1, 6: 1}.get(k)
                T2 = {0: 2, 1: 3, 3: 1, 5: 2, 6: 2}.get(k)

                def step(t):
                    g = t.at(T1) if T1 else None
                    if g is not None:
                        (sg.normed if k in (0, 1) else sg.mixed).wait(eng, g)
                        if self.late:
                            sg.landed.wait(eng, g, self.loads)
                        sg.turned_sb.wait(eng, g, back=2)
                        gate(eng, "pe")
                        src = self.hn[:, g.slot] if self.late else (self.mix if k == 2 else self.hb)[:, g.pair]
                        for j in range(GT):
                            mm = nc.tensor.transpose(self.tp[g.pair][:, bass.ts(j, P)], src[:, j, :], ident)
                        mm.then_inc(sg.turned.sem, 1)
                    g = t.at(T2) if T2 else None
                    if g is not None and k == 6:
                        sg.turned_sb.wait(eng, g)
                        sg.hidden.wait(eng, g, back=2)
                        gate(eng, "pe")
                        nc.tensor.matmul(self.hidp[g.pair][:], wn1, self.ts[:, g.pair, :], start=True, stop=True
                                         ).then_inc(sg.hid_sum.sem, 1)
                    if g is not None and k != 6:
                        (sg.shifted if k == 3 else sg.turned_sb).wait(eng, g)
                        (sg.x_new if k == 5 else sg.scaled).wait(eng, g, back=2)
                        gate(eng, "pe")
                        src = self.zs[:, g.pair, :] if k == 3 else self.ts[:, g.pair, :]
                        w = {0: w1.rearrange("k h n -> k (h n)"), 1: wg1, 3: wg2, 5: wl2}[k]
                        for j in range(GT):
                            mm = nc.tensor.matmul(self.mp[g.pair][:, j, :], src[:, bass.ts(j, P)], w, start=True, stop=True,
                                                  skip_group_check=True)
                        mm.then_inc(sg.multiplied.sem, 1)
                    g = t.at(3) if k == 6 else None
                    if g is not None:
                        sg.hidden.wait(eng, g)
                        sg.x_new.wait(eng, g, back=2)
                        gate(eng, "pe")
                        for j in range(GT):
                            mm = nc.tensor.matmul(self.mp[g.pair][:, j, :], self.hids[:, g.pair, bass.ts(j, P)], wn2,
                                                  start=True, stop=True, skip_group_check=True)
                        mm.then_inc(sg.multiplied.sem, 1)
                    g = t.at(0)
                    if g is not None and self.windowed:
                        sg.hot.wait(eng, g)
                        sg.landed.wait(eng, g, self.loads)
                        sg.mixed.wait(eng, g, back=2)
                        gate(eng, "pe")
                        for j in range(GT):
                            for w in range(WK):
                                mm = nc.tensor.matmul(self.agg[g.pair][:, j, :], self.hot[:, g.pair, j, w, :],
                                                      self.win[:, g.slot, j, w, 0:D], start=w == 0, stop=w == WK - 1,
                                                      skip_group_check=True)
                        mm.then_inc(sg.agged.sem, 1)
                if k != 4 or self.windowed:
                    steps(eng, step, max(T1 or 0, T2 or 0, 3 if k == 6 else 0))

            def act(self, eng):
                sg, k = self.sg, self.kind
                C = {0: 1, 1: 2, 2: 1, 5: 1, 6: 1}.get(k)

                def step(t):
                    g = t.at(0) if k == 3 else None
                    if g is not None:
                        sg.landed.wait(eng, g, self.loads)
                        sg.shifted.wait(eng, g, back=2)
                        nc.scalar.activation(self.zb[:, g.pair, :], self.yin[:, g.slot, :], ACT.Identity,
                                             bias=bn[:, 5:6], scale=bn[:, 4:5]).then_inc(sg.affined.sem, 1)
                    g = t.at(C) if C else None
                    if g is not None:
                        sg.turned.wait(eng, g)
                        if k == 2:
                            sg.stored.wait(eng, g, self.stores, back=1)
                            nc.scalar.activation(self.yout[:, g.slot, :], self.tp[g.pair][:], ACT.Identity,
                                                 bias=col("L1_gnn_b1")).then_inc(sg.turned_sb.sem, 1)
                        else:
                            (sg.hid_sum if k == 6 else sg.multiplied).wait(eng, g, back=2)
                            nc.scalar.copy(self.ts[:, g.pair, :], self.tp[g.pair][:]).then_inc(sg.turned_sb.sem, 1)
                    g = t.at(2) if k == 6 else None
                    if g is not None:
                        sg.hid_sum.wait(eng, g)
                        sg.multiplied.wait(eng, g, back=2)
                        nc.scalar.activation(self.hids[:, g.pair, :], self.hidp[g.pair][:], ACT.Relu,
                                             bias=col("L3_gnn_node_b1", HID)).then_inc(sg.hidden.sem, 1)
                    g = t.at(self.mid) if self.norms or k == 6 else None
                    if g is not None:
                        sg.varied.wait(eng, g)
                        nc.scalar.activation(self.sd[:, g.pair, :], self.s2[:, g.pair, :], ACT.Sqrt, bias=epsc,
                                             scale=1.0 / D).then_inc(sg.rooted.sem, 1)
                steps(eng, step, max(C or 0, 2 if k == 6 else 0, self.mid))

            def dve(self, eng):
                sg, k, v = self.sg, self.kind, nc.vector

                def centre(g, src):
                    gate(eng, "dve")
                    v.tensor_reduce(self.s1[:, g.pair, :], src, AX_X, ALU.add).then_inc(sg.summed.sem, 1)
                    sg.summed.wait(eng, g)
                    v.scalar_tensor_tensor(out=self.xc[:, g.pair], in0=over4(self.s1[:, g.pair, :]), scalar=-1.0 / D, in1=src,
                                           op0=ALU.mult, op1=ALU.add).then_inc(sg.centred.sem, 1)
                    sg.centred.wait(eng, g)
                    v.tensor_tensor(self.sq[:, g.pair], self.xc[:, g.pair], self.xc[:, g.pair], ALU.mult).then_inc(sg.squared.sem, 1)
                    sg.squared.wait(eng, g)
                    sg.rooted.wait(eng, g, back=2)
                    v.tensor_reduce(self.s2[:, g.pair, :], self.sq[:, g.pair], AX_X, ALU.add).then_inc(sg.varied.sem, 1)

                def feats(g):
                    return xs[:, bass.ds(g.g * GT, GT), :]

                def here(vec, g):
                    return over4(vec[:, bass.ds(g.g * GT, GT)])

                def step(t):
                    g = t.at(0 if k == 0 else 1)
                    if g is not None:
                        if self.windowed:
                            sg.agged.wait(eng, g)
                            agg = self.agg[g.pair][:]
                        elif self.gathered:
                            sg.fetched.wait(eng, g, GT)
                            agg = self.aggs[:, g.slot, :, 0:D]
                        if k == 0:
                            sg.landed.wait(eng, g, self.loads)
                            centre(g, feats(g))
                        elif k == 1:
                            v.tensor_tensor(feats(g), feats(g), agg, ALU.add).then_inc(sg.mixed.sem, 1)
                            sg.mixed.wait(eng, g)
                            centre(g, feats(g))
                        elif k in (2, 4):
                            if self.gathered:
                                sg.landed.wait(eng, g, self.loads)
                            if k == 2:
                                sg.turned.wait(eng, g, back=2)
                            v.tensor_tensor(self.mix[:, g.pair], self.ownb[:, g.slot], agg, ALU.add).then_inc(sg.joined.sem, 1)
                            sg.joined.wait(eng, g)
                            v.tensor_tensor(self.mix[:, g.pair], self.mix[:, g.pair], here(dinv, g), ALU.mult).then_inc(sg.mixed.sem, 1)
                            if k == 4:
                                sg.mixed.wait(eng, g)
                                v.tensor_tensor(self.mix[:, g.pair], self.mix[:, g.pair], row("L1_gnn_b2"), ALU.add).then_inc(sg.biased.sem, 1)
                                sg.biased.wait(eng, g)
                                v.tensor_tensor(feats(g), feats(g), self.mix[:, g.pair], ALU.add).then_inc(sg.x_new.sem, 1)
                                sg.x_new.wait(eng, g)
                                centre(g, feats(g))
                        elif k == 5:
                            sg.turned.wait(eng, g, back=UNROLL)
                            v.tensor_tensor(self.hn[:, g.slot, :, D:P], agg, here(invdeg, g), ALU.mult).then_inc(sg.mixed.sem, 1)
                        elif k == 6:
                            sg.turned.wait(eng, g, back=UNROLL)
                            v.tensor_copy(self.hn[:, g.slot, :, D:P], agg).then_inc(sg.mixed.sem, 1)
                        elif k == 3:
                            sg.affined.wait(eng, g)
                            sg.multiplied.wait(eng, g, back=2)
                            v.scalar_tensor_tensor(out=self.zs[:, g.pair, :], in0=self.zb[:, g.pair, :], scalar=SLOPE,
                                                   in1=self.zb[:, g.pair, :], op0=ALU.mult, op1=ALU.max).then_inc(sg.shifted.sem, 1)
                    g = t.at(2) if k == 2 else None
                    if g is not None:
                        sg.turned_sb.wait(eng, g)
                        gate(eng, "dve")
                        last = GR if not (g.known and g.g == GROUPS - 1) else N_TRUE - (GROUPS - 1) * GR
                        v.bn_stats(stats[:, bass.ds(g.g, 1), :].rearrange("p o s -> p (o s)"), self.yout[:, g.slot, 0:last]
                                   ).then_inc(sg.stat.sem, 1)
                    g = t.at(self.mid) if self.late else None
                    if g is not None:
                        sg.multiplied.wait(eng, g)
                        if k == 5:
                            v.tensor_tensor(feats(g), feats(g), self.mp[g.pair][:], ALU.add).then_inc(sg.x_new.sem, 1)
                            sg.x_new.wait(eng, g)
                            v.tensor_tensor(feats(g), feats(g), row("L2_gnn_b"), ALU.add).then_inc(sg.biased.sem, 1)
                            sg.biased.wait(eng, g)
                            centre(g, feats(g))
                        else:
                            v.tensor_tensor(self.yb[:, g.pair], self.mp[g.pair][:], row("L3_gnn_node_b2"), ALU.add).then_inc(sg.x_new.sem, 1)
                            sg.x_new.wait(eng, g)
                            centre(g, self.yb[:, g.pair])
                    g = t.at(self.fin) if self.norms or k == 6 else None
                    if g is not None:
                        sg.rooted.wait(eng, g)
                        v.reciprocal(self.rs[:, g.pair, :], self.sd[:, g.pair, :]).then_inc(sg.inverted.sem, 1)
                        sg.inverted.wait(eng, g)
                        r = over4(self.rs[:, g.pair, :])
                        if k < 6:
                            if k in (0, 1):
                                sg.turned.wait(eng, g, back=2)
                                to = self.hb[:, g.pair]
                            else:
                                sg.stored.wait(eng, g, self.stores, back=1)
                                to = self.hout[:, g.slot]
                            v.scalar_tensor_tensor(out=to, in0=self.xc[:, g.pair], scalar=0.0, in1=r, op0=ALU.max,
                                                   op1=ALU.mult).then_inc(sg.normed.sem, 1)
                        else:
                            c, f = self.xc[:, g.pair], self.fb[:, g.slot]
                            v.tensor_tensor(c, c, r, ALU.mult).then_inc(sg.normed.sem, 1)
                            sg.normed.wait(eng, g)
                            v.tensor_tensor(c, c, row("L3_gnn_ln_scale"), ALU.mult).then_inc(sg.scaled.sem, 1)
                            sg.scaled.wait(eng, g)
                            v.tensor_tensor(c, c, row("L3_gnn_ln_offset"), ALU.add).then_inc(sg.offset.sem, 1)
                            sg.offset.wait(eng, g)
                            v.tensor_tensor(c, c, self.hn[:, g.slot, :, 0:D], ALU.add).then_inc(sg.with_h.sem, 1)
                            sg.with_h.wait(eng, g)
                            sg.stored.wait(eng, g, self.stores, back=1)
                            v.tensor_tensor(f, c, feats(g), ALU.add).then_inc(sg.final.sem, 1)
                    E = {0: 3, 1: 4, 3: 2}.get(k)
                    g = t.at(E) if E else None
                    if g is not None:
                        sg.multiplied.wait(eng, g)
                        sg.stored.wait(eng, g, self.stores, back=1)
                        if k == 0:
                            v.tensor_copy(self.outb[:, g.slot], self.mp[g.pair][:]).then_inc(sg.scaled.sem, 1)
                        else:
                            v.tensor_tensor(self.outb[:, g.slot], self.mp[g.pair][:], here(dinv, g), ALU.mult).then_inc(sg.scaled.sem, 1)
                    g = t.at(0) if self.windowed else None
                    if g is not None:
                        sg.landed.wait(eng, g, self.loads)
                        c = D + (1 if k == 1 else 0)
                        v.tensor_tensor(self.relw[:, g.pair], self.win[:, g.slot, :, :, c],
                                        blockf[0:WP, bass.ds(g.g * GT, GT)].unsqueeze(2).to_broadcast([WP, GT, WK]),
                                        ALU.subtract).then_inc(sg.rel.sem, 1)
                        sg.rel.wait(eng, g)
                        sg.agged.wait(eng, g, back=2)
                        v.tensor_tensor(self.hot[:, g.pair].rearrange("p j k n -> p (j k) n"),
                                        iota[0:WP, :].unsqueeze(1).to_broadcast([WP, GT * WK, P]),
                                        self.relw[:, g.pair].rearrange("p j k -> p (j k)").unsqueeze(2).to_broadcast([WP, GT * WK, P]),
                                        ALU.is_equal).then_inc(sg.hot.sem, 1)
                steps(eng, step, {0: 3, 1: 4, 2: 2, 3: 2, 4: 2, 5: 4, 6: 4}[k])

        class EdgePass:

            def __init__(self, kind, general, sg):
                self.kind, self.general, self.sg = kind, general, sg
                self.scans = kind == "max" or general
                self.spread = kind in ("max", "mlp") and not general
                self.both = kind in ("max", "mlp") and general
                self.gathers = GT * (2 if self.both else 1)
                self.loads = 1 + (5 if self.spread else 0) + self.both + self.scans + (kind == "mlp")
                self.store_lag = 5 if self.scans else 3 if kind == "mlp" else 2

            def buffers(self, tmp, ps):
                k = self.kind
                self.W = P if k == "mlp" else D
                self.sidx = tmp("sidx", [P, UNROLL, GT], I32)
                self.rowsb = tmp("rowsb", [P, UNROLL, GT, self.W])
                if self.both:
                    self.tidx = tmp("tidx", [P, UNROLL, GT], I32)
                    self.trows = tmp("trows", [P, UNROLL, GT, D])
                if self.spread:
                    self.win = tmp("twin", [WP, UNROLL, GT, WK, D])
                    self.relb = tmp("relb", [WP, UNROLL, GR])
                    self.hot = tmp("ehot", [WP, 2, WK, GR])
                if k != "sum" or self.scans:
                    self.s_ps = [ps(f"s_ps{b}", [self.W, GR]) for b in range(2)]
                    self.h_sb = tmp("h_sb", [self.W, 2, GR])
                if k == "mlp":
                    self.t_ps = [ps(f"t_ps{b}", [D, GR]) for b in range(1)]
                    self.t_sb = tmp("t_sb", [D, 2, GR])
                    self.hid_ps = [ps(f"hid_ps{b}", [HID, GR]) for b in range(2)]
                    self.hid = tmp("hid", [HID, 2, GR])
                if self.scans:
                    self.mask = tmp("mask", [D, UNROLL, GR])
                    self.sc = tmp("scan", [D, 2, GR])
                    if k != "sum":
                        self.m_ps = ps("m_ps", [D, GR])
                        self.m_sb = tmp("m_sb", [D, 2, GR])
                if self.scans or k == "mlp":
                    self.o_ps = [ps(f"o_ps{b}", [P, GT, D]) for b in range(2)]
                    self.outb = tmp("eoutb", [P, UNROLL, GT, D])
                else:
                    self.outb = self.rowsb

            def sp(self, eng):
                sg, k = self.sg, self.kind

                def step(t):
                    g = t.at(0)
                    if g is not None:
                        land = sg.landed.sems[g.slot]
                        if g.from_(UNROLL):
                            sg.fetched.wait(eng, g, self.gathers, back=1)
                        eng.dma_start(self.sidx[:, g.slot, :], a["src"].rearrange("(g p j) -> g p j", p=P, j=GT)[bass.ds(g.g, 1)].rearrange("o p j -> (o p) j")).then_inc(land, 16)
                        if self.both:
                            eng.dma_start(self.tidx[:, g.slot, :], a["dst"][1:1 + N].rearrange("(g p j) -> g p j", p=P, j=GT)[bass.ds(g.g, 1)].rearrange("o p j -> (o p) j")).then_inc(land, 16)
                        if k == "mlp":
                            sg.summed_e.wait(eng, g, back=UNROLL)
                            eng.dma_start(self.rowsb[:, g.slot, :, D:P], edgerows(a["edge_attr_64"], g.g)).then_inc(land, 16)
                        if self.scans:
                            sg.scanned.wait(eng, g, back=UNROLL)
                            eng.dma_start(self.mask[:, g.slot, :], edgecols(farrow if k == "max" else keeprow, g.g, D)).then_inc(land, 16)
                        if self.spread:
                            sg.rel_hot.wait(eng, g, back=UNROLL)
                            eng.dma_start(self.relb[:, g.slot, :], edgecols(relrow, g.g, WP)).then_inc(land, 16)
                            sg.summed_e.wait(eng, g, back=UNROLL)
                            for j, s in enumerate(window_starts(eng, firsts, g.g)):
                                eng.dma_start(self.win[:, g.slot, j, :, :], (tabP if k == "max" else tabQ)[bass.ds(s, WIN), :].rearrange(
                                    "(p k) f -> p k f", k=WK)).then_inc(land, 16)
                    g = t.at(self.store_lag)
                    if g is not None:
                        if self.outb is self.rowsb:
                            sg.fetched.wait(eng, g, self.gathers)
                        else:
                            sg.out_ready.wait(eng, g)
                        eng.dma_start(edgerows(msgs[0:N, :], g.g)[:, :, 0:D], self.outb[:, g.slot]).then_inc(sg.stored.sems[g.slot], 16)
                steps(eng, step, self.store_lag)
                sg.stored.wait_all(eng, 1, GROUPS)

            def pool(self, eng):
                sg, k = self.sg, self.kind
                srctab = tabQ
                tgttab = tabP if k == "max" else tabQ

                def step(t):
                    g = t.at(0)
                    if g is None:
                        return
                    sg.landed.wait(eng, g, self.loads)
                    if self.outb is self.rowsb:
                        sg.stored.wait(eng, g, 1, back=1)
                    else:
                        sg.summed_e.wait(eng, g, back=UNROLL)
                    gate(eng, "pool")
                    for j in range(GT):
                        nc.gpsimd.indirect_dma_start(self.rowsb[:, g.slot, j, 0:D], None, srctab,
                                                     bass.IndirectOffsetOnAxis(ap=self.sidx[:, g.slot, j:j + 1], axis=0)
                                                     ).then_inc(sg.fetched.sems[g.slot], 16)
                        if self.both:
                            nc.gpsimd.indirect_dma_start(self.trows[:, g.slot, j, :], None, tgttab,
                                                         bass.IndirectOffsetOnAxis(ap=self.tidx[:, g.slot, j:j + 1], axis=0)
                                                         ).then_inc(sg.fetched.sems[g.slot], 16)
                steps(eng, step, 0)

            def targets(self, g, to):
                if self.spread:
                    for j in range(GT):
                        for w in range(WK):
                            mm = nc.tensor.matmul(to[:, bass.ts(j, P)], self.win[:, g.slot, j, w, :], self.hot[:, g.pair, w, bass.ts(j, P)],
                                                  start=j == 0 and w == 0, stop=w == WK - 1, skip_group_check=True)
                else:
                    for j in range(GT):
                        mm = nc.tensor.matmul(to[:, j::GT], self.trows[:, g.slot, j, :], ident, start=j == 0, stop=True,
                                              skip_group_check=True)
                return mm

            def pe(self, eng):
                sg, k = self.sg, self.kind
                if k == "sum" and not self.scans:
                    return

                def step(t):
                    g = t.at(0)
                    if g is not None:
                        sg.fetched.wait(eng, g, self.gathers)
                        sg.landed.wait(eng, g, self.loads)
                        if self.spread:
                            sg.rel_hot.wait(eng, g)
                        sg.hidden_e.wait(eng, g, back=2)
                        if k == "mlp":
                            sg.tgt_sb.wait(eng, g, back=1)
                        gate(eng, "pe")
                        if k == "max":
                            self.targets(g, self.s_ps[g.pair])
                            for j in range(GT):
                                mm = nc.tensor.matmul(self.s_ps[g.pair][:, j::GT], self.rowsb[:, g.slot, j, :], ident,
                                                      start=False, stop=True, skip_group_check=True)
                        else:
                            if k == "mlp":
                                self.targets(g, self.t_ps[0])
                            for j in range(GT):
                                mm = nc.tensor.transpose(self.s_ps[g.pair][:, j::GT], self.rowsb[:, g.slot, j, :], ident)
                        mm.then_inc(sg.summed_e.sem, 1)
                    if k != "sum":
                        g = t.at(1)
                        if g is not None and k == "mlp":
                            sg.hidden_e.wait(eng, g)
                            sg.tgt_sb.wait(eng, g)
                            sg.hid_sb.wait(eng, g, back=2)
                            gate(eng, "pe")
                            nc.tensor.matmul(self.hid_ps[g.pair][:], wmse, self.h_sb[:, g.pair, :], start=True, stop=False)
                            nc.tensor.matmul(self.hid_ps[g.pair][:], wmt, self.t_sb[:, g.pair, :], start=False, stop=True
                                             ).then_inc(sg.hid_sum.sem, 1)
                        g = t.at(2 if k == "mlp" else 1)
                        if g is not None:
                            hid_ready = sg.hid_sb if k == "mlp" else sg.hidden_e
                            hid, w = (self.hid, wm2) if k == "mlp" else (self.h_sb, w2)
                            hid_ready.wait(eng, g)
                            if self.scans:
                                sg.msg_sb.wait(eng, g, back=1)
                                gate(eng, "pe")
                                nc.tensor.matmul(self.m_ps[:], w, hid[:, g.pair, :], start=True, stop=True).then_inc(sg.msg.sem, 1)
                            else:
                                sg.out_ready.wait(eng, g, back=2)
                                gate(eng, "pe")
                                nc.tensor.matmul(self.o_ps[g.pair][:].rearrange("p j f -> p (j f)"), ones1, b2row.rearrange("o j f -> o (j f)"),
                                                 start=True, stop=False, skip_group_check=True)
                                for j in range(GT):
                                    mm = nc.tensor.matmul(self.o_ps[g.pair][:, j, :], hid[:, g.pair, j::GT], w, start=False, stop=True,
                                                          skip_group_check=True)
                                mm.then_inc(sg.msg.sem, 1)
                    g = t.at({"sum": 2, "max": 3, "mlp": 4}[k]) if self.scans else None
                    if g is not None:
                        sg.scanned.wait(eng, g)
                        sg.out_ready.wait(eng, g, back=2)
                        gate(eng, "pe")
                        for j in range(GT):
                            mm = nc.tensor.transpose(self.o_ps[g.pair][:, j, :], self.sc[:, g.pair, j::GT], ident[0:D, 0:D])
                        mm.then_inc(sg.turned_e.sem, 1)
                steps(eng, step, {"sum": 2, "max": 3, "mlp": 4}[k])

            def act(self, eng):
                sg, k = self.sg, self.kind
                if k == "sum" and not self.scans:
                    return

                def step(t):
                    g = t.at(0)
                    if g is not None:
                        sg.summed_e.wait(eng, g)
                        h = self.h_sb[:, g.pair, :]
                        if k == "max":
                            sg.msg.wait(eng, g, back=2)
                            nc.scalar.activation(h, self.s_ps[g.pair][:], ACT.Relu, bias=col("L0_gnn_b1")).then_inc(sg.hidden_e.sem, 1)
                        elif k == "sum":
                            sg.scanned.wait(eng, g, back=2)
                            nc.scalar.copy(h, self.s_ps[g.pair][:]).then_inc(sg.hidden_e.sem, 1)
                        else:
                            sg.hid_sum.wait(eng, g, back=2)
                            nc.scalar.copy(self.t_sb[:, g.pair, :], self.t_ps[0][:]).then_inc(sg.tgt_sb.sem, 1)
                            nc.scalar.copy(h, self.s_ps[g.pair][:]).then_inc(sg.hidden_e.sem, 1)
                    g = t.at(1) if k == "mlp" else None
                    if g is not None:
                        sg.hid_sum.wait(eng, g)
                        sg.msg.wait(eng, g, back=2)
                        nc.scalar.activation(self.hid[:, g.pair, :], self.hid_ps[g.pair][:], ACT.Relu,
                                             bias=col("L3_gnn_msg_b1", HID)).then_inc(sg.hid_sb.sem, 1)
                    g = t.at(2 if k == "mlp" else 1) if self.scans and k != "sum" else None
                    if g is not None:
                        sg.msg.wait(eng, g)
                        sg.scanned.wait(eng, g, back=2)
                        nc.scalar.activation(self.m_sb[:, g.pair, :], self.m_ps[:], ACT.Relu if k == "mlp" else ACT.Identity,
                                             bias=col("L3_gnn_msg_b2" if k == "mlp" else "L0_gnn_b2")).then_inc(sg.msg_sb.sem, 1)
                    g = t.at({"sum": 2, "max": 3, "mlp": 4}[k]) if self.scans else None
                    if g is not None:
                        sg.turned_e.wait(eng, g)
                        sg.stored.wait(eng, g, 1, back=1)
                        nc.scalar.copy(self.outb[:, g.slot], self.o_ps[g.pair][:]).then_inc(sg.out_ready.sem, 1)
                steps(eng, step, {"sum": 2, "max": 3, "mlp": 4}[k] if self.scans else 1)

            def dve(self, eng):
                sg, k, v = self.sg, self.kind, nc.vector
                if k == "sum" and not self.scans:
                    return

                def step(t):
                    g = t.at(0) if self.spread else None
                    if g is not None:
                        sg.landed.wait(eng, g, self.loads)
                        sg.summed_e.wait(eng, g, back=2)
                        for w in range(WK):
                            mm = v.tensor_scalar(self.hot[:, g.pair, w, :], self.relb[:, g.slot, :], pcol[0:WP, w:w + 1], None, ALU.is_equal)
                        mm.then_inc(sg.rel_hot.sem, 1)
                    g = t.at({"sum": 1, "max": 2, "mlp": 3}[k]) if self.scans else None
                    if g is not None:
                        (sg.hidden_e if k == "sum" else sg.msg_sb).wait(eng, g)
                        sg.scanned.wait(eng, g, back=1)
                        sg.turned_e.wait(eng, g, back=2)
                        if not g.known or g.g > 0:
                            initial = self.sc[:, 1 - g.pair, GR - 1:GR]
                        else:
                            initial = 0.0
                        data = (self.h_sb if k == "sum" else self.m_sb)[:, g.pair, :]
                        ops = (ALU.add, ALU.max) if k == "max" else (ALU.mult, ALU.add)
                        v.tensor_tensor_scan(self.sc[:, g.pair, :], self.mask[:, g.slot, :], data, initial, *ops).then_inc(sg.scanned.sem, 1)
                    g = t.at(2) if not self.scans else None
                    if g is not None:
                        sg.msg.wait(eng, g)
                        sg.stored.wait(eng, g, 1, back=1)
                        v.tensor_scalar(self.outb[:, g.slot], self.o_ps[g.pair][:], 0.0, None, ALU.max).then_inc(sg.out_ready.sem, 1)
                steps(eng, step, {"sum": 1, "max": 2, "mlp": 3}[k] if self.scans else 2)

        def run(number, make):
            paths = {p: make(p == "general", sigs[p]) for p in ("fast", "general") if mode in (p, "both")}
            with ExitStack() as inner:
                def shared(maker, cache):
                    def get(name, shape, dt=F32):
                        key = (name, tuple(shape))
                        if key not in cache:
                            cache[key] = inner.enter_context(maker(f"pass{number}_{name}_{len(cache)}", shape, dt))
                        return cache[key]
                    return get
                kept_sb, kept_ps = {}, {}
                tmp_, ps_ = shared(nc.sbuf_tensor, kept_sb), shared(nc.psum_tensor, kept_ps)
                for p in paths.values():
                    p.buffers(lambda n, s, d=F32: tmp_(n, s, d)[:], lambda n, s: ps_(n, s))
                fast, general = paths.get("fast"), paths.get("general")

                with nc.Block() as block:
                    @block.sync
                    def _(sp):
                        either(sp, fast and fast.sp, general and general.sp)

                    @block.gpsimd
                    def _(pool):
                        either(pool, fast and fast.pool, general and general.pool)

                    @block.tensor
                    def _(pe):
                        either(pe, fast and fast.pe, general and general.pe)

                    @block.scalar
                    def _(act):
                        either(act, fast and fast.act, general and general.act)

                    @block.vector
                    def _(dve):
                        either(dve, fast and fast.dve, general and general.dve)
            for name, p in paths.items():
                if isinstance(p, NodePass):
                    p.sg.close(p.loads, GT if p.gathered else 0, p.stores)
                else:
                    p.sg.close(p.loads, p.gathers, 1)

        def batch_norm():
            with nc.semaphore("bn_chain") as chain, nc.semaphore("bn_rooted") as rooted, nc.Block() as block:
                @block.vector
                def _(dve):
                    n = [0]

                    def link(ins):
                        n[0] += 1
                        ins.then_inc(chain, 1)
                        dve.wait_ge(chain, n[0])
                    v = nc.vector
                    link(v.bn_aggr(bn[:, 0:2], stats.rearrange("p g s -> p (g s)")))
                    dve.wait_ge(rooted, 1)
                    link(v.reciprocal(bn[:, 3:4], bn[:, 2:3]))
                    link(v.tensor_tensor(bn[:, 4:5], bn[:, 3:4], col("L1_gnn_gamma"), ALU.mult))
                    link(v.tensor_tensor(bn[:, 6:7], bn[:, 4:5], bn[:, 0:1], ALU.mult))
                    link(v.tensor_tensor(bn[:, 5:6], col("L1_gnn_beta"), bn[:, 6:7], ALU.subtract))

                @block.scalar
                def _(act):
                    act.wait_ge(chain, 1)
                    nc.scalar.activation(bn[:, 2:3], bn[:, 1:2], ACT.Sqrt, bias=epsc[0:D, :]).then_inc(rooted, 1)

        sigs = {p: Signals(p) for p in ("fast", "general") if mode in (p, "both")}
        setup()
        run(1, lambda general, sg: NodePass(0, general, sg))
        run(2, lambda general, sg: EdgePass("max", general, sg))
        run(3, lambda general, sg: NodePass(1, general, sg))
        run(4, lambda general, sg: EdgePass("sum", general, sg))
        run(5, lambda general, sg: NodePass(2, general, sg))
        batch_norm()
        run(6, lambda general, sg: NodePass(3, general, sg))
        run(7, lambda general, sg: EdgePass("sum", general, sg))
        run(8, lambda general, sg: NodePass(4, general, sg))
        run(9, lambda general, sg: EdgePass("sum", general, sg))
        run(10, lambda general, sg: NodePass(5, general, sg))
        run(11, lambda general, sg: EdgePass("mlp", general, sg))
        run(12, lambda general, sg: NodePass(6, general, sg))


MODE = "both"
NAMES = ["L0_gnn_W1", "L0_gnn_b1", "L0_gnn_W2", "L0_gnn_b2", "L1_gnn_W1", "L1_gnn_b1", "L1_gnn_gamma",
         "L1_gnn_beta", "L1_gnn_W2", "L1_gnn_b2", "L2_gnn_W", "L2_gnn_b", "L3_gnn_msg_W1", "L3_gnn_msg_b1",
         "L3_gnn_msg_W2", "L3_gnn_msg_b2", "L3_gnn_node_W1", "L3_gnn_node_b1", "L3_gnn_node_W2",
         "L3_gnn_node_b2", "L3_gnn_ln_scale", "L3_gnn_ln_offset"]


def kernel(**inputs):
    import numpy as _np
    import concourse.bacc as _bacc
    from concourse import mybir as _mybir
    from concourse.bass_utils import run_bass_kernel_spmd as _run

    nc = _bacc.Bacc("TRN2", target_bir_lowering=False, num_devices=1)
    arrays = {n: _np.ascontiguousarray(inputs[n]) for n in NAMES}
    more = N - N_TRUE
    for n in ("x", "edge_attr_64"):
        arrays[n] = _np.concatenate([_np.asarray(inputs[n]), _np.zeros((more, D), _np.float32)])
    arrays["src"] = _np.concatenate([_np.asarray(inputs["src"]), _np.zeros((more,), _np.int32)])
    arrays["dst"] = _np.concatenate([_np.full((1,), -1, _np.int32), _np.asarray(inputs["dst"]),
                                     _np.arange(N_TRUE, N + 1, dtype=_np.int32)])
    aps = {n: nc.dram_tensor(f"in_{n}", v.shape, _mybir.dt.from_np(v.dtype), kind="ExternalInput").ap()
           for n, v in arrays.items()}
    out = nc.dram_tensor("out", (N, D), F32, kind="ExternalOutput").ap()
    build(nc, MODE, aps, out)
    r = _run(nc, [{f"in_{n}": v for n, v in arrays.items()}], core_ids=[0])
    return r.results[0]["out"][:N_TRUE]
```

```python
from contextlib import ExitStack

import concourse.bass as bass
from concourse import mybir

F32 = mybir.dt.float32
F16 = mybir.dt.float16
I32 = mybir.dt.int32
ALU = mybir.AluOpType
ACT = mybir.ActivationFunctionType
AX_X = mybir.AxisListType.X
RMAX = bass.bass_isa.ReduceOp.max

P = 128
D = 64
HID = 128
N_TRUE = 50000
TILES = 392
GT = 4
GROUPS = TILES // GT
GR = GT * P
N = TILES * P
WP, WK = 96, 2
WIN = WP * WK
MW = D + 2
UNROLL = 4
AHEAD = 3
EPS = 1e-5
SLOPE = 0.01
FAR = -3.0e38


class Turn:

    def __init__(self, i, part, n):
        self.i, self.part, self.n, self.begun = i, part, n, 0
        self.known = isinstance(i, int)

    def later(self, steps):
        t = Turn(self.i, self.part, self.n)
        t.begun = self.begun + steps
        return t

    def at(self, lag):
        lag = lag + self.begun
        slot = (self.part - lag) % UNROLL
        turn = self.i + (self.part - lag - slot) // UNROLL
        g = self.i * UNROLL + (self.part - lag)
        if self.known and not 0 <= g < self.n:
            return None
        return Group(g, turn, slot, self.known)


class Group:

    def __init__(self, g, turn, slot, known):
        self.g, self.turn, self.slot, self.pair, self.known = g, turn, slot, slot % 2, known

    def from_(self, k):
        return not self.known or self.g >= k


class Tally:

    def __init__(self, sem):
        self.sem, self.base, self.used = sem, 0, False

    def after(self, t, back=0):
        self.used = True
        return t.g + (1 - back + self.base)


class Landing:

    def __init__(self, sems):
        self.sems, self.base = sems, [0] * len(sems)

    def after(self, t, dmas, back=0):
        return t.turn * (16 * dmas) + ((1 - back) * 16 * dmas + self.base[t.slot])

    def held(self, slot, n):
        return (n - slot + UNROLL - 1) // UNROLL

    def wait_all(self, eng, dmas, n):
        for s in range(UNROLL):
            eng.wait_ge(self.sems[s], self.held(s, n) * 16 * dmas + self.base[s])

    def close(self, dmas, n):
        for s in range(UNROLL):
            self.base[s] += self.held(s, n) * 16 * dmas


def steps(eng, step, lag, n=GROUPS):
    head = -(-(lag + UNROLL) // UNROLL)
    loop = n // UNROLL
    for s in range(head * UNROLL):
        step(Turn(s // UNROLL, s % UNROLL, n))
    with eng.Fori(head, loop) as i:
        for part in range(UNROLL):
            step(Turn(i, part, n))
    for s in range(loop * UNROLL, n + lag):
        step(Turn(s // UNROLL, s % UNROLL, n))


def build(nc, mode, a, out):
    with ExitStack() as ctx:
        def sb(name, shape, dt=F32):
            return ctx.enter_context(nc.sbuf_tensor(name, shape, dt))[:]

        def sem(name):
            return ctx.enter_context(nc.semaphore(name))

        def dram(name, shape, dt=F32):
            return nc.dram_tensor(name, shape, dt).ap()

        tabP = dram("tabP", (N, D))
        tabQ = [dram(f"tabQ{k}", (N, D)) for k in range(2)]
        msgs = dram("msgs", (N + P, MW))
        yT = dram("yT", (D, N))
        relrow = dram("relrow", (N,), F16)
        farrow = dram("farrow", (N,))
        keeprow = dram("keeprow", (N,))
        firstnode = dram("firstnode", (TILES,), I32)
        fetchidx = dram("fetchidx", (GROUPS, P, GT), I32)

        xs = sb("xs", [P, TILES, D])
        deg = sb("deg", [P, TILES])
        dinv = sb("dinv", [P, TILES])
        invdeg = sb("invdeg", [P, TILES])
        blockf = sb("blockf", [P, TILES])
        starts = sb("starts", [1, TILES], I32)
        firsts = sb("firsts", [1, TILES], I32)
        flag = sb("flag", [1, 1], I32)
        ident = sb("ident", [P, P])
        iota = sb("iota", [P, P])
        pcol = sb("pcol", [P, WK])
        stats = sb("stats", [D, GROUPS, 6])
        bn = sb("bn", [D, 8])
        epsc = sb("epsc", [P, 1])

        w1raw = sb("w1raw", [D, 2, D])
        w1 = sb("w1", [D, 2, D])
        w2 = sb("w2", [D, D])
        wg1 = sb("wg1", [D, D])
        wg2 = sb("wg2", [D, D])
        wl2 = sb("wl2", [P, D])
        wmse = sb("wmse", [P, HID])
        wmt = sb("wmt", [D, HID])
        wm2 = sb("wm2", [HID, D])
        wn1 = sb("wn1", [P, HID])
        wn2 = sb("wn2", [HID, D])
        COLS = ["L0_gnn_b1", "L0_gnn_b2", "L1_gnn_b1", "L1_gnn_gamma", "L1_gnn_beta", "L3_gnn_msg_b1",
                "L3_gnn_msg_b2", "L3_gnn_node_b1"]
        ROWS = ["L1_gnn_b2", "L2_gnn_b", "L3_gnn_node_b2", "L3_gnn_ln_scale", "L3_gnn_ln_offset"]
        cols = sb("cols", [P, len(COLS)])
        rows = sb("rows", [P, len(ROWS), D])
        b2row = sb("b2row", [1, GT, D])
        ones1 = sb("ones1", [1, P])

        def col(name, k=D):
            return cols[0:k, COLS.index(name):COLS.index(name) + 1]

        def row(name):
            return rows[:, ROWS.index(name):ROWS.index(name) + 1, :].to_broadcast([P, GT, D])

        passed = {e: sem(f"passed_{e}") for e in ("pe", "pool", "dve", "sp")}

        def gate(eng, name):
            eng.sem_inc(passed[name], 1)

        def over4(v):
            return v.unsqueeze(2).to_broadcast([P, GT, D])

        def window_starts(eng, table, g):
            _, values = nc.values_load_multi_w_load_instructions(
                table[0:1, bass.ds(g * GT, GT)], engines=(eng.engine,), min_val=0, max_val=N - WIN,
                skip_runtime_bounds_check_because="VectorE limits every start to N - WIN, and none is negative")
            return values

        def setup():
            with ExitStack() as inner:
                def tmp(name, shape, dt=F32):
                    return inner.enter_context(nc.sbuf_tensor(name, shape, dt))[:]

                def sig(name):
                    return inner.enter_context(nc.semaphore(name))

                E98 = GROUPS
                cur, nxt, prv = (tmp(n, [E98, GR], I32) for n in ("cur", "nxt", "prv"))
                last, lastt, far, keep, rel = (tmp(n, [E98, GR]) for n in ("last", "lastt", "far", "keep", "rel"))
                tgts = tmp("tgts", [E98, GR, MW - D])
                relh = tmp("relh", [E98, GR], F16)
                first4 = tmp("first4", [E98, GT])
                first4i = tmp("first4i", [E98, GT], I32)
                relmax = tmp("relmax", [P, 1])
                relall = tmp("relall", [P, 1])
                dsti, loi, hii = (tmp(n, [P, TILES], I32) for n in ("dsti", "loi", "hii"))
                lo, hi = (tmp(n, [P, TILES]) for n in ("lo", "hi"))
                ioti = tmp("ioti", [P, TILES], I32)
                ioth = tmp("ioth", [P, TILES], F16)
                hotlo = tmp("hotlo", [P, UNROLL, P], F16)
                hothi = tmp("hothi", [P, UNROLL, TILES], F16)
                ones = tmp("ones", [P, P])
                below = tmp("below", [P, P])
                degp = tmp("degp", [P, TILES])
                tot, incl, excl, st, has = (tmp(n, [P, TILES]) for n in ("tot", "incl", "excl", "st", "has"))
                idxf = tmp("idxf", [P, TILES])
                idxi = tmp("idxi", [P, TILES], I32)
                sc = tmp("sc", [1, TILES])
                over = tmp("over", [1, 8])
                blocki = tmp("blocki", [P, TILES], I32)
                pcoli = tmp("pcoli", [P, WK], I32)
                zero = tmp("zero", [P, MW])
                hist = inner.enter_context(nc.psum_tensor("hist", [P, TILES], F32))
                prefix = inner.enter_context(nc.psum_tensor("prefix", [P, TILES], F32))
                totals = inner.enter_context(nc.psum_tensor("totals", [P, TILES], F32))

                weights_in, edges_in, dst_in = sig("weights_in"), sig("edges_in"), sig("dst_in")
                rows_out, first_out, first_in = sig("rows_out"), sig("first_out"), sig("first_in")
                made = sig("made")
                chain = sig("chain")
                hot, hot_used = Tally(sig("hot")), Tally(sig("hot_used"))
                sums = sig("sums")
                rooted = sig("rooted")
                start_ready, idx_ready, zero_out = sig("start_ready"), sig("idx_ready"), sig("zero_out")
                rel_ready, relall_ready = sig("rel_ready"), sig("relall_ready")
                rows_ready, firsts_ready = sig("rows_ready"), sig("firsts_ready")
                deg_ready = sig("deg_ready")
                zero_ready = sig("zero_ready")

                dstp = a["dst"]
                loads = [(w1raw[:], a["L0_gnn_W1"].rearrange("(h k) n -> k h n", h=2)),
                         (w2[:], a["L0_gnn_W2"]), (wg1[:], a["L1_gnn_W1"]), (wg2[:], a["L1_gnn_W2"]),
                         (wl2[:], a["L2_gnn_W"]),
                         (wmse[0:D, :], a["L3_gnn_msg_W1"][0:D, :]),
                         (wmt[:], a["L3_gnn_msg_W1"][D:2 * D, :]),
                         (wmse[D:P, :], a["L3_gnn_msg_W1"][2 * D:3 * D, :]),
                         (wm2[:], a["L3_gnn_msg_W2"]), (wn1[:], a["L3_gnn_node_W1"]), (wn2[:], a["L3_gnn_node_W2"])]
                for k, n in enumerate(COLS):
                    size = a[n].shape[0]
                    loads.append((cols[0:size, k:k + 1], a[n].rearrange("(n o) -> n o", o=1)))
                for k, n in enumerate(ROWS):
                    loads.append((rows[:, k, :], a[n].rearrange("(o n) -> o n", o=1).to_broadcast([P, D])))
                for j in range(GT):
                    loads.append((b2row[:, j, :], a["L3_gnn_msg_b2"].rearrange("(o n) -> o n", o=1)))

                with nc.Block() as block:
                    @block.sync
                    def _(sp):
                        sp.dma_start(dsti[:], dstp[1:1 + N].rearrange("(p c) -> p c", p=P)).then_inc(dst_in, 16)
                        for t, off in ((cur, 1), (nxt, 2), (prv, 0)):
                            sp.dma_start(t[:], dstp[off:off + N].rearrange("(q c) -> q c", q=E98)).then_inc(edges_in, 16)
                        sp.wait_ge(rows_ready, 5)
                        for t, to in ((relh, relrow), (far, farrow), (keep, keeprow)):
                            sp.dma_start(to.rearrange("(q c) -> q c", q=E98), t).then_inc(rows_out, 16)
                        sp.dma_start(msgs[0:N, D:MW].rearrange("(q c) f -> q c f", q=E98), tgts).then_inc(rows_out, 16)
                        sp.dma_start(firstnode.rearrange("(q j) -> q j", q=E98), first4i[:]).then_inc(first_out, 16)
                        sp.wait_ge(first_out, 16)
                        sp.dma_start(firsts[:], firstnode.rearrange("(o t) -> o t", o=1)).then_inc(first_in, 16)
                        sp.wait_ge(rows_out, 64)
                        sp.wait_ge(idx_ready, 1)
                        sp.dma_start(fetchidx.rearrange("g p j -> p g j"), idxi.rearrange("p (g j) -> p g j", j=GT)
                                     ).then_inc(rows_out, 16)
                        sp.wait_ge(zero_ready, 1)
                        sp.dma_start(msgs[N:N + P, :], zero[:]).then_inc(zero_out, 16)
                        sp.wait_ge(rows_out, 80)
                        sp.wait_ge(first_in, 16)
                        sp.wait_ge(zero_out, 16)

                    @block.scalar
                    def _(act):
                        for to, frm in loads:
                            act.dma_start(to, frm).then_inc(weights_in, 16)
                        act.wait_ge(weights_in, 16 * len(loads))
                        act.wait_ge(deg_ready, 1)
                        nc.scalar.activation(dinv[:], degp[:], ACT.Sqrt).then_inc(rooted, 1)

                    @block.gpsimd
                    def _(pool):
                        nc.gpsimd.iota(ioti[:], [[1, TILES]], base=0, channel_multiplier=0).then_inc(made, 1)
                        nc.gpsimd.iota(blocki[:], [[P, TILES]], base=0, channel_multiplier=0).then_inc(made, 1)
                        nc.gpsimd.iota(pcoli[:], [[1, WK]], base=0, channel_multiplier=WK).then_inc(made, 1)
                        nc.gpsimd.memset(ident[:], 0.0).then_inc(made, 1)
                        nc.gpsimd.memset(ones[:], 1.0).then_inc(made, 1)
                        nc.gpsimd.memset(ones1[:], 1.0).then_inc(made, 1)
                        nc.gpsimd.memset(relmax[:], 0.0).then_inc(made, 1)
                        nc.gpsimd.memset(zero[:], 0.0).then_inc(zero_ready, 1)
                        nc.gpsimd.memset(epsc[:], EPS).then_inc(made, 1)
                        pool.wait_ge(made, 8)
                        nc.gpsimd.affine_select(out=ident[:], in_=ident[:], compare_op=ALU.not_equal, fill=1.0, base=0,
                                                pattern=[[-1, P]], channel_multiplier=1).then_inc(made, 1)
                        nc.gpsimd.affine_select(out=below[:], in_=ones[:], compare_op=ALU.is_ge, fill=0.0, base=-1,
                                                pattern=[[1, P]], channel_multiplier=-1).then_inc(made, 1)
                        pool.wait_ge(rel_ready, 1)
                        nc.gpsimd.partition_all_reduce(relall[:], relmax[:], P, RMAX).then_inc(relall_ready, 1)

                    @block.tensor
                    def _(pe):
                        def count(t):
                            g = t.at(0)
                            if g is None:
                                return
                            pe.wait_ge(hot.sem, hot.after(g))
                            gate(pe, "pe")
                            nc.tensor.matmul(hist[:], hotlo[:, g.slot, :], hothi[:, g.slot, :],
                                             start=g.known and g.g == 0, stop=g.known and g.g == TILES - 1,
                                             skip_group_check=True).then_inc(hot_used.sem, 1)
                        steps(pe, count, 0, TILES)
                        pe.wait_ge(sums, 1)
                        pe.wait_ge(made, 10)
                        nc.tensor.matmul(prefix[:], below[:], deg[:], start=True, stop=True)
                        nc.tensor.matmul(totals[:], ones[:], deg[:], start=True, stop=True).then_inc(sums, 1)

                    @block.vector
                    def _(dve):
                        n = [0]

                        def link(ins):
                            n[0] += 1
                            ins.then_inc(chain, 1)
                            dve.wait_ge(chain, n[0])

                        v = nc.vector
                        dve.wait_ge(made, 8)
                        v.tensor_copy(ioth[:], ioti[:]).then_inc(chain, 1)
                        v.tensor_copy(iota[:], ioti[:, 0:P]).then_inc(chain, 1)
                        v.tensor_copy(pcol[:], pcoli[:]).then_inc(chain, 1)
                        n[0] = 3
                        link(v.tensor_copy(blockf[:], blocki[:]))
                        dve.wait_ge(dst_in, 16)
                        link(v.tensor_scalar(loi[:], dsti[:], P - 1, None, ALU.bitwise_and))
                        link(v.tensor_scalar(hii[:], dsti[:], 7, None, ALU.logical_shift_right))
                        link(v.tensor_copy(lo[:], loi[:]))
                        link(v.tensor_copy(hi[:], hii[:]))

                        def onehot(t):
                            g = t.at(0)
                            if g is None:
                                return
                            if g.from_(UNROLL):
                                dve.wait_ge(hot_used.sem, hot_used.after(g, UNROLL))
                            v.tensor_scalar(hotlo[:, g.slot, :], ioth[:, 0:P], lo[:, bass.ds(g.g, 1)], None, ALU.is_equal)
                            v.tensor_scalar(hothi[:, g.slot, :], ioth[:], hi[:, bass.ds(g.g, 1)], None,
                                            ALU.is_equal).then_inc(hot.sem, 1)
                        steps(dve, onehot, 0, TILES)

                        dve.wait_ge(edges_in, 48)
                        link(v.tensor_tensor(last[:], cur[:], nxt[:], ALU.not_equal))
                        link(v.scalar_tensor_tensor(out=lastt[:], in0=cur[:], scalar=1.0, in1=last[:], op0=ALU.add, op1=ALU.mult))
                        v.tensor_scalar(tgts[:, :, 1], lastt[:], -1.0, None, ALU.add)
                        v.tensor_copy(tgts[:, :, 0], cur[:])
                        link(v.tensor_tensor(keep[:], cur[:], prv[:], ALU.is_equal))
                        v.tensor_scalar(far[:], keep[:], -FAR, FAR, ALU.mult, ALU.add).then_inc(rows_ready, 1)
                        link(v.tensor_scalar(first4[:], cur.rearrange("q (j c) -> q j c", j=GT)[:, :, 0], float(N - WIN), None, ALU.min))
                        v.tensor_copy(first4i[:], first4[:]).then_inc(rows_ready, 1)
                        link(v.tensor_tensor(rel.rearrange("q (j c) -> q j c", j=GT), cur.rearrange("q (j c) -> q j c", j=GT),
                                             first4.unsqueeze(2).to_broadcast([E98, GT, P]), ALU.subtract))
                        link(v.tensor_copy(relh, rel))
                        v.tensor_reduce(relmax[0:E98, :], rel[:], AX_X, ALU.max).then_inc(rel_ready, 1)
                        dve.sem_inc(rows_ready, 3)

                        dve.wait_ge(hot_used.sem, TILES)
                        v.tensor_copy(deg[:], hist[:]).then_inc(sums, 1)
                        dve.wait_ge(sums, 2)
                        v.tensor_scalar(degp[:], deg[:], 1.0, None, ALU.add).then_inc(deg_ready, 1)
                        link(v.tensor_scalar(invdeg[:], deg[:], 1.0, None, ALU.max))
                        link(v.reciprocal(invdeg[:], invdeg[:]))
                        link(v.tensor_copy(tot[:], totals[:]))
                        link(v.tensor_scalar(has[:], deg[:], 1.0, None, ALU.min))
                        link(v.tensor_tensor_scan(incl[:], iota[:, 0:1].to_broadcast([P, TILES]), tot[:], 0.0, ALU.add, ALU.add))
                        link(v.tensor_tensor(excl[:], incl[:], tot[:], ALU.subtract))
                        link(v.tensor_scalar(sc[:], excl[0:1, :], float(N - WIN), None, ALU.min))
                        v.tensor_copy(starts[:], sc[:]).then_inc(start_ready, 1)
                        link(v.tensor_tensor(st[:], excl[:], prefix[:], ALU.add))
                        link(v.scalar_tensor_tensor(out=idxf[:], in0=st[:], scalar=float(-1 - N), in1=deg[:], op0=ALU.add, op1=ALU.add))
                        link(v.tensor_tensor(idxf[:], idxf[:], has[:], ALU.mult))
                        link(v.tensor_scalar(idxf[:], idxf[:], float(N), None, ALU.add))
                        v.tensor_copy(idxi[:], idxf[:]).then_inc(idx_ready, 1)
                        link(v.tensor_tensor(has[0:1, :], sc[:], blockf[0:1, :], ALU.subtract))
                        link(v.tensor_reduce(over[:, 4:5], has[0:1, :], AX_X, ALU.max))
                        link(v.tensor_scalar(over[:, 5:6], over[:, 4:5], float((1 + AHEAD) * GR - (GT - 1) * P - WIN), None, ALU.is_gt))
                        link(v.tensor_tensor(sc[:], incl[0:1, :], sc[:], ALU.subtract))
                        link(v.tensor_reduce(over[:, 0:1], sc[:], AX_X, ALU.max))
                        link(v.tensor_scalar(over[:, 1:2], over[:, 0:1], float(WIN), None, ALU.is_gt))
                        dve.wait_ge(relall_ready, 1)
                        link(v.tensor_scalar(over[:, 2:3], relall[0:1, :], float(WIN - 1), None, ALU.is_gt))
                        link(v.tensor_tensor(over[:, 3:4], over[:, 1:2], over[:, 2:3], ALU.max))
                        link(v.tensor_tensor(over[:, 6:7], over[:, 3:4], over[:, 5:6], ALU.max))
                        link(v.tensor_copy(flag[:], over[:, 6:7]))
                        dve.wait_ge(rooted, 1)
                        link(v.reciprocal(dinv[:], dinv[:]))
                        dve.wait_ge(weights_in, 16 * len(loads))
                        link(v.tensor_tensor(w1[:, 0, :], w1raw[:, 0, :], w1raw[:, 1, :], ALU.subtract))
                        link(v.tensor_copy(w1[:, 1, :], w1raw[:, 1, :]))
        class Signals:

            def __init__(self, path):
                self.path, self.tallies = path, []
                self.landed = Landing([sem(f"{path}_landed{k}") for k in range(UNROLL)])
                self.fetched = Landing([sem(f"{path}_fetched{k}") for k in range(UNROLL)])
                self.stored = Landing([sem(f"{path}_stored{k}") for k in range(UNROLL)])

            def tally(self, name):
                self.tallies.append(Tally(sem(f"{self.path}_{name}")))
                return self.tallies[-1]

            def close(self, loads, gathers, stores):
                for t in self.tallies:
                    if t.used:
                        t.base, t.used = t.base + GROUPS, False
                self.landed.close(loads, GROUPS)
                self.fetched.close(gathers, GROUPS)
                self.stored.close(stores, GROUPS)

            def close_own(self):
                self.owned.close(1, GROUPS)

        class NodeSignals(Signals):
            def __init__(self, path):
                super().__init__(path)
                tally = self.tally
                self.owned = Landing([sem(f"{path}_owned{k}") for k in range(UNROLL)])
                self.rel = tally("rel")
                self.hot = tally("hot")
                self.joined = tally("joined")
                self.mixed = tally("mixed")
                self.biased = tally("biased")
                self.x_new = tally("x_new")
                self.summed = tally("summed")
                self.centred = tally("centred")
                self.squared = tally("squared")
                self.varied = tally("varied")
                self.inverted = tally("inverted")
                self.normed = tally("normed")
                self.scaled = tally("scaled")
                self.offset = tally("offset")
                self.with_h = tally("with_h")
                self.final = tally("final")
                self.shifted = tally("shifted")
                self.stat = tally("stat")
                self.agged = tally("agged")
                self.turned = tally("turned")
                self.multiplied = tally("multiplied")
                self.hid_sum = tally("hid_sum")
                self.rooted = tally("rooted")
                self.turned_sb = tally("turned_sb")
                self.hidden = tally("hidden")
                self.affined = tally("affined")

        class EdgeSignals(Signals):
            def __init__(self, path):
                super().__init__(path)
                tally = self.tally
                self.rel_hot = tally("rel_hot")
                self.summed_e = tally("summed_e")
                self.hidden_e = tally("hidden_e")
                self.tgt_sb = tally("tgt_sb")
                self.hid_sum = tally("ehid_sum")
                self.hid_sb = tally("hid_sb")
                self.msg = tally("msg")
                self.msg_sb = tally("msg_sb")
                self.scanned = tally("scanned")
                self.turned_e = tally("turned_e")
                self.out_ready = tally("out_ready")

        def either(eng, fast, general):
            if mode != "both":
                return (general if mode == "general" else fast)(eng)
            v = nc.values_load(flag[0:1, 0:1], engines=(eng.engine,), min_val=0, max_val=1)
            with eng.If(v > 0):
                general(eng)
            if fast:
                with eng.Else():
                    fast(eng)

        def tabrows(tab, g):
            return tab.rearrange("(g j p) f -> g p j f", p=P, j=GT)[bass.ds(g, 1)].rearrange("o p j f -> (o p) j f")

        def edgerows(tab, g):
            return tab.rearrange("(g p j) f -> g p j f", p=P, j=GT)[bass.ds(g, 1)].rearrange("o p j f -> (o p) j f")

        def edgecols(vec, g, parts):
            return vec.rearrange("(g c) -> g c", c=GR)[bass.ds(g, 1)].to_broadcast([parts, GR])

        class NodePass:

            def __init__(self, kind, general, sg, qin, qout, banks, source=None):
                self.kind, self.general, self.sg, self.qin, self.qout = kind, general, sg, qin, qout
                self.banks, self.source = banks, source
                self.windowed = kind in (1, 2, 4, 5, 6) and not general
                self.gathered = kind in (1, 2, 4, 5, 6) and general
                self.norms = kind in (0, 1, 4, 5)
                self.own = kind in (2, 4, 5, 6)
                self.late = kind in (5, 6)
                self.loads = (4 if self.windowed else 0) + (1 if self.gathered else 0) + (kind in (0, 3))
                self.gathers = GT if self.gathered else 0
                self.stores = 2 if kind == 0 else 1
                mix = {0: 0, 3: 1, 6: 1}.get(kind, 2)
                self.mix = mix
                self.turn = {0: 2, 1: mix + 2, 2: mix + 1, 5: mix + 1, 6: mix + 1}.get(kind)
                self.product = {0: 3, 1: mix + 3, 3: 2, 5: mix + 2, 6: mix + 3}.get(kind)
                self.norm = self.product + 1 if self.late else mix
                self.scale = self.norm + 1
                self.evac = self.product + 1 if kind in (0, 1, 3) else None
                self.store = 1 + (self.evac or (self.turn if kind == 2 else self.scale))

            def bank(self, tensors, g):
                return tensors[g.pair % len(tensors)]

            def buffers(self, tmp, ps):
                k = self.kind
                if self.windowed:
                    self.win = tmp("win", [WP, UNROLL, GT, WK, MW])
                    self.hot = tmp("hot", [WP, 2, GT, WK, P])
                    self.relw = tmp("relw", [WP, 2, GT, WK])
                    self.agg = [ps(f"agg{b}", [P, GT, D]) for b in range(self.banks["agg"])]
                if self.gathered:
                    self.fidx = tmp("fidx", [P, UNROLL, GT], I32)
                    self.aggs = tmp("aggs", [P, UNROLL, GT, MW])
                if self.own and not self.late:
                    self.ownb = tmp("ownb", [P, UNROLL, GT, D])
                if self.late:
                    self.hn = tmp("hn", [P, UNROLL, GT, P])
                if k == 3:
                    self.yin = tmp("yin", [D, UNROLL, GR])
                    self.zb = tmp("zb", [D, 2, GR])
                    self.zs = tmp("zs", [D, 2, GR])
                if k == 2:
                    self.mixb = tmp("mix", [P, 2, GT, D])
                    self.yout = tmp("yout", [D, UNROLL, GR])
                if k == 4:
                    self.mixb = tmp("mix", [P, 2, GT, D])
                    self.hout = tmp("hout", [P, UNROLL, GT, D])
                if k == 5:
                    self.hout = tmp("hout", [P, UNROLL, GT, D])
                if self.norms or k == 6:
                    self.s1, self.s2, self.sd, self.rs = (tmp(n, [P, 2, GT]) for n in ("s1", "s2", "sd", "rs"))
                    self.xc, self.sq = tmp("xc", [P, 2, GT, D]), tmp("sq", [P, 2, GT, D])
                if k in (0, 1):
                    self.hb = tmp("hb", [P, 2, GT, D])
                if k == 6:
                    self.yb, self.fb = tmp("yb", [P, 2, GT, D]), tmp("fb", [P, UNROLL, GT, D])
                    self.hidp = [ps("hidp0", [HID, GR])]
                    self.hids = tmp("hids", [HID, 2, GR])
                self.rowsT = P if self.late else D
                if k != 4 and k != 3:
                    self.tp = [ps(f"tp{b}", [self.rowsT, GR]) for b in range(self.banks["tp"])]
                if k in (0, 1, 5, 6):
                    self.ts = tmp("ts", [self.rowsT, 2, GR])
                if k in (0, 1, 3, 5, 6):
                    self.width = 2 * D if k == 0 else D
                    self.mp = [ps(f"mp{b}", [P, GT, self.width]) for b in range(self.banks["mp"])]
                if k in (0, 1, 3):
                    self.outb = tmp("outb", [P, UNROLL, GT, self.width])

            def sp(self, eng):
                sg, k = self.sg, self.kind

                def step(t):
                    g = t.at(0)
                    if g is not None:
                        land = sg.landed.sems[g.slot]
                        if k == 0:
                            if g.from_(UNROLL):
                                eng.wait_ge(sg.summed.sem, sg.summed.after(g, UNROLL))
                            gate(eng, "sp")
                            eng.dma_start(xs[:, bass.ds(g.g * GT, GT), :], tabrows(a["x"], g.g)).then_inc(land, 16)
                        if k == 3:
                            if g.from_(UNROLL):
                                eng.wait_ge(sg.affined.sem, sg.affined.after(g, UNROLL))
                            gate(eng, "sp")
                            eng.dma_start(self.yin[:, g.slot, :], yT[:, bass.ds(g.g * GR, GR)]).then_inc(land, 16)
                        if self.gathered:
                            if g.from_(UNROLL):
                                if g.from_(UNROLL):
                                    eng.wait_ge(sg.fetched.sems[g.slot], sg.fetched.after(g, GT, 1))
                                gate(eng, "sp")
                            eng.dma_start(self.fidx[:, g.slot, :], fetchidx[bass.ds(g.g, 1)].rearrange("o p j -> (o p) j")).then_inc(land, 16)
                        if self.windowed:
                            self.wait_for_messages(eng, g)
                            if g.from_(UNROLL):
                                eng.wait_ge(sg.agged.sem, sg.agged.after(g, UNROLL))
                            gate(eng, "sp")
                            for j, s in enumerate(window_starts(eng, starts, g.g)):
                                eng.dma_start(self.win[:, g.slot, j, :, :],
                                              msgs[bass.ds(s, WIN), :].rearrange("(p k) f -> p k f", k=WK)).then_inc(land, 16)
                    g = t.at(self.mix) if self.own else None
                    if g is not None:
                        if g.from_(UNROLL):
                            if self.late:
                                eng.wait_ge(sg.turned.sem, sg.turned.after(g, UNROLL))
                                gate(eng, "sp")
                            if k == 6:
                                eng.wait_ge(sg.with_h.sem, sg.with_h.after(g, UNROLL))
                            if not self.late:
                                eng.wait_ge(sg.mixed.sem, sg.mixed.after(g, UNROLL))
                        gate(eng, "sp")
                        to = self.hn[:, g.slot, :, 0:D] if self.late else self.ownb[:, g.slot]
                        eng.dma_start(to, tabrows(self.qin, g.g)).then_inc(sg.owned.sems[g.slot], 16)
                return step, self.mix if self.own else 0

            def wait_for_messages(self, eng, g):
                if self.source is None:
                    return
                if not g.known:
                    groups = [Group(g.g + AHEAD, g.turn + (g.slot + AHEAD) // UNROLL, (g.slot + AHEAD) % UNROLL, False)]
                else:
                    groups = [Group(e, e // UNROLL, e % UNROLL, True)
                              for e in range(0 if g.g == 0 else g.g + AHEAD, min(g.g + AHEAD, GROUPS - 1) + 1)]
                for e in groups:
                    eng.wait_ge(self.source.sg.stored.sems[e.slot], self.source.sg.stored.after(e, 1))
                gate(eng, "sp")

            def pool(self, eng):
                sg = self.sg
                if not self.gathered:
                    return None

                def step(t):
                    g = t.at(0)
                    if g is None:
                        return
                    eng.wait_ge(sg.landed.sems[g.slot], sg.landed.after(g, self.loads))
                    if g.from_(UNROLL):
                        eng.wait_ge(sg.mixed.sem, sg.mixed.after(g, UNROLL))
                    gate(eng, "pool")
                    for j in range(GT):
                        nc.gpsimd.indirect_dma_start(self.aggs[:, g.slot, j, :], None, msgs,
                                                     bass.IndirectOffsetOnAxis(ap=self.fidx[:, g.slot, j:j + 1], axis=0)
                                                     ).then_inc(sg.fetched.sems[g.slot], 16)
                return step, 0

            def pe(self, eng):
                sg, k = self.sg, self.kind

                def step(t):
                    g = t.at(self.product) if self.product else None
                    if g is not None:
                        of = {3: sg.shifted, 6: sg.hidden}.get(k, sg.turned_sb)
                        eng.wait_ge(of.sem, of.after(g))
                        of = sg.x_new if self.late else sg.scaled
                        if g.from_(len(self.mp)):
                            eng.wait_ge(of.sem, of.after(g, len(self.mp)))
                        gate(eng, "pe")
                        src = self.zs if k == 3 else self.hids if k == 6 else self.ts
                        w = {0: w1.rearrange("k h n -> k (h n)"), 1: wg1, 3: wg2, 5: wl2, 6: wn2}[k]
                        for j in range(GT):
                            mm = nc.tensor.matmul(self.bank(self.mp, g)[:, j, :], src[:, g.pair, bass.ts(j, P)], w, start=True, stop=True,
                                                  skip_group_check=True)
                        mm.then_inc(sg.multiplied.sem, 1)
                    g = t.at(self.turn + 1) if k == 6 else None
                    if g is not None:
                        eng.wait_ge(sg.turned_sb.sem, sg.turned_sb.after(g))
                        if g.from_(1):
                            eng.wait_ge(sg.hidden.sem, sg.hidden.after(g, 1))
                        gate(eng, "pe")
                        nc.tensor.matmul(self.hidp[0][:], wn1, self.ts[:, g.pair, :], start=True, stop=True
                                         ).then_inc(sg.hid_sum.sem, 1)
                    g = t.at(self.turn) if self.turn else None
                    if g is not None:
                        of = (sg.normed if k in (0, 1) else sg.mixed)
                        eng.wait_ge(of.sem, of.after(g))
                        if self.late:
                            eng.wait_ge(sg.owned.sems[g.slot], sg.owned.after(g, 1))
                        if g.from_(len(self.tp)):
                            eng.wait_ge(sg.turned_sb.sem, sg.turned_sb.after(g, len(self.tp)))
                        gate(eng, "pe")
                        src = self.hn[:, g.slot] if self.late else (self.mixb if k == 2 else self.hb)[:, g.pair]
                        for j in range(GT):
                            mm = nc.tensor.transpose(self.bank(self.tp, g)[:, bass.ts(j, P)], src[:, j, :], ident)
                        mm.then_inc(sg.turned.sem, 1)
                    g = t.at(0) if self.windowed else None
                    if g is not None:
                        eng.wait_ge(sg.hot.sem, sg.hot.after(g))
                        eng.wait_ge(sg.landed.sems[g.slot], sg.landed.after(g, self.loads))
                        if g.from_(len(self.agg)):
                            eng.wait_ge(sg.mixed.sem, sg.mixed.after(g, len(self.agg)))
                        gate(eng, "pe")
                        for j in range(GT):
                            for w in range(WK):
                                mm = nc.tensor.matmul(self.bank(self.agg, g)[:, j, :], self.hot[:, g.pair, j, w, :],
                                                      self.win[:, g.slot, j, w, 0:D], start=w == 0, stop=w == WK - 1,
                                                      skip_group_check=True)
                        mm.then_inc(sg.agged.sem, 1)
                if k == 4 and not self.windowed:
                    return None
                return step, max(self.turn or 0, self.product or 0)

            def act(self, eng):
                sg, k = self.sg, self.kind

                def banks(t):
                    g = t.at(self.turn + 1) if k == 6 else None
                    if g is not None:
                        eng.wait_ge(sg.hid_sum.sem, sg.hid_sum.after(g))
                        if g.from_(2):
                            eng.wait_ge(sg.multiplied.sem, sg.multiplied.after(g, 2))
                        nc.scalar.activation(self.hids[:, g.pair, :], self.hidp[0][:], ACT.Relu,
                                             bias=col("L3_gnn_node_b1", HID)).then_inc(sg.hidden.sem, 1)
                    g = t.at(self.turn) if self.turn else None
                    if g is not None:
                        eng.wait_ge(sg.turned.sem, sg.turned.after(g))
                        if k == 2:
                            if g.from_(UNROLL):
                                eng.wait_ge(sg.stored.sems[g.slot], sg.stored.after(g, self.stores, 1))
                            nc.scalar.activation(self.yout[:, g.slot, :], self.bank(self.tp, g)[:], ACT.Identity,
                                                 bias=col("L1_gnn_b1")).then_inc(sg.turned_sb.sem, 1)
                        else:
                            of = sg.hid_sum if k == 6 else sg.multiplied
                            if g.from_(2):
                                eng.wait_ge(of.sem, of.after(g, 2))
                            nc.scalar.copy(self.ts[:, g.pair, :], self.bank(self.tp, g)[:]).then_inc(sg.turned_sb.sem, 1)
                    g = t.at(0) if k == 3 else None
                    if g is not None:
                        eng.wait_ge(sg.landed.sems[g.slot], sg.landed.after(g, self.loads))
                        if g.from_(2):
                            eng.wait_ge(sg.shifted.sem, sg.shifted.after(g, 2))
                        nc.scalar.activation(self.zb[:, g.pair, :], self.yin[:, g.slot, :], ACT.Identity,
                                             bias=bn[:, 5:6], scale=bn[:, 4:5]).then_inc(sg.affined.sem, 1)

                def root(t):
                    g = t.at(self.norm) if self.norms or k == 6 else None
                    if g is not None:
                        eng.wait_ge(sg.varied.sem, sg.varied.after(g))
                        nc.scalar.activation(self.sd[:, g.pair, :], self.s2[:, g.pair, :], ACT.Sqrt, bias=epsc,
                                             scale=1.0 / D).then_inc(sg.rooted.sem, 1)

                def store(t):
                    g = t.at(self.store)
                    if g is not None:
                        done = sg.stored.sems[g.slot]
                        if k == 0:
                            eng.wait_ge(sg.scaled.sem, sg.scaled.after(g))
                            eng.dma_start(tabrows(tabP, g.g), self.outb[:, g.slot, :, 0:D]).then_inc(done, 16)
                            eng.dma_start(tabrows(self.qout, g.g), self.outb[:, g.slot, :, D:2 * D]).then_inc(done, 16)
                        elif k in (1, 3):
                            eng.wait_ge(sg.scaled.sem, sg.scaled.after(g))
                            eng.dma_start(tabrows(self.qout, g.g), self.outb[:, g.slot]).then_inc(done, 16)
                        elif k == 2:
                            eng.wait_ge(sg.turned_sb.sem, sg.turned_sb.after(g))
                            eng.dma_start(yT[:, bass.ds(g.g * GR, GR)], self.yout[:, g.slot, :]).then_inc(done, 16)
                        elif k in (4, 5):
                            eng.wait_ge(sg.normed.sem, sg.normed.after(g))
                            eng.dma_start(tabrows(self.qout, g.g), self.hout[:, g.slot]).then_inc(done, 16)
                        else:
                            eng.wait_ge(sg.final.sem, sg.final.after(g))
                            eng.dma_start(tabrows(out, g.g), self.fb[:, g.slot]).then_inc(done, 16)
                return [(banks, self.store), (root, self.store), (store, self.store)]

            def dve(self, eng):
                sg, k, v = self.sg, self.kind, nc.vector

                def centre(g, src):
                    gate(eng, "dve")
                    v.tensor_reduce(self.s1[:, g.pair, :], src, AX_X, ALU.add).then_inc(sg.summed.sem, 1)
                    eng.wait_ge(sg.summed.sem, sg.summed.after(g))
                    v.scalar_tensor_tensor(out=self.xc[:, g.pair], in0=over4(self.s1[:, g.pair, :]), scalar=-1.0 / D, in1=src,
                                           op0=ALU.mult, op1=ALU.add).then_inc(sg.centred.sem, 1)
                    eng.wait_ge(sg.centred.sem, sg.centred.after(g))
                    v.tensor_tensor(self.sq[:, g.pair], self.xc[:, g.pair], self.xc[:, g.pair], ALU.mult).then_inc(sg.squared.sem, 1)
                    eng.wait_ge(sg.squared.sem, sg.squared.after(g))
                    if g.from_(2):
                        eng.wait_ge(sg.rooted.sem, sg.rooted.after(g, 2))
                    v.tensor_reduce(self.s2[:, g.pair, :], self.sq[:, g.pair], AX_X, ALU.add).then_inc(sg.varied.sem, 1)

                def feats(g):
                    return xs[:, bass.ds(g.g * GT, GT), :]

                def here(vec, g):
                    return over4(vec[:, bass.ds(g.g * GT, GT)])

                def step(t):
                    g = t.at(self.norm) if self.late else None
                    if g is not None:
                        eng.wait_ge(sg.multiplied.sem, sg.multiplied.after(g))
                        if k == 5:
                            v.tensor_tensor(feats(g), feats(g), self.bank(self.mp, g)[:], ALU.add).then_inc(sg.x_new.sem, 1)
                        else:
                            v.tensor_tensor(self.yb[:, g.pair], self.bank(self.mp, g)[:], row("L3_gnn_node_b2"), ALU.add).then_inc(sg.x_new.sem, 1)
                    g = t.at(self.mix) if k == 6 else None
                    if g is not None:
                        if self.windowed:
                            eng.wait_ge(sg.agged.sem, sg.agged.after(g))
                            agg = self.bank(self.agg, g)[:]
                        elif self.gathered:
                            eng.wait_ge(sg.fetched.sems[g.slot], sg.fetched.after(g, GT))
                            agg = self.aggs[:, g.slot, :, 0:D]
                        if g.from_(UNROLL):
                            eng.wait_ge(sg.turned.sem, sg.turned.after(g, UNROLL))
                        v.tensor_copy(self.hn[:, g.slot, :, D:P], agg).then_inc(sg.mixed.sem, 1)
                        eng.wait_ge(sg.owned.sems[g.slot], sg.owned.after(g, 1))
                        v.tensor_tensor(feats(g), feats(g), self.hn[:, g.slot, :, 0:D], ALU.add).then_inc(sg.with_h.sem, 1)
                    g = t.at(self.evac) if self.evac else None
                    if g is not None:
                        eng.wait_ge(sg.multiplied.sem, sg.multiplied.after(g))
                        if g.from_(UNROLL):
                            eng.wait_ge(sg.stored.sems[g.slot], sg.stored.after(g, self.stores, 1))
                        if k == 0:
                            v.tensor_copy(self.outb[:, g.slot], self.bank(self.mp, g)[:]).then_inc(sg.scaled.sem, 1)
                        else:
                            v.tensor_tensor(self.outb[:, g.slot], self.bank(self.mp, g)[:], here(dinv, g), ALU.mult).then_inc(sg.scaled.sem, 1)
                    g = t.at(0) if self.windowed else None
                    if g is not None:
                        eng.wait_ge(sg.landed.sems[g.slot], sg.landed.after(g, self.loads))
                        c = D + (1 if k == 1 else 0)
                        v.tensor_tensor(self.relw[:, g.pair], self.win[:, g.slot, :, :, c],
                                        blockf[0:WP, bass.ds(g.g * GT, GT)].unsqueeze(2).to_broadcast([WP, GT, WK]),
                                        ALU.subtract).then_inc(sg.rel.sem, 1)
                        eng.wait_ge(sg.rel.sem, sg.rel.after(g))
                        if g.from_(2):
                            eng.wait_ge(sg.agged.sem, sg.agged.after(g, 2))
                        v.tensor_tensor(self.hot[:, g.pair].rearrange("p j k n -> p (j k) n"),
                                        iota[0:WP, :].unsqueeze(1).to_broadcast([WP, GT * WK, P]),
                                        self.relw[:, g.pair].rearrange("p j k -> p (j k)").unsqueeze(2).to_broadcast([WP, GT * WK, P]),
                                        ALU.is_equal).then_inc(sg.hot.sem, 1)
                    g = t.at(self.scale) if self.norms or k == 6 else None
                    if g is not None:
                        eng.wait_ge(sg.rooted.sem, sg.rooted.after(g))
                        v.reciprocal(self.rs[:, g.pair, :], self.sd[:, g.pair, :]).then_inc(sg.inverted.sem, 1)
                        eng.wait_ge(sg.inverted.sem, sg.inverted.after(g))
                        r = over4(self.rs[:, g.pair, :])
                        if k < 6:
                            if k in (0, 1):
                                if g.from_(2):
                                    eng.wait_ge(sg.turned.sem, sg.turned.after(g, 2))
                                to = self.hb[:, g.pair]
                            else:
                                if g.from_(UNROLL):
                                    eng.wait_ge(sg.stored.sems[g.slot], sg.stored.after(g, self.stores, 1))
                                to = self.hout[:, g.slot]
                            v.scalar_tensor_tensor(out=to, in0=self.xc[:, g.pair], scalar=0.0, in1=r, op0=ALU.max,
                                                   op1=ALU.mult).then_inc(sg.normed.sem, 1)
                        else:
                            c, f = self.xc[:, g.pair], self.fb[:, g.slot]
                            v.tensor_tensor(c, c, r, ALU.mult).then_inc(sg.normed.sem, 1)
                            eng.wait_ge(sg.normed.sem, sg.normed.after(g))
                            v.tensor_tensor(c, c, row("L3_gnn_ln_scale"), ALU.mult).then_inc(sg.scaled.sem, 1)
                            eng.wait_ge(sg.scaled.sem, sg.scaled.after(g))
                            v.tensor_tensor(c, c, row("L3_gnn_ln_offset"), ALU.add).then_inc(sg.offset.sem, 1)
                            eng.wait_ge(sg.offset.sem, sg.offset.after(g))
                            eng.wait_ge(sg.with_h.sem, sg.with_h.after(g))
                            if g.from_(UNROLL):
                                eng.wait_ge(sg.stored.sems[g.slot], sg.stored.after(g, self.stores, 1))
                            v.tensor_tensor(f, c, feats(g), ALU.add).then_inc(sg.final.sem, 1)
                    g = t.at(self.norm) if self.late else None
                    if g is not None:
                        if k == 5:
                            eng.wait_ge(sg.x_new.sem, sg.x_new.after(g))
                            v.tensor_tensor(feats(g), feats(g), row("L2_gnn_b"), ALU.add).then_inc(sg.biased.sem, 1)
                            eng.wait_ge(sg.biased.sem, sg.biased.after(g))
                            centre(g, feats(g))
                        else:
                            eng.wait_ge(sg.x_new.sem, sg.x_new.after(g))
                            centre(g, self.yb[:, g.pair])
                    g = t.at(self.turn + 1) if k == 2 else None
                    if g is not None:
                        eng.wait_ge(sg.turned_sb.sem, sg.turned_sb.after(g))
                        gate(eng, "dve")
                        last = GR if not (g.known and g.g == GROUPS - 1) else N_TRUE - (GROUPS - 1) * GR
                        v.bn_stats(stats[:, bass.ds(g.g, 1), :].rearrange("p o s -> p (o s)"), self.yout[:, g.slot, 0:last]
                                   ).then_inc(sg.stat.sem, 1)
                    g = t.at(self.mix) if k != 6 else None
                    if g is not None:
                        if self.windowed:
                            eng.wait_ge(sg.agged.sem, sg.agged.after(g))
                            agg = self.bank(self.agg, g)[:]
                        elif self.gathered:
                            eng.wait_ge(sg.fetched.sems[g.slot], sg.fetched.after(g, GT))
                            agg = self.aggs[:, g.slot, :, 0:D]
                        if k == 0:
                            eng.wait_ge(sg.landed.sems[g.slot], sg.landed.after(g, self.loads))
                            centre(g, feats(g))
                        elif k == 1:
                            v.tensor_tensor(feats(g), feats(g), agg, ALU.add).then_inc(sg.mixed.sem, 1)
                            eng.wait_ge(sg.mixed.sem, sg.mixed.after(g))
                            centre(g, feats(g))
                        elif k in (2, 4):
                            eng.wait_ge(sg.owned.sems[g.slot], sg.owned.after(g, 1))
                            if k == 2:
                                if g.from_(2):
                                    eng.wait_ge(sg.turned.sem, sg.turned.after(g, 2))
                            v.tensor_tensor(self.mixb[:, g.pair], self.ownb[:, g.slot], agg, ALU.add).then_inc(sg.joined.sem, 1)
                            eng.wait_ge(sg.joined.sem, sg.joined.after(g))
                            v.tensor_tensor(self.mixb[:, g.pair], self.mixb[:, g.pair], here(dinv, g), ALU.mult).then_inc(sg.mixed.sem, 1)
                            if k == 4:
                                eng.wait_ge(sg.mixed.sem, sg.mixed.after(g))
                                v.tensor_tensor(self.mixb[:, g.pair], self.mixb[:, g.pair], row("L1_gnn_b2"), ALU.add).then_inc(sg.biased.sem, 1)
                                eng.wait_ge(sg.biased.sem, sg.biased.after(g))
                                v.tensor_tensor(feats(g), feats(g), self.mixb[:, g.pair], ALU.add).then_inc(sg.x_new.sem, 1)
                                eng.wait_ge(sg.x_new.sem, sg.x_new.after(g))
                                centre(g, feats(g))
                        elif k == 5:
                            if g.from_(UNROLL):
                                eng.wait_ge(sg.turned.sem, sg.turned.after(g, UNROLL))
                            v.tensor_tensor(self.hn[:, g.slot, :, D:P], agg, here(invdeg, g), ALU.mult).then_inc(sg.mixed.sem, 1)
                        elif k == 3:
                            eng.wait_ge(sg.affined.sem, sg.affined.after(g))
                            if g.from_(2):
                                eng.wait_ge(sg.multiplied.sem, sg.multiplied.after(g, 2))
                            v.scalar_tensor_tensor(out=self.zs[:, g.pair, :], in0=self.zb[:, g.pair, :], scalar=SLOPE,
                                                   in1=self.zb[:, g.pair, :], op0=ALU.mult, op1=ALU.max).then_inc(sg.shifted.sem, 1)
                return step, max(self.evac or 0, self.scale if self.norms or k == 6 else 0, self.turn + 1 if k == 2 else 0)

        class EdgePass:

            def __init__(self, kind, general, sg, qin, banks):
                self.kind, self.general, self.sg, self.qin, self.banks = kind, general, sg, qin, banks
                self.stores = 1
                self.scans = kind == "max" or general
                self.spread = kind in ("max", "mlp") and not general
                self.both = kind in ("max", "mlp") and general
                self.gathers = GT * (2 if self.both else 1)
                self.loads = 1 + (5 if self.spread else 0) + self.both + self.scans + (kind == "mlp")
                self.store = {"sum": 2, "max": 3, "mlp": 4}[kind] + 1 if self.scans else 4 if kind == "mlp" else 1

            def bank(self, tensors, g):
                return tensors[g.pair % len(tensors)]

            def buffers(self, tmp, ps):
                k = self.kind
                self.W = P if k == "mlp" else D
                self.sidx = tmp("sidx", [P, UNROLL, GT], I32)
                self.rowsb = tmp("rowsb", [P, UNROLL, GT, self.W])
                if self.both:
                    self.tidx = tmp("tidx", [P, UNROLL, GT], I32)
                    self.trows = tmp("trows", [P, UNROLL, GT, D])
                if self.spread:
                    self.win = tmp("twin", [WP, UNROLL, GT, WK, D])
                    self.relb = tmp("relb", [WP, UNROLL, GR], F16)
                    self.hot = tmp("ehot", [WP, 2, WK, GR])
                if k != "sum" or self.scans:
                    self.s_ps = [ps(f"s_ps{b}", [self.W, GR]) for b in range(self.banks["s"])]
                    self.h_sb = tmp("h_sb", [self.W, 2, GR])
                if k == "mlp":
                    self.t_ps = ps("t_ps", [D, GR])
                    self.t_sb = tmp("t_sb", [D, 2, GR])
                    self.hid_ps = ps("hid_ps", [HID, GR])
                    self.hid = tmp("hid", [HID, 2, GR])
                if self.scans:
                    self.mask = tmp("mask", [D, UNROLL, GR])
                    self.sc = tmp("scan", [D, 2, GR])
                    if k != "sum":
                        self.m_ps = ps("m_ps", [D, GR])
                        self.m_sb = tmp("m_sb", [D, 2, GR])
                if self.scans or k == "mlp":
                    self.o_ps = [ps(f"o_ps{b}", [P, GT, D]) for b in range(self.banks["o"])]
                    self.outb = tmp("eoutb", [P, UNROLL, GT, D])
                else:
                    self.outb = self.rowsb

            def sp(self, eng):
                sg, k = self.sg, self.kind

                def step(t):
                    g = t.at(0)
                    if g is not None:
                        land = sg.landed.sems[g.slot]
                        if g.from_(UNROLL):
                            if g.from_(UNROLL):
                                eng.wait_ge(sg.fetched.sems[g.slot], sg.fetched.after(g, self.gathers, 1))
                            gate(eng, "sp")
                        eng.dma_start(self.sidx[:, g.slot, :], a["src"].rearrange("(g p j) -> g p j", p=P, j=GT)[bass.ds(g.g, 1)].rearrange("o p j -> (o p) j")).then_inc(land, 16)
                        if self.both:
                            eng.dma_start(self.tidx[:, g.slot, :], a["dst"][1:1 + N].rearrange("(g p j) -> g p j", p=P, j=GT)[bass.ds(g.g, 1)].rearrange("o p j -> (o p) j")).then_inc(land, 16)
                        if k == "mlp":
                            if g.from_(UNROLL):
                                eng.wait_ge(sg.summed_e.sem, sg.summed_e.after(g, UNROLL))
                            gate(eng, "sp")
                            eng.dma_start(self.rowsb[:, g.slot, :, D:P], edgerows(a["edge_attr_64"], g.g)).then_inc(land, 16)
                        if self.scans:
                            if g.from_(UNROLL):
                                eng.wait_ge(sg.scanned.sem, sg.scanned.after(g, UNROLL))
                            gate(eng, "sp")
                            eng.dma_start(self.mask[:, g.slot, :], edgecols(farrow if k == "max" else keeprow, g.g, D)).then_inc(land, 16)
                        if self.spread:
                            if g.from_(UNROLL):
                                eng.wait_ge(sg.rel_hot.sem, sg.rel_hot.after(g, UNROLL))
                            gate(eng, "sp")
                            eng.dma_start(self.relb[:, g.slot, :], edgecols(relrow, g.g, WP)).then_inc(land, 16)
                            if g.from_(UNROLL):
                                eng.wait_ge(sg.summed_e.sem, sg.summed_e.after(g, UNROLL))
                            gate(eng, "sp")
                            for j, s in enumerate(window_starts(eng, firsts, g.g)):
                                eng.dma_start(self.win[:, g.slot, j, :, :], (tabP if k == "max" else self.qin)[bass.ds(s, WIN), :].rearrange(
                                    "(p k) f -> p k f", k=WK)).then_inc(land, 16)
                return step, 0

            def pool(self, eng):
                sg, k = self.sg, self.kind
                srctab = self.qin
                tgttab = tabP if k == "max" else self.qin

                def step(t):
                    g = t.at(0)
                    if g is None:
                        return
                    eng.wait_ge(sg.landed.sems[g.slot], sg.landed.after(g, self.loads))
                    if self.outb is self.rowsb:
                        if g.from_(UNROLL):
                            eng.wait_ge(sg.stored.sems[g.slot], sg.stored.after(g, 1, 1))
                    else:
                        if g.from_(UNROLL):
                            eng.wait_ge(sg.summed_e.sem, sg.summed_e.after(g, UNROLL))
                    gate(eng, "pool")
                    for j in range(GT):
                        nc.gpsimd.indirect_dma_start(self.rowsb[:, g.slot, j, 0:D], None, srctab,
                                                     bass.IndirectOffsetOnAxis(ap=self.sidx[:, g.slot, j:j + 1], axis=0)
                                                     ).then_inc(sg.fetched.sems[g.slot], 16)
                        if self.both:
                            nc.gpsimd.indirect_dma_start(self.trows[:, g.slot, j, :], None, tgttab,
                                                         bass.IndirectOffsetOnAxis(ap=self.tidx[:, g.slot, j:j + 1], axis=0)
                                                         ).then_inc(sg.fetched.sems[g.slot], 16)
                return step, 0

            def targets(self, g, to):
                if self.spread:
                    for j in range(GT):
                        for w in range(WK):
                            mm = nc.tensor.matmul(to[:, bass.ts(j, P)], self.win[:, g.slot, j, w, :], self.hot[:, g.pair, w, bass.ts(j, P)],
                                                  start=j == 0 and w == 0, stop=w == WK - 1, skip_group_check=True)
                else:
                    for j in range(GT):
                        mm = nc.tensor.matmul(to[:, j::GT], self.trows[:, g.slot, j, :], ident, start=j == 0, stop=True,
                                              skip_group_check=True)
                return mm

            def pe(self, eng):
                sg, k = self.sg, self.kind
                if k == "sum" and not self.scans:
                    return None

                def step(t):
                    g = t.at({"sum": 2, "max": 3, "mlp": 4}[k]) if self.scans else None
                    if g is not None:
                        eng.wait_ge(sg.scanned.sem, sg.scanned.after(g))
                        if g.from_(self.banks["o"]):
                            eng.wait_ge(sg.out_ready.sem, sg.out_ready.after(g, self.banks["o"]))
                        gate(eng, "pe")
                        for j in range(GT):
                            mm = nc.tensor.transpose(self.bank(self.o_ps, g)[:, j, :], self.sc[:, g.pair, j::GT], ident[0:D, 0:D])
                        mm.then_inc(sg.turned_e.sem, 1)
                    if k != "sum":
                        g = t.at(2 if k == "mlp" else 1)
                        if g is not None:
                            hid_ready = sg.hid_sb if k == "mlp" else sg.hidden_e
                            hid, w = (self.hid, wm2) if k == "mlp" else (self.h_sb, w2)
                            eng.wait_ge(hid_ready.sem, hid_ready.after(g))
                            if self.scans:
                                if g.from_(1):
                                    eng.wait_ge(sg.msg_sb.sem, sg.msg_sb.after(g, 1))
                                gate(eng, "pe")
                                nc.tensor.matmul(self.m_ps[:], w, hid[:, g.pair, :], start=True, stop=True).then_inc(sg.msg.sem, 1)
                            else:
                                if g.from_(self.banks["o"]):
                                    eng.wait_ge(sg.out_ready.sem, sg.out_ready.after(g, self.banks["o"]))
                                gate(eng, "pe")
                                nc.tensor.matmul(self.bank(self.o_ps, g)[:].rearrange("p j f -> p (j f)"), ones1, b2row.rearrange("o j f -> o (j f)"),
                                                 start=True, stop=False, skip_group_check=True)
                                for j in range(GT):
                                    mm = nc.tensor.matmul(self.bank(self.o_ps, g)[:, j, :], hid[:, g.pair, j::GT], w, start=False, stop=True,
                                                          skip_group_check=True)
                                mm.then_inc(sg.msg.sem, 1)
                        g = t.at(1)
                        if g is not None and k == "mlp":
                            eng.wait_ge(sg.hidden_e.sem, sg.hidden_e.after(g))
                            eng.wait_ge(sg.tgt_sb.sem, sg.tgt_sb.after(g))
                            if g.from_(1):
                                eng.wait_ge(sg.hid_sb.sem, sg.hid_sb.after(g, 1))
                            gate(eng, "pe")
                            nc.tensor.matmul(self.hid_ps[:], wmse, self.h_sb[:, g.pair, :], start=True, stop=False)
                            nc.tensor.matmul(self.hid_ps[:], wmt, self.t_sb[:, g.pair, :], start=False, stop=True
                                             ).then_inc(sg.hid_sum.sem, 1)
                    g = t.at(0)
                    if g is not None:
                        eng.wait_ge(sg.fetched.sems[g.slot], sg.fetched.after(g, self.gathers))
                        eng.wait_ge(sg.landed.sems[g.slot], sg.landed.after(g, self.loads))
                        if self.spread:
                            eng.wait_ge(sg.rel_hot.sem, sg.rel_hot.after(g))
                        if g.from_(self.banks["s"]):
                            eng.wait_ge(sg.hidden_e.sem, sg.hidden_e.after(g, self.banks["s"]))
                        if k == "mlp":
                            if g.from_(1):
                                eng.wait_ge(sg.tgt_sb.sem, sg.tgt_sb.after(g, 1))
                        gate(eng, "pe")
                        if k == "max":
                            self.targets(g, self.bank(self.s_ps, g))
                            for j in range(GT):
                                mm = nc.tensor.matmul(self.bank(self.s_ps, g)[:, j::GT], self.rowsb[:, g.slot, j, :], ident,
                                                      start=False, stop=True, skip_group_check=True)
                        else:
                            if k == "mlp":
                                self.targets(g, self.t_ps)
                            for j in range(GT):
                                mm = nc.tensor.transpose(self.bank(self.s_ps, g)[:, j::GT], self.rowsb[:, g.slot, j, :], ident)
                        mm.then_inc(sg.summed_e.sem, 1)
                return step, {"sum": 2, "max": 3, "mlp": 4}[k]

            def act(self, eng):
                sg, k = self.sg, self.kind

                def results(t):
                    g = t.at({"sum": 2, "max": 3, "mlp": 4}[k]) if self.scans else None
                    if g is not None:
                        eng.wait_ge(sg.turned_e.sem, sg.turned_e.after(g))
                        if g.from_(UNROLL):
                            eng.wait_ge(sg.stored.sems[g.slot], sg.stored.after(g, 1, 1))
                        nc.scalar.copy(self.outb[:, g.slot], self.bank(self.o_ps, g)[:]).then_inc(sg.out_ready.sem, 1)
                    g = t.at(2 if k == "mlp" else 1) if self.scans and k != "sum" else None
                    if g is not None:
                        eng.wait_ge(sg.msg.sem, sg.msg.after(g))
                        if g.from_(2):
                            eng.wait_ge(sg.scanned.sem, sg.scanned.after(g, 2))
                        nc.scalar.activation(self.m_sb[:, g.pair, :], self.m_ps[:], ACT.Relu if k == "mlp" else ACT.Identity,
                                             bias=col("L3_gnn_msg_b2" if k == "mlp" else "L0_gnn_b2")).then_inc(sg.msg_sb.sem, 1)
                    g = t.at(1) if k == "mlp" else None
                    if g is not None:
                        eng.wait_ge(sg.hid_sum.sem, sg.hid_sum.after(g))
                        if g.from_(2):
                            eng.wait_ge(sg.msg.sem, sg.msg.after(g, 2))
                        nc.scalar.activation(self.hid[:, g.pair, :], self.hid_ps[:], ACT.Relu,
                                             bias=col("L3_gnn_msg_b1", HID)).then_inc(sg.hid_sb.sem, 1)

                def copies(t):
                    g = t.at(0) if k != "sum" or self.scans else None
                    if g is not None:
                        eng.wait_ge(sg.summed_e.sem, sg.summed_e.after(g))
                        h = self.h_sb[:, g.pair, :]
                        if k == "max":
                            if g.from_(2):
                                eng.wait_ge(sg.msg.sem, sg.msg.after(g, 2))
                            nc.scalar.activation(h, self.bank(self.s_ps, g)[:], ACT.Relu, bias=col("L0_gnn_b1")).then_inc(sg.hidden_e.sem, 1)
                        elif k == "sum":
                            if g.from_(2):
                                eng.wait_ge(sg.scanned.sem, sg.scanned.after(g, 2))
                            nc.scalar.copy(h, self.bank(self.s_ps, g)[:]).then_inc(sg.hidden_e.sem, 1)
                        else:
                            if g.from_(2):
                                eng.wait_ge(sg.hid_sum.sem, sg.hid_sum.after(g, 2))
                            nc.scalar.copy(self.t_sb[:, g.pair, :], self.t_ps[:]).then_inc(sg.tgt_sb.sem, 1)
                            nc.scalar.copy(h, self.bank(self.s_ps, g)[:]).then_inc(sg.hidden_e.sem, 1)

                def store(t):
                    g = t.at(self.store)
                    if g is not None:
                        if self.outb is self.rowsb:
                            eng.wait_ge(sg.fetched.sems[g.slot], sg.fetched.after(g, self.gathers))
                        else:
                            eng.wait_ge(sg.out_ready.sem, sg.out_ready.after(g))
                        eng.dma_start(edgerows(msgs[0:N, :], g.g)[:, :, 0:D], self.outb[:, g.slot]).then_inc(sg.stored.sems[g.slot], 16)
                return [(results, self.store), (copies, self.store), (store, self.store)]

            def dve(self, eng):
                sg, k, v = self.sg, self.kind, nc.vector
                if k == "sum" and not self.scans:
                    return None

                def step(t):
                    g = t.at(3) if not self.scans else None
                    if g is not None:
                        eng.wait_ge(sg.msg.sem, sg.msg.after(g))
                        if g.from_(UNROLL):
                            eng.wait_ge(sg.stored.sems[g.slot], sg.stored.after(g, 1, 1))
                        v.tensor_scalar(self.outb[:, g.slot], self.bank(self.o_ps, g)[:], 0.0, None, ALU.max).then_inc(sg.out_ready.sem, 1)
                    g = t.at(0) if self.spread else None
                    if g is not None:
                        eng.wait_ge(sg.landed.sems[g.slot], sg.landed.after(g, self.loads))
                        if g.from_(2):
                            eng.wait_ge(sg.summed_e.sem, sg.summed_e.after(g, 2))
                        for w in range(WK):
                            mm = v.tensor_scalar(self.hot[:, g.pair, w, :], self.relb[:, g.slot, :], pcol[0:WP, w:w + 1], None, ALU.is_equal)
                        mm.then_inc(sg.rel_hot.sem, 1)
                    g = t.at({"sum": 1, "max": 2, "mlp": 3}[k]) if self.scans else None
                    if g is not None:
                        of = sg.hidden_e if k == "sum" else sg.msg_sb
                        eng.wait_ge(of.sem, of.after(g))
                        if g.from_(1):
                            eng.wait_ge(sg.scanned.sem, sg.scanned.after(g, 1))
                        if g.from_(2):
                            eng.wait_ge(sg.turned_e.sem, sg.turned_e.after(g, 2))
                        if not g.known or g.g > 0:
                            initial = self.sc[:, 1 - g.pair, GR - 1:GR]
                        else:
                            initial = 0.0
                        data = (self.h_sb if k == "sum" else self.m_sb)[:, g.pair, :]
                        ops = (ALU.add, ALU.max) if k == "max" else (ALU.mult, ALU.add)
                        v.tensor_tensor_scan(self.sc[:, g.pair, :], self.mask[:, g.slot, :], data, initial, *ops).then_inc(sg.scanned.sem, 1)
                return step, {"sum": 1, "max": 2, "mlp": 3}[k] if self.scans else 3

        def run(number, fast, general):
            used = {"fast": [fast], "general": [general], "both": [fast, general]}[mode]
            for n, passes in enumerate(used):
                with ExitStack() as memory:
                    for p, _ in passes:
                        p.buffers(lambda name, shape, dt=F32: memory.enter_context(nc.sbuf_tensor(f"r{number}_{n}_{name}", shape, dt))[:],
                                  lambda name, shape: memory.enter_context(nc.psum_tensor(f"r{number}_{n}_{name}", shape, F32)))

            def program(passes, of):
                if not passes:
                    return None

                def emit(eng):
                    parts = [(of(p, eng), lag) for p, lag in passes]
                    parts = [(part, lag) for part, lag in parts if part]
                    if parts and isinstance(parts[0][0], list):
                        parts = [(stages[k], lag) for k in range(3) for stages, lag in parts]
                    if not parts:
                        return

                    def step(t):
                        for (one, _), lag in parts:
                            one(t.later(lag))
                    steps(eng, step, max(own + lag for (_, own), lag in parts))
                return emit

            def stored(passes):
                go = program(passes[::-1], lambda p, e: p.act(e))
                if go is None:
                    return None

                def emit(eng):
                    go(eng)
                    for p, _ in passes:
                        p.sg.stored.wait_all(eng, p.stores, GROUPS)
                return emit

            def both(build_one):
                return build_one(fast), build_one(general)

            if not any(used):
                return
            with nc.Block() as block:
                @block.sync
                def _(sp):
                    either(sp, *both(lambda ps: program(ps, lambda p, e: p.sp(e))))

                @block.gpsimd
                def _(pool):
                    either(pool, *both(lambda ps: program(ps, lambda p, e: p.pool(e))))

                @block.tensor
                def _(pe):
                    either(pe, *both(lambda ps: program(ps[::-1], lambda p, e: p.pe(e))))

                @block.scalar
                def _(act):
                    either(act, *both(stored))

                @block.vector
                def _(dve):
                    either(dve, *both(lambda ps: program(ps, lambda p, e: p.dve(e))))
            for passes in used:
                for p, _ in passes:
                    p.sg.close(p.loads, p.gathers, p.stores)
                    if isinstance(p, NodePass) and p.own:
                        p.sg.close_own()

        def layer(number, edge_kind, node_kind, qin, qout):
            tight = {"agg": 1, "tp": 1, "mp": 1, "s": 1, "o": 1} if edge_kind == "mlp" else \
                {"agg": 2, "tp": 1, "mp": 1, "s": 2, "o": 1} if edge_kind == "max" else WIDE
            fe = fn = ge = gn = None
            if mode != "general":
                fe = EdgePass(edge_kind, False, signals["fast_e"], qin, tight)
                fn = NodePass(node_kind, False, signals["fast_n"], qin, qout, tight, source=fe)
            if mode != "fast":
                ge = EdgePass(edge_kind, True, signals["general_e"], qin, WIDE if edge_kind != "mlp" else dict(WIDE, o=2))
                gn = NodePass(node_kind, True, signals["general_n"], qin, qout, WIDE)
            run(number, [(fe, 0), (fn, AHEAD + fe.store + SLACK)] if fe else [], [(ge, 0)] if ge else [])
            run(number + 1, [], [(gn, 0)] if gn else [])

        def nodes_only(number, kind, qout):
            on = {path: [(NodePass(kind, path == "general", signals[path + "_n"], None, qout, WIDE), 0)]
                  for path in ("fast", "general") if mode in (path, "both")}
            run(number, on.get("fast", []), on.get("general", []))

        def batch_norm():
            with nc.semaphore("bn_chain") as chain, nc.semaphore("bn_rooted") as rooted, nc.Block() as block:
                @block.vector
                def _(dve):
                    n = [0]

                    def link(ins):
                        n[0] += 1
                        ins.then_inc(chain, 1)
                        dve.wait_ge(chain, n[0])
                    v = nc.vector
                    link(v.bn_aggr(bn[:, 0:2], stats.rearrange("p g s -> p (g s)")))
                    dve.wait_ge(rooted, 1)
                    link(v.reciprocal(bn[:, 3:4], bn[:, 2:3]))
                    link(v.tensor_tensor(bn[:, 4:5], bn[:, 3:4], col("L1_gnn_gamma"), ALU.mult))
                    link(v.tensor_tensor(bn[:, 6:7], bn[:, 4:5], bn[:, 0:1], ALU.mult))
                    link(v.tensor_tensor(bn[:, 5:6], col("L1_gnn_beta"), bn[:, 6:7], ALU.subtract))

                @block.scalar
                def _(act):
                    act.wait_ge(chain, 1)
                    nc.scalar.activation(bn[:, 2:3], bn[:, 1:2], ACT.Sqrt, bias=epsc[0:D, :]).then_inc(rooted, 1)

        SLACK = 4
        WIDE = {"agg": 2, "tp": 2, "mp": 2, "s": 2, "o": 2}
        signals = {}
        for path in ("fast", "general"):
            if mode in (path, "both"):
                signals[path + "_e"], signals[path + "_n"] = EdgeSignals(path + "_e"), NodeSignals(path + "_n")
        setup()
        nodes_only(1, 0, tabQ[0])
        layer(2, "max", 1, tabQ[0], tabQ[1])
        layer(4, "sum", 2, tabQ[1], None)
        batch_norm()
        nodes_only(6, 3, tabQ[0])
        layer(7, "sum", 4, tabQ[0], tabQ[1])
        layer(9, "sum", 5, tabQ[1], tabQ[0])
        layer(11, "mlp", 6, tabQ[0], None)


MODE = "both"
NAMES = ["L0_gnn_W1", "L0_gnn_b1", "L0_gnn_W2", "L0_gnn_b2", "L1_gnn_W1", "L1_gnn_b1", "L1_gnn_gamma",
         "L1_gnn_beta", "L1_gnn_W2", "L1_gnn_b2", "L2_gnn_W", "L2_gnn_b", "L3_gnn_msg_W1", "L3_gnn_msg_b1",
         "L3_gnn_msg_W2", "L3_gnn_msg_b2", "L3_gnn_node_W1", "L3_gnn_node_b1", "L3_gnn_node_W2",
         "L3_gnn_node_b2", "L3_gnn_ln_scale", "L3_gnn_ln_offset"]


def kernel(**inputs):
    import numpy as _np
    import concourse.bacc as _bacc
    from concourse import mybir as _mybir
    from concourse.bass_utils import run_bass_kernel_spmd as _run

    nc = _bacc.Bacc("TRN2", target_bir_lowering=False, num_devices=1)
    arrays = {n: _np.ascontiguousarray(inputs[n]) for n in NAMES}
    more = N - N_TRUE
    for n in ("x", "edge_attr_64"):
        arrays[n] = _np.concatenate([_np.asarray(inputs[n]), _np.zeros((more, D), _np.float32)])
    arrays["src"] = _np.concatenate([_np.asarray(inputs["src"]), _np.zeros((more,), _np.int32)])
    arrays["dst"] = _np.concatenate([_np.full((1,), -1, _np.int32), _np.asarray(inputs["dst"]),
                                     _np.arange(N_TRUE, N + 1, dtype=_np.int32)])
    aps = {n: nc.dram_tensor(f"in_{n}", v.shape, _mybir.dt.from_np(v.dtype), kind="ExternalInput").ap()
           for n, v in arrays.items()}
    out = nc.dram_tensor("out", (N, D), F32, kind="ExternalOutput").ap()
    build(nc, MODE, aps, out)
    r = _run(nc, [{f"in_{n}": v for n, v in arrays.items()}], core_ids=[0])
    return r.results[0]["out"][:N_TRUE]
```

```python
from contextlib import ExitStack

import concourse.bass as bass
from concourse import mybir

F32 = mybir.dt.float32
F16 = mybir.dt.float16
I32 = mybir.dt.int32
ALU = mybir.AluOpType
ACT = mybir.ActivationFunctionType
AX_X = mybir.AxisListType.X
RMAX = bass.bass_isa.ReduceOp.max

P = 128
D = 64
HID = 128
N_TRUE = 50000
TILES = 392
GT = 4
GROUPS = TILES // GT
GR = GT * P
N = TILES * P
WP, WK = 96, 2
WIN = WP * WK
MW = D + 2
UNROLL = 4
AHEAD = 3
LEAD = 2
EPS = 1e-5
SLOPE = 0.01
FAR = -3.0e38


class Turn:

    def __init__(self, i, part, n):
        self.i, self.part, self.n, self.begun = i, part, n, 0
        self.known = isinstance(i, int)

    def later(self, steps):
        t = Turn(self.i, self.part, self.n)
        t.begun = self.begun + steps
        return t

    def at(self, lag):
        lag = lag + self.begun
        slot = (self.part - lag) % UNROLL
        turn = self.i + (self.part - lag - slot) // UNROLL
        g = self.i * UNROLL + (self.part - lag)
        if self.known and not 0 <= g < self.n:
            return None
        return Group(g, turn, slot, self.known)


class Group:

    def __init__(self, g, turn, slot, known):
        self.g, self.turn, self.slot, self.pair, self.known = g, turn, slot, slot % 2, known

    def from_(self, k):
        return not self.known or self.g >= k


class Tally:

    def __init__(self, sem):
        self.sem, self.base, self.used = sem, 0, False

    def after(self, t, back=0):
        self.used = True
        return t.g + (1 - back + self.base)


class Landing:

    def __init__(self, sems):
        self.sems, self.base = sems, [0] * len(sems)

    def after(self, t, dmas, back=0):
        return t.turn * (16 * dmas) + ((1 - back) * 16 * dmas + self.base[t.slot])

    def held(self, slot, n):
        return (n - slot + UNROLL - 1) // UNROLL

    def wait_all(self, eng, dmas, n):
        for s in range(UNROLL):
            eng.wait_ge(self.sems[s], self.held(s, n) * 16 * dmas + self.base[s])

    def close(self, dmas, n):
        for s in range(len(self.sems)):
            self.base[s] += self.held(s, n) * 16 * dmas


def steps(eng, step, lag, n=GROUPS):
    head = -(-(lag + UNROLL) // UNROLL)
    loop = n // UNROLL
    for s in range(head * UNROLL):
        step(Turn(s // UNROLL, s % UNROLL, n))
    with eng.Fori(head, loop) as i:
        for part in range(UNROLL):
            step(Turn(i, part, n))
    for s in range(loop * UNROLL, n + lag):
        step(Turn(s // UNROLL, s % UNROLL, n))


def build(nc, mode, a, out):
    with ExitStack() as ctx:
        def sb(name, shape, dt=F32):
            return ctx.enter_context(nc.sbuf_tensor(name, shape, dt))[:]

        def sem(name):
            return ctx.enter_context(nc.semaphore(name))

        def dram(name, shape, dt=F32):
            return nc.dram_tensor(name, shape, dt).ap()

        tabP = dram("tabP", (N, D))
        tabQ = [dram(f"tabQ{k}", (N, D)) for k in range(2)]
        msgs = dram("msgs", (N + P, MW))
        yT = dram("yT", (D, N))
        relrow = dram("relrow", (N,), F16)
        farrow = dram("farrow", (N,))
        keeprow = dram("keeprow", (N,))
        firstnode = dram("firstnode", (TILES,), I32)
        fetchidx = dram("fetchidx", (GROUPS, P, GT), I32)

        xs = sb("xs", [P, TILES, D])
        deg = sb("deg", [P, TILES])
        dinv = sb("dinv", [P, TILES])
        invdeg = sb("invdeg", [P, TILES])
        blockf = sb("blockf", [P, TILES])
        starts = sb("starts", [1, TILES], I32)
        firsts = sb("firsts", [1, TILES], I32)
        srcs = sb("srcs", [P, TILES], I32)
        flag = sb("flag", [1, 1], I32)
        ident = sb("ident", [P, P])
        iota = sb("iota", [P, P])
        pcol = sb("pcol", [P, WK])
        stats = sb("stats", [D, GROUPS, 6])
        bn = sb("bn", [D, 8])
        epsc = sb("epsc", [P, 1])

        w1raw = sb("w1raw", [D, 2, D])
        w1 = sb("w1", [D, 2, D])
        w2 = sb("w2", [D, D])
        wg1 = sb("wg1", [D, D])
        wg2 = sb("wg2", [D, D])
        wl2 = sb("wl2", [P, D])
        wl2sum = sb("wl2sum", [D, D])
        wmse = sb("wmse", [P, HID])
        wmt = sb("wmt", [D, HID])
        wm2 = sb("wm2", [HID, D])
        wn1 = sb("wn1", [P, HID])
        wn2 = sb("wn2", [HID, D])
        COLS = ["L0_gnn_b1", "L0_gnn_b2", "L1_gnn_b1", "L1_gnn_gamma", "L1_gnn_beta", "L3_gnn_msg_b1",
                "L3_gnn_msg_b2", "L3_gnn_node_b1"]
        ROWS = ["L1_gnn_b2", "L2_gnn_b", "L3_gnn_msg_b2", "L3_gnn_node_b2", "L3_gnn_ln_scale", "L3_gnn_ln_offset"]
        cols = sb("cols", [P, len(COLS)])
        rows = sb("rows", [P, len(ROWS), D])

        def col(name, k=D):
            return cols[0:k, COLS.index(name):COLS.index(name) + 1]

        def row(name):
            return rows[:, ROWS.index(name):ROWS.index(name) + 1, :].to_broadcast([P, GT, D])

        passed = {e: sem(f"passed_{e}") for e in ("pe", "pool", "dve", "sp", "act")}

        bn_chain, bn_rooted = sem("bn_chain"), sem("bn_rooted")

        def gate(eng, name):
            eng.sem_inc(passed[name], 1)

        def over4(v):
            return v.unsqueeze(2).to_broadcast([P, GT, D])

        def window_starts(eng, table, g):
            _, values = nc.values_load_multi_w_load_instructions(
                table[0:1, bass.ds(g * GT, GT)], engines=(eng.engine,), min_val=0, max_val=N - WIN,
                skip_runtime_bounds_check_because="VectorE limits every start to N - WIN, and none is negative")
            return values

        def setup(first):
            with ExitStack() as inner:
                def tmp(name, shape, dt=F32):
                    return inner.enter_context(nc.sbuf_tensor(name, shape, dt))[:]

                def sig(name):
                    return inner.enter_context(nc.semaphore(name))

                E98 = GROUPS
                cur, nxt, prv = (tmp(n, [E98, GR], I32) for n in ("cur", "nxt", "prv"))
                last, lastt, far, keep, rel = (tmp(n, [E98, GR]) for n in ("last", "lastt", "far", "keep", "rel"))
                tgts = tmp("tgts", [E98, GR, MW - D])
                relh = tmp("relh", [E98, GR], F16)
                first4 = tmp("first4", [E98, GT])
                first4i = tmp("first4i", [E98, GT], I32)
                relmax = tmp("relmax", [P, 1])
                relall = tmp("relall", [P, 1])
                dsti, loi, hii = (tmp(n, [P, TILES], I32) for n in ("dsti", "loi", "hii"))
                lo, hi = (tmp(n, [P, TILES]) for n in ("lo", "hi"))
                ioti = tmp("ioti", [P, TILES], I32)
                ioth = tmp("ioth", [P, TILES], F16)
                hotlo = tmp("hotlo", [P, UNROLL, P], F16)
                hothi = tmp("hothi", [P, UNROLL, TILES], F16)
                ones = tmp("ones", [P, P])
                below = tmp("below", [P, P])
                degp = tmp("degp", [P, TILES])
                tot, incl, excl, st, has = (tmp(n, [P, TILES]) for n in ("tot", "incl", "excl", "st", "has"))
                idxf = tmp("idxf", [P, TILES])
                idxi = tmp("idxi", [P, TILES], I32)
                sc = tmp("sc", [1, TILES])
                over = tmp("over", [1, 8])
                blocki = tmp("blocki", [P, TILES], I32)
                pcoli = tmp("pcoli", [P, WK], I32)
                zero = tmp("zero", [P, MW])
                hist = inner.enter_context(nc.psum_tensor("hist", [P, TILES], F32))
                prefix = inner.enter_context(nc.psum_tensor("prefix", [P, TILES], F32))
                totals = inner.enter_context(nc.psum_tensor("totals", [P, TILES], F32))

                weights_in, edges_in, dst_in = sig("weights_in"), sig("edges_in"), sig("dst_in")
                rows_out, first_out, first_in = sig("rows_out"), sig("first_out"), sig("first_in")
                made = sig("made")
                chain = sig("chain")
                hot, hot_used = Tally(sig("hot")), Tally(sig("hot_used"))
                sums = sig("sums")
                rooted = sig("rooted")
                idx_ready = sig("idx_ready")
                rel_ready, relall_ready = sig("rel_ready"), sig("relall_ready")
                rows_ready, firsts_ready = sig("rows_ready"), sig("firsts_ready")
                deg_ready = sig("deg_ready")
                zero_ready = sig("zero_ready")
                w1_ready = sig("w1_ready")
                first.buffers(lambda name, shape, dt=F32: tmp("first_" + name, shape, dt),
                              lambda name, shape: inner.enter_context(nc.psum_tensor("first_" + name, shape, F32)))

                def tile_of(g, j):
                    return Group(g.g * GT + j, g.g, j, g.known)

                dstp = a["dst"]
                loads = [(w1raw[:], a["L0_gnn_W1"].rearrange("(h k) n -> k h n", h=2)),
                         (w2[:], a["L0_gnn_W2"]), (wg1[:], a["L1_gnn_W1"]), (wg2[:], a["L1_gnn_W2"]),
                         (wl2[:], a["L2_gnn_W"]), (wl2sum[:], a["L2_gnn_W"][D:2 * D, :]),
                         (wmse[0:D, :], a["L3_gnn_msg_W1"][0:D, :]),
                         (wmt[:], a["L3_gnn_msg_W1"][D:2 * D, :]),
                         (wmse[D:P, :], a["L3_gnn_msg_W1"][2 * D:3 * D, :]),
                         (wm2[:], a["L3_gnn_msg_W2"]), (wn1[:], a["L3_gnn_node_W1"]), (wn2[:], a["L3_gnn_node_W2"])]
                loads.append((srcs.rearrange("p (g j) -> p g j", j=GT), a["src"].rearrange("(g p j) -> p g j", p=P, j=GT)))
                for k, n in enumerate(COLS):
                    size = a[n].shape[0]
                    loads.append((cols[0:size, k:k + 1], a[n].rearrange("(n o) -> n o", o=1)))
                for k, n in enumerate(ROWS):
                    loads.append((rows[:, k, :], a[n].rearrange("(o n) -> o n", o=1).to_broadcast([P, D])))

                with nc.Block() as block:
                    @block.sync
                    def _(sp):
                        sp.dma_start(dsti[:], dstp[1:1 + N].rearrange("(p c) -> p c", p=P)).then_inc(dst_in, 16)
                        for t, off in ((cur, 1), (nxt, 2), (prv, 0)):
                            sp.dma_start(t[:], dstp[off:off + N].rearrange("(q c) -> q c", q=E98)).then_inc(edges_in, 16)
                        steps(sp, *first.sp(sp))
                        sp.wait_ge(rows_ready, 5)
                        for t, to in ((relh, relrow), (far, farrow), (keep, keeprow)):
                            sp.dma_start(to.rearrange("(q c) -> q c", q=E98), t).then_inc(rows_out, 16)
                        sp.dma_start(msgs[0:N, D:MW].rearrange("(q c) f -> q c f", q=E98), tgts).then_inc(rows_out, 16)
                        sp.dma_start(firstnode.rearrange("(q j) -> q j", q=E98), first4i[:]).then_inc(first_out, 16)
                        sp.wait_ge(first_out, 16)
                        sp.dma_start(firsts[:], firstnode.rearrange("(o t) -> o t", o=1)).then_inc(first_in, 16)
                        sp.wait_ge(rows_out, 64)
                        sp.wait_ge(idx_ready, 1)
                        sp.dma_start(fetchidx.rearrange("g p j -> p g j"), idxi.rearrange("p (g j) -> p g j", j=GT)
                                     ).then_inc(rows_out, 16)
                        sp.wait_ge(zero_ready, 1)
                        sp.dma_start(msgs[N:N + P, :], zero[:]).then_inc(rows_out, 16)
                        sp.wait_ge(rows_out, 96)
                        sp.wait_ge(first_in, 16)

                    @block.scalar
                    def _(act):
                        for to, frm in loads:
                            act.dma_start(to, frm).then_inc(weights_in, 16)
                        act.wait_ge(weights_in, 16 * len(loads))
                        act.wait_ge(made, 9)
                        stages = first.act(act)

                        def nodes(t):
                            for stage, _ in stages:
                                stage(t)
                        steps(act, nodes, first.store)
                        first.sg.stored.wait_all(act, first.stores, GROUPS)
                        act.wait_ge(deg_ready, 1)
                        nc.scalar.activation(dinv[:], degp[:], ACT.Sqrt).then_inc(rooted, 1)

                    @block.gpsimd
                    def _(pool):
                        nc.gpsimd.iota(ioti[:], [[1, TILES]], base=0, channel_multiplier=0).then_inc(made, 1)
                        nc.gpsimd.iota(blocki[:], [[P, TILES]], base=0, channel_multiplier=0).then_inc(made, 1)
                        nc.gpsimd.iota(pcoli[:], [[1, WK]], base=0, channel_multiplier=WK).then_inc(made, 1)
                        nc.gpsimd.memset(ident[:], 0.0).then_inc(made, 1)
                        nc.gpsimd.memset(ones[:], 1.0).then_inc(made, 1)
                        nc.gpsimd.memset(relmax[:], 0.0).then_inc(made, 1)
                        nc.gpsimd.memset(zero[:], 0.0).then_inc(zero_ready, 1)
                        nc.gpsimd.memset(epsc[:], EPS).then_inc(made, 1)
                        pool.wait_ge(made, 7)
                        nc.gpsimd.affine_select(out=ident[:], in_=ident[:], compare_op=ALU.not_equal, fill=1.0, base=0,
                                                pattern=[[-1, P]], channel_multiplier=1).then_inc(made, 1)
                        nc.gpsimd.affine_select(out=below[:], in_=ones[:], compare_op=ALU.is_ge, fill=0.0, base=-1,
                                                pattern=[[1, P]], channel_multiplier=-1).then_inc(made, 1)
                        pool.wait_ge(rel_ready, 1)
                        nc.gpsimd.partition_all_reduce(relall[:], relmax[:], P, RMAX).then_inc(relall_ready, 1)

                    @block.tensor
                    def _(pe):
                        pe.wait_ge(made, 9)
                        pe.wait_ge(w1_ready, 1)
                        nodes, lag = first.pe(pe)

                        def nodes_and_counts(t):
                            nodes(t)
                            g = t.at(0)
                            if g is None:
                                return
                            for j in range(GT):
                                tile = tile_of(g, j)
                                pe.wait_ge(hot.sem, hot.after(tile))
                                gate(pe, "pe")
                                nc.tensor.matmul(hist[:], hotlo[:, j, :], hothi[:, j, :],
                                                 start=tile.known and tile.g == 0, stop=tile.known and tile.g == TILES - 1,
                                                 skip_group_check=True).then_inc(hot_used.sem, 1)
                        steps(pe, nodes_and_counts, lag)
                        pe.wait_ge(sums, 1)
                        nc.tensor.matmul(prefix[:], below[:], deg[:], start=True, stop=True)
                        nc.tensor.matmul(totals[:], ones[:], deg[:], start=True, stop=True).then_inc(sums, 1)

                    @block.vector
                    def _(dve):
                        n = [0]

                        def link(ins):
                            n[0] += 1
                            ins.then_inc(chain, 1)
                            dve.wait_ge(chain, n[0])

                        v = nc.vector
                        dve.wait_ge(made, 7)
                        v.tensor_copy(ioth[:], ioti[:]).then_inc(chain, 1)
                        v.tensor_copy(iota[:], ioti[:, 0:P]).then_inc(chain, 1)
                        v.tensor_copy(pcol[:], pcoli[:]).then_inc(chain, 1)
                        n[0] = 3
                        link(v.tensor_copy(blockf[:], blocki[:]))
                        dve.wait_ge(dst_in, 16)
                        link(v.tensor_scalar(loi[:], dsti[:], P - 1, None, ALU.bitwise_and))
                        link(v.tensor_scalar(hii[:], dsti[:], 7, None, ALU.logical_shift_right))
                        link(v.tensor_copy(lo[:], loi[:]))
                        link(v.tensor_copy(hi[:], hii[:]))

                        dve.wait_ge(edges_in, 48)
                        link(v.tensor_tensor(last[:], cur[:], nxt[:], ALU.not_equal))
                        link(v.scalar_tensor_tensor(out=lastt[:], in0=cur[:], scalar=1.0, in1=last[:], op0=ALU.add, op1=ALU.mult))
                        v.tensor_scalar(tgts[:, :, 1], lastt[:], -1.0, None, ALU.add)
                        v.tensor_copy(tgts[:, :, 0], cur[:])
                        link(v.tensor_tensor(keep[:], cur[:], prv[:], ALU.is_equal))
                        v.tensor_scalar(far[:], keep[:], -FAR, FAR, ALU.mult, ALU.add).then_inc(rows_ready, 1)
                        link(v.tensor_scalar(first4[:], cur.rearrange("q (j c) -> q j c", j=GT)[:, :, 0], float(N - WIN), None, ALU.min))
                        v.tensor_copy(first4i[:], first4[:]).then_inc(rows_ready, 1)
                        link(v.tensor_tensor(rel.rearrange("q (j c) -> q j c", j=GT), cur.rearrange("q (j c) -> q j c", j=GT),
                                             first4.unsqueeze(2).to_broadcast([E98, GT, P]), ALU.subtract))
                        link(v.tensor_copy(relh, rel))
                        v.tensor_reduce(relmax[0:E98, :], rel[:], AX_X, ALU.max).then_inc(rel_ready, 1)
                        dve.sem_inc(rows_ready, 3)

                        dve.wait_ge(weights_in, 16 * len(loads))
                        link(v.tensor_tensor(w1[:, 0, :], w1raw[:, 0, :], w1raw[:, 1, :], ALU.subtract))
                        link(v.tensor_copy(w1[:, 1, :], w1raw[:, 1, :]))
                        dve.sem_inc(w1_ready, 1)

                        nodes, lag = first.dve(dve)

                        def nodes_and_onehots(t):
                            nodes(t)
                            g = t.at(0)
                            if g is None:
                                return
                            for j in range(GT):
                                tile = tile_of(g, j)
                                if tile.from_(GT):
                                    dve.wait_ge(hot_used.sem, hot_used.after(tile, GT))
                                v.tensor_scalar(hotlo[:, j, :], ioth[:, 0:P], lo[:, bass.ds(tile.g, 1)], None, ALU.is_equal)
                                v.tensor_scalar(hothi[:, j, :], ioth[:], hi[:, bass.ds(tile.g, 1)], None,
                                                ALU.is_equal).then_inc(hot.sem, 1)
                        steps(dve, nodes_and_onehots, lag)

                        dve.wait_ge(hot_used.sem, TILES)
                        v.tensor_copy(deg[:], hist[:]).then_inc(sums, 1)
                        dve.wait_ge(sums, 2)
                        v.tensor_scalar(degp[:], deg[:], 1.0, None, ALU.add).then_inc(deg_ready, 1)
                        link(v.tensor_scalar(invdeg[:], deg[:], 1.0, None, ALU.max))
                        link(v.reciprocal(invdeg[:], invdeg[:]))
                        link(v.tensor_copy(tot[:], totals[:]))
                        link(v.tensor_scalar(has[:], deg[:], 1.0, None, ALU.min))
                        link(v.tensor_tensor_scan(incl[:], iota[:, 0:1].to_broadcast([P, TILES]), tot[:], 0.0, ALU.add, ALU.add))
                        link(v.tensor_tensor(excl[:], incl[:], tot[:], ALU.subtract))
                        link(v.tensor_scalar(sc[:], excl[0:1, :], float(N - WIN), None, ALU.min))
                        v.tensor_copy(starts[:], sc[:]).then_inc(chain, 1)
                        n[0] += 1
                        link(v.tensor_tensor(st[:], excl[:], prefix[:], ALU.add))
                        link(v.scalar_tensor_tensor(out=idxf[:], in0=st[:], scalar=float(-1 - N), in1=deg[:], op0=ALU.add, op1=ALU.add))
                        link(v.tensor_tensor(idxf[:], idxf[:], has[:], ALU.mult))
                        link(v.tensor_scalar(idxf[:], idxf[:], float(N), None, ALU.add))
                        v.tensor_copy(idxi[:], idxf[:]).then_inc(idx_ready, 1)
                        link(v.tensor_tensor(has[0:1, :], sc[:], blockf[0:1, :], ALU.subtract))
                        link(v.tensor_reduce(over[:, 4:5], has[0:1, :], AX_X, ALU.max))
                        link(v.tensor_scalar(over[:, 5:6], over[:, 4:5], float((1 + AHEAD) * GR - (GT - 1) * P - WIN), None, ALU.is_gt))
                        link(v.tensor_tensor(sc[:], incl[0:1, :], sc[:], ALU.subtract))
                        link(v.tensor_reduce(over[:, 0:1], sc[:], AX_X, ALU.max))
                        link(v.tensor_scalar(over[:, 1:2], over[:, 0:1], float(WIN), None, ALU.is_gt))
                        dve.wait_ge(relall_ready, 1)
                        link(v.tensor_scalar(over[:, 2:3], relall[0:1, :], float(WIN - 1), None, ALU.is_gt))
                        link(v.tensor_tensor(over[:, 3:4], over[:, 1:2], over[:, 2:3], ALU.max))
                        link(v.tensor_tensor(over[:, 6:7], over[:, 3:4], over[:, 5:6], ALU.max))
                        link(v.tensor_copy(flag[:], over[:, 6:7]))
                        dve.wait_ge(rooted, 1)
                        link(v.reciprocal(dinv[:], dinv[:]))
        class Signals:

            def __init__(self, path):
                self.path, self.tallies = path, []
                self.landed = Landing([sem(f"{path}_landed{k}") for k in range(UNROLL)])
                gathers = path != "fast_n"
                self.fetched = Landing([sem(f"{path}_fetched{k}") for k in range(UNROLL)] if gathers else [])
                self.stored = Landing([sem(f"{path}_stored{k}") for k in range(UNROLL)])

            def tally(self, name):
                self.tallies.append(Tally(sem(f"{self.path}_{name}")))
                return self.tallies[-1]

            def close(self, loads, gathers, stores):
                for t in self.tallies:
                    if t.used:
                        t.base, t.used = t.base + GROUPS, False
                self.landed.close(loads, GROUPS)
                self.fetched.close(gathers, GROUPS)
                self.stored.close(stores, GROUPS)

            def close_own(self):
                self.owned.close(1, GROUPS)

        class NodeSignals(Signals):
            def __init__(self, path):
                super().__init__(path)
                tally = self.tally
                self.owned = Landing([sem(f"{path}_owned{k}") for k in range(UNROLL)])
                if path == "fast_n":
                    self.rel = tally("rel")
                    self.hot = tally("hot")
                self.joined = tally("joined")
                self.mixed = tally("mixed")
                self.biased = tally("biased")
                self.x_new = tally("x_new")
                self.summed = tally("summed")
                self.centred = tally("centred")
                self.inverted = tally("inverted")
                self.normed = tally("normed")
                self.scaled = tally("scaled")
                self.offset = tally("offset")
                self.with_h = tally("with_h")
                self.final = tally("final")
                self.shifted = tally("shifted")
                self.stat = tally("stat")
                if path == "fast_n":
                    self.agged = tally("agged")
                self.turned = tally("turned")
                self.multiplied = tally("multiplied")
                self.hid_sum = tally("hid_sum")
                self.varied = tally("varied")
                self.rooted = tally("rooted")
                self.turned_sb = tally("turned_sb")
                self.hidden = tally("hidden")
                self.affined = tally("affined")

        class EdgeSignals(Signals):
            def __init__(self, path):
                super().__init__(path)
                tally = self.tally
                if path == "fast_e":
                    self.targeted = Landing([sem(f"{path}_targeted{k}") for k in range(UNROLL)])
                self.indexed = tally("indexed")
                if path == "fast_e":
                    self.rel_hot = tally("rel_hot")
                self.summed_e = tally("summed_e")
                self.hidden_e = tally("hidden_e")
                self.tgt_sb = tally("tgt_sb")
                self.hid_sum = tally("ehid_sum")
                self.hid_sb = tally("hid_sb")
                self.msg = tally("msg")
                self.msg_sb = tally("msg_sb")
                self.scanned = tally("scanned")
                self.turned_e = tally("turned_e")
                self.out_ready = tally("out_ready")

        def either(eng, fast, general):
            if mode != "both":
                return (general if mode == "general" else fast)(eng)
            v = nc.values_load(flag[0:1, 0:1], engines=(eng.engine,), min_val=0, max_val=1)
            with eng.If(v > 0):
                general(eng)
            if fast:
                with eng.Else():
                    fast(eng)

        def tabrows(tab, g):
            return tab.rearrange("(g j p) f -> g p j f", p=P, j=GT)[bass.ds(g, 1)].rearrange("o p j f -> (o p) j f")

        def edgerows(tab, g):
            return tab.rearrange("(g p j) f -> g p j f", p=P, j=GT)[bass.ds(g, 1)].rearrange("o p j f -> (o p) j f")

        def edgecols(vec, g, parts):
            return vec.rearrange("(g c) -> g c", c=GR)[bass.ds(g, 1)].to_broadcast([parts, GR])

        class NodePass:

            def __init__(self, kind, general, sg, qin, qout, banks, source=None):
                self.kind, self.general, self.sg, self.qin, self.qout = kind, general, sg, qin, qout
                self.banks, self.source = banks, source
                self.windowed = kind in (1, 2, 4, 5, 6) and not general
                self.gathered = kind in (1, 2, 4, 5, 6) and general
                self.norms = kind in (0, 1, 4, 5)
                self.own = kind in (2, 4, 5, 6)
                self.late = kind in (5, 6)
                self.apart = kind == 5 and not general
                self.loads = (4 if self.windowed else 0) + (1 if self.gathered else 0) + (kind in (0, 3))
                self.gathers = GT if self.gathered else 0
                self.stores = 2 if kind == 0 else 1
                mix = 1 if self.apart else {0: 0, 3: 1, 6: 1}.get(kind, 2)
                self.mix = mix
                self.turn = {0: 2, 1: mix + 2, 2: mix + 1, 5: mix + 1, 6: mix + 1}.get(kind)
                self.product = {0: 4, 1: mix + 3, 3: 2, 5: mix + 2, 6: mix + 3}.get(kind)
                if self.apart:
                    self.turn = 1
                self.norm = self.product + 1 if self.late else mix
                self.scale = self.norm + 1
                self.evac = self.product + 1 if kind in (0, 1, 3) else None
                self.store = 1 + (self.evac or (self.turn if kind == 2 else self.scale))

            def bank(self, tensors, g):
                return tensors[g.pair % len(tensors)]

            def buffers(self, tmp, ps):
                k = self.kind
                if self.windowed:
                    self.win = tmp("win", [WP, UNROLL, GT, WK, MW])
                    self.hot = tmp("hot", [WP, 2, GT, WK, P])
                    self.relw = tmp("relw", [WP, 2, GT, WK])
                    if self.apart:
                        self.agg = [ps(f"agg{b}", [D, GR]) for b in range(self.banks["agg"])]
                        self.agg_sb = tmp("agg_sb", [D, 2, GR])
                        self.mean = tmp("mean", [P, 2, GT, D])
                    else:
                        self.agg = [ps(f"agg{b}", [P, GT, D]) for b in range(self.banks["agg"])]
                if self.gathered:
                    self.fidx = tmp("fidx", [P, UNROLL, GT], I32)
                    self.aggs = tmp("aggs", [P, UNROLL, GT, MW])
                if self.own and (not self.late or self.apart):
                    self.ownb = tmp("ownb", [P, UNROLL, GT, D])
                if self.late and not self.apart:
                    self.hn = tmp("hn", [P, UNROLL, GT, P])
                if k == 3:
                    self.yin = tmp("yin", [D, UNROLL, GR])
                    self.zb = tmp("zb", [D, 2, GR])
                    self.zs = tmp("zs", [D, 2, GR])
                if k == 2:
                    self.mixb = tmp("mix", [P, 2, GT, D])
                    self.yout = tmp("yout", [D, UNROLL, GR])
                if k == 4:
                    self.mixb = tmp("mix", [P, 2, GT, D])
                    self.hout = tmp("hout", [P, UNROLL, GT, D])
                if k == 5:
                    self.hout = tmp("hout", [P, UNROLL, GT, D])
                if self.norms or k == 6:
                    self.s1, self.s2, self.sd, self.rs = (tmp(n, [P, 2, GT]) for n in ("s1", "s2", "sd", "rs"))
                    self.xc, self.sq = tmp("xc", [P, 2, GT, D]), tmp("sq", [P, 2, GT, D])
                if k in (0, 1):
                    self.hb = tmp("hb", [P, 2, GT, D])
                if k == 6:
                    self.yb, self.fb = tmp("yb", [P, 2, GT, D]), tmp("fb", [P, UNROLL, GT, D])
                    self.hidp = [ps("hidp0", [HID, GR])]
                    self.hids = tmp("hids", [HID, 2, GR])
                self.rowsT = P if self.late and not self.apart else D
                if k != 4 and k != 3:
                    self.tp = [ps(f"tp{b}", [self.rowsT, GR]) for b in range(self.banks["tp"])]
                if k in (0, 1, 5, 6):
                    self.ts = tmp("ts", [self.rowsT, 2, GR])
                if k in (0, 1, 3, 5, 6):
                    self.width = 2 * D if k == 0 or self.apart else D
                    self.mp = [ps(f"mp{b}", [P, GT, self.width]) for b in range(self.banks["mp"])]
                if k in (0, 1, 3):
                    self.outb = tmp("outb", [P, UNROLL, GT, self.width])

            def sp(self, eng):
                sg, k = self.sg, self.kind

                def step(t):
                    g = t.at(0)
                    if g is not None:
                        land = sg.landed.sems[g.slot]
                        if k == 0:
                            if g.from_(UNROLL):
                                eng.wait_ge(sg.summed.sem, sg.summed.after(g, UNROLL))
                            gate(eng, "sp")
                            eng.dma_start(xs[:, bass.ds(g.g * GT, GT), :], tabrows(a["x"], g.g)).then_inc(land, 16)
                        if k == 3:
                            if g.from_(UNROLL):
                                eng.wait_ge(sg.affined.sem, sg.affined.after(g, UNROLL))
                            gate(eng, "sp")
                            eng.dma_start(self.yin[:, g.slot, :], yT[:, bass.ds(g.g * GR, GR)]).then_inc(land, 16)
                        if self.gathered:
                            if g.from_(UNROLL):
                                eng.wait_ge(sg.fetched.sems[g.slot], sg.fetched.after(g, GT, 1))
                                gate(eng, "sp")
                            eng.dma_start(self.fidx[:, g.slot, :], fetchidx[bass.ds(g.g, 1)].rearrange("o p j -> (o p) j")).then_inc(land, 16)
                        if self.windowed:
                            self.wait_for_messages(eng, g)
                            if g.from_(UNROLL):
                                eng.wait_ge(sg.agged.sem, sg.agged.after(g, UNROLL))
                            gate(eng, "sp")
                            for j, s in enumerate(window_starts(eng, starts, g.g)):
                                eng.dma_start(self.win[:, g.slot, j, :, :],
                                              msgs[bass.ds(s, WIN), :].rearrange("(p k) f -> p k f", k=WK)).then_inc(land, 16)
                    g = t.at(self.mix) if self.own else None
                    if g is not None:
                        if g.from_(UNROLL):
                            if self.late:
                                eng.wait_ge(sg.turned.sem, sg.turned.after(g, UNROLL))
                                gate(eng, "sp")
                            if k == 6:
                                eng.wait_ge(sg.with_h.sem, sg.with_h.after(g, UNROLL))
                            if not self.late:
                                eng.wait_ge(sg.mixed.sem, sg.mixed.after(g, UNROLL))
                        gate(eng, "sp")
                        to = self.hn[:, g.slot, :, 0:D] if self.late and not self.apart else self.ownb[:, g.slot]
                        eng.dma_start(to, tabrows(self.qin, g.g)).then_inc(sg.owned.sems[g.slot], 16)
                return step, self.mix if self.own else 0

            def wait_for_messages(self, eng, g):
                if self.source is None:
                    return
                if not g.known:
                    groups = [Group(g.g + AHEAD, g.turn + (g.slot + AHEAD) // UNROLL, (g.slot + AHEAD) % UNROLL, False)]
                else:
                    groups = [Group(e, e // UNROLL, e % UNROLL, True)
                              for e in range(0 if g.g == 0 else g.g + AHEAD, min(g.g + AHEAD, GROUPS - 1) + 1)]
                for e in groups:
                    eng.wait_ge(self.source.sg.stored.sems[e.slot], self.source.sg.stored.after(e, 1))
                gate(eng, "sp")

            def pool(self, eng):
                sg = self.sg
                if not self.gathered:
                    return None

                def step(t):
                    g = t.at(0)
                    if g is None:
                        return
                    eng.wait_ge(sg.landed.sems[g.slot], sg.landed.after(g, self.loads))
                    if g.from_(UNROLL):
                        eng.wait_ge(sg.mixed.sem, sg.mixed.after(g, UNROLL))
                    gate(eng, "pool")
                    for j in range(GT):
                        nc.gpsimd.indirect_dma_start(self.aggs[:, g.slot, j, :], None, msgs,
                                                     bass.IndirectOffsetOnAxis(ap=self.fidx[:, g.slot, j:j + 1], axis=0)
                                                     ).then_inc(sg.fetched.sems[g.slot], 16)
                return step, 0

            def pe(self, eng):
                sg, k = self.sg, self.kind

                def step(t):
                    g = t.at(self.product) if self.product else None
                    if g is not None:
                        of = {3: sg.shifted, 6: sg.hidden}.get(k, sg.turned_sb)
                        eng.wait_ge(of.sem, of.after(g))
                        of = sg.x_new if self.late else sg.scaled
                        if g.from_(len(self.mp)):
                            eng.wait_ge(of.sem, of.after(g, len(self.mp)))
                        gate(eng, "pe")
                        src = self.zs if k == 3 else self.hids if k == 6 else self.ts
                        w = {0: w1.rearrange("k h n -> k (h n)"), 1: wg1, 3: wg2, 5: wl2, 6: wn2}[k]
                        if not self.apart:
                            for j in range(GT):
                                mm = nc.tensor.matmul(self.bank(self.mp, g)[:, j, :], src[:, g.pair, bass.ts(j, P)], w,
                                                      start=True, stop=True, skip_group_check=True)
                        else:
                            eng.wait_ge(sg.mixed.sem, sg.mixed.after(g))
                            gate(eng, "pe")
                            for j in range(GT):
                                nc.tensor.matmul(self.bank(self.mp, g)[:, j, 0:D], self.ts[:, g.pair, bass.ts(j, P)], wl2[0:D, :],
                                                 start=True, stop=True, skip_group_check=True)
                                mm = nc.tensor.matmul(self.bank(self.mp, g)[:, j, D:2 * D], self.agg_sb[:, g.pair, bass.ts(j, P)],
                                                      wl2sum, start=True, stop=True, skip_group_check=True)
                        mm.then_inc(sg.multiplied.sem, 1)
                    g = t.at(self.turn + 1) if k == 6 else None
                    if g is not None:
                        eng.wait_ge(sg.turned_sb.sem, sg.turned_sb.after(g))
                        if g.from_(1):
                            eng.wait_ge(sg.hidden.sem, sg.hidden.after(g, 1))
                        gate(eng, "pe")
                        nc.tensor.matmul(self.hidp[0][:], wn1, self.ts[:, g.pair, :], start=True, stop=True
                                         ).then_inc(sg.hid_sum.sem, 1)
                    g = t.at(self.turn) if self.turn else None
                    if g is not None:
                        if not self.apart:
                            of = sg.normed if k in (0, 1) else sg.mixed
                            eng.wait_ge(of.sem, of.after(g))
                        if self.late:
                            eng.wait_ge(sg.owned.sems[g.slot], sg.owned.after(g, 1))
                        if g.from_(len(self.tp)):
                            eng.wait_ge(sg.turned_sb.sem, sg.turned_sb.after(g, len(self.tp)))
                        gate(eng, "pe")
                        src = self.ownb[:, g.slot] if self.apart else self.hn[:, g.slot] if self.late else (self.mixb if k == 2 else self.hb)[:, g.pair]
                        for j in range(GT):
                            mm = nc.tensor.transpose(self.bank(self.tp, g)[:, bass.ts(j, P)], src[:, j, :], ident)
                        mm.then_inc(sg.turned.sem, 1)
                    g = t.at(0) if self.windowed else None
                    if g is not None:
                        eng.wait_ge(sg.hot.sem, sg.hot.after(g))
                        eng.wait_ge(sg.landed.sems[g.slot], sg.landed.after(g, self.loads))
                        if g.from_(len(self.agg)):
                            eng.wait_ge(sg.mixed.sem, sg.mixed.after(g, len(self.agg)))
                        gate(eng, "pe")
                        for j in range(GT):
                            for w in range(WK):
                                if self.apart:
                                    mm = nc.tensor.matmul(self.bank(self.agg, g)[:, bass.ts(j, P)], self.win[:, g.slot, j, w, 0:D],
                                                          self.hot[:, g.pair, j, w, :], start=w == 0, stop=w == WK - 1,
                                                          skip_group_check=True)
                                    continue
                                mm = nc.tensor.matmul(self.bank(self.agg, g)[:, j, :], self.hot[:, g.pair, j, w, :],
                                                      self.win[:, g.slot, j, w, 0:D], start=w == 0, stop=w == WK - 1,
                                                      skip_group_check=True)
                        mm.then_inc(sg.agged.sem, 1)
                if k == 4 and not self.windowed:
                    return None
                return step, max(self.turn or 0, self.product or 0)

            def act(self, eng):
                sg, k = self.sg, self.kind

                def banks(t):
                    g = t.at(self.evac) if k == 0 else None
                    if g is not None:
                        eng.wait_ge(sg.multiplied.sem, sg.multiplied.after(g))
                        if g.from_(UNROLL):
                            eng.wait_ge(sg.stored.sems[g.slot], sg.stored.after(g, self.stores, 1))
                        nc.scalar.copy(self.outb[:, g.slot], self.bank(self.mp, g)[:]).then_inc(sg.scaled.sem, 1)
                    g = t.at(self.turn + 1) if k == 6 else None
                    if g is not None:
                        eng.wait_ge(sg.hid_sum.sem, sg.hid_sum.after(g))
                        if g.from_(2):
                            eng.wait_ge(sg.multiplied.sem, sg.multiplied.after(g, 2))
                        nc.scalar.activation(self.hids[:, g.pair, :], self.hidp[0][:], ACT.Relu,
                                             bias=col("L3_gnn_node_b1", HID)).then_inc(sg.hidden.sem, 1)
                    g = t.at(self.mix) if self.apart else None
                    if g is not None:
                        eng.wait_ge(sg.agged.sem, sg.agged.after(g))
                        if g.from_(2):
                            eng.wait_ge(sg.multiplied.sem, sg.multiplied.after(g, 2))
                        nc.scalar.copy(self.agg_sb[:, g.pair, :], self.bank(self.agg, g)[:]).then_inc(sg.mixed.sem, 1)
                    g = t.at(self.turn) if self.turn else None
                    if g is not None:
                        eng.wait_ge(sg.turned.sem, sg.turned.after(g))
                        if k == 2:
                            if g.from_(UNROLL):
                                eng.wait_ge(sg.stored.sems[g.slot], sg.stored.after(g, self.stores, 1))
                            nc.scalar.activation(self.yout[:, g.slot, :], self.bank(self.tp, g)[:], ACT.Identity,
                                                 bias=col("L1_gnn_b1")).then_inc(sg.turned_sb.sem, 1)
                        else:
                            of = sg.hid_sum if k == 6 else sg.multiplied
                            if g.from_(2):
                                eng.wait_ge(of.sem, of.after(g, 2))
                            nc.scalar.copy(self.ts[:, g.pair, :], self.bank(self.tp, g)[:]).then_inc(sg.turned_sb.sem, 1)
                    g = t.at(0) if k == 3 else None
                    if g is not None:
                        eng.wait_ge(sg.landed.sems[g.slot], sg.landed.after(g, self.loads))
                        if g.from_(2):
                            eng.wait_ge(sg.shifted.sem, sg.shifted.after(g, 2))
                        nc.scalar.activation(self.zb[:, g.pair, :], self.yin[:, g.slot, :], ACT.Identity,
                                             bias=bn[:, 5:6], scale=bn[:, 4:5]).then_inc(sg.affined.sem, 1)

                def root(t):
                    g = t.at(self.norm) if self.norms or k == 6 else None
                    if g is not None:
                        eng.wait_ge(sg.centred.sem, sg.centred.after(g))
                        for j in range(GT):
                            sq = nc.scalar.activation(self.sq[:, g.pair, j, :], self.xc[:, g.pair, j, :], ACT.Square,
                                                      accum_out=self.s2[:, g.pair, j:j + 1])
                        sq.then_inc(sg.varied.sem, 1)
                        eng.wait_ge(sg.varied.sem, sg.varied.after(g))
                        if g.from_(2):
                            eng.wait_ge(sg.inverted.sem, sg.inverted.after(g, 2))
                        nc.scalar.activation(self.sd[:, g.pair, :], self.s2[:, g.pair, :], ACT.Sqrt, bias=epsc,
                                             scale=1.0 / D).then_inc(sg.rooted.sem, 1)

                def store(t):
                    g = t.at(self.store)
                    if g is not None:
                        done = sg.stored.sems[g.slot]
                        if k == 0:
                            eng.wait_ge(sg.scaled.sem, sg.scaled.after(g))
                            eng.dma_start(tabrows(tabP, g.g), self.outb[:, g.slot, :, 0:D]).then_inc(done, 16)
                            eng.dma_start(tabrows(self.qout, g.g), self.outb[:, g.slot, :, D:2 * D]).then_inc(done, 16)
                        elif k in (1, 3):
                            eng.wait_ge(sg.scaled.sem, sg.scaled.after(g))
                            eng.dma_start(tabrows(self.qout, g.g), self.outb[:, g.slot]).then_inc(done, 16)
                        elif k == 2:
                            eng.wait_ge(sg.turned_sb.sem, sg.turned_sb.after(g))
                            eng.dma_start(yT[:, bass.ds(g.g * GR, GR)], self.yout[:, g.slot, :]).then_inc(done, 16)
                        elif k in (4, 5):
                            eng.wait_ge(sg.normed.sem, sg.normed.after(g))
                            eng.dma_start(tabrows(self.qout, g.g), self.hout[:, g.slot]).then_inc(done, 16)
                        else:
                            eng.wait_ge(sg.final.sem, sg.final.after(g))
                            eng.dma_start(tabrows(out, g.g), self.fb[:, g.slot]).then_inc(done, 16)
                return [(banks, self.store), (root, self.store), (store, self.store)]

            def dve(self, eng):
                sg, k, v = self.sg, self.kind, nc.vector

                def feats(g):
                    return xs[:, bass.ds(g.g * GT, GT), :]

                def here(vec, g):
                    return over4(vec[:, bass.ds(g.g * GT, GT)])

                def step(t):
                    g = t.at(self.norm) if self.late else None
                    if g is not None:
                        eng.wait_ge(sg.multiplied.sem, sg.multiplied.after(g))
                        if self.apart:
                            v.tensor_tensor(self.mean[:, g.pair], self.bank(self.mp, g)[:, :, D:2 * D], here(invdeg, g), ALU.mult
                                            ).then_inc(sg.joined.sem, 1)
                        if k == 5:
                            v.tensor_tensor(feats(g), feats(g), self.bank(self.mp, g)[:, :, 0:D], ALU.add).then_inc(sg.x_new.sem, 1)
                        else:
                            v.tensor_tensor(self.yb[:, g.pair], self.bank(self.mp, g)[:], row("L3_gnn_node_b2"), ALU.add).then_inc(sg.x_new.sem, 1)
                    g = t.at(self.mix) if k == 6 else None
                    if g is not None:
                        if self.windowed:
                            eng.wait_ge(sg.agged.sem, sg.agged.after(g))
                            agg = self.bank(self.agg, g)[:]
                        elif self.gathered:
                            eng.wait_ge(sg.fetched.sems[g.slot], sg.fetched.after(g, GT))
                            agg = self.aggs[:, g.slot, :, 0:D]
                        if g.from_(UNROLL):
                            eng.wait_ge(sg.turned.sem, sg.turned.after(g, UNROLL))
                        v.tensor_copy(self.hn[:, g.slot, :, D:P], agg).then_inc(sg.mixed.sem, 1)
                        eng.wait_ge(sg.owned.sems[g.slot], sg.owned.after(g, 1))
                        v.tensor_tensor(feats(g), feats(g), self.hn[:, g.slot, :, 0:D], ALU.add).then_inc(sg.with_h.sem, 1)
                    g = t.at(self.evac) if k in (1, 3) else None
                    if g is not None:
                        eng.wait_ge(sg.multiplied.sem, sg.multiplied.after(g))
                        if g.from_(UNROLL):
                            eng.wait_ge(sg.stored.sems[g.slot], sg.stored.after(g, self.stores, 1))
                        v.tensor_tensor(self.outb[:, g.slot], self.bank(self.mp, g)[:], here(dinv, g), ALU.mult).then_inc(sg.scaled.sem, 1)
                    mix = t.at(self.mix) if k != 6 and not self.apart else None
                    hot = t.at(0) if self.windowed else None
                    norm = t.at(self.norm) if self.norms or k == 6 else None
                    scale = t.at(self.scale) if self.norms or k == 6 else None
                    g = mix
                    if g is not None:
                        if self.windowed:
                            eng.wait_ge(sg.agged.sem, sg.agged.after(g))
                            agg = self.bank(self.agg, g)[:]
                        elif self.gathered:
                            eng.wait_ge(sg.fetched.sems[g.slot], sg.fetched.after(g, GT))
                            agg = self.aggs[:, g.slot, :, 0:D]
                        if k == 1:
                            v.tensor_tensor(feats(g), feats(g), agg, ALU.add).then_inc(sg.mixed.sem, 1)
                        elif k in (2, 4):
                            eng.wait_ge(sg.owned.sems[g.slot], sg.owned.after(g, 1))
                            if k == 2:
                                if g.from_(2):
                                    eng.wait_ge(sg.turned.sem, sg.turned.after(g, 2))
                            v.tensor_tensor(self.mixb[:, g.pair], self.ownb[:, g.slot], agg, ALU.add).then_inc(sg.joined.sem, 1)
                        elif k == 5:
                            if g.from_(UNROLL):
                                eng.wait_ge(sg.turned.sem, sg.turned.after(g, UNROLL))
                            v.tensor_tensor(self.hn[:, g.slot, :, D:P], agg, here(invdeg, g), ALU.mult).then_inc(sg.mixed.sem, 1)
                        elif k == 3:
                            eng.wait_ge(sg.affined.sem, sg.affined.after(g))
                            if g.from_(2):
                                eng.wait_ge(sg.multiplied.sem, sg.multiplied.after(g, 2))
                            v.scalar_tensor_tensor(out=self.zs[:, g.pair, :], in0=self.zb[:, g.pair, :], scalar=SLOPE,
                                                   in1=self.zb[:, g.pair, :], op0=ALU.mult, op1=ALU.max).then_inc(sg.shifted.sem, 1)
                    g = hot
                    if g is not None:
                        eng.wait_ge(sg.landed.sems[g.slot], sg.landed.after(g, self.loads))
                        c = D + (1 if k == 1 else 0)
                        v.tensor_tensor(self.relw[:, g.pair], self.win[:, g.slot, :, :, c],
                                        blockf[0:WP, bass.ds(g.g * GT, GT)].unsqueeze(2).to_broadcast([WP, GT, WK]),
                                        ALU.subtract).then_inc(sg.rel.sem, 1)
                    g = mix
                    if g is not None and k in (2, 4):
                        eng.wait_ge(sg.joined.sem, sg.joined.after(g))
                        v.tensor_tensor(self.mixb[:, g.pair], self.mixb[:, g.pair], here(dinv, g), ALU.mult).then_inc(sg.mixed.sem, 1)
                    g = norm
                    if g is not None and k == 5:
                        eng.wait_ge(sg.x_new.sem, sg.x_new.after(g))
                        v.tensor_tensor(feats(g), feats(g), row("L2_gnn_b"), ALU.add).then_inc(sg.biased.sem, 1)
                    g = hot
                    if g is not None:
                        eng.wait_ge(sg.rel.sem, sg.rel.after(g))
                        if g.from_(2):
                            eng.wait_ge(sg.agged.sem, sg.agged.after(g, 2))
                        v.tensor_tensor(self.hot[:, g.pair].rearrange("p j k n -> p (j k) n"),
                                        iota[0:WP, :].unsqueeze(1).to_broadcast([WP, GT * WK, P]),
                                        self.relw[:, g.pair].rearrange("p j k -> p (j k)").unsqueeze(2).to_broadcast([WP, GT * WK, P]),
                                        ALU.is_equal).then_inc(sg.hot.sem, 1)
                    g = norm
                    if g is not None and self.apart:
                        eng.wait_ge(sg.biased.sem, sg.biased.after(g))
                        eng.wait_ge(sg.joined.sem, sg.joined.after(g))
                        v.tensor_tensor(feats(g), feats(g), self.mean[:, g.pair], ALU.add).then_inc(sg.with_h.sem, 1)
                    g = mix
                    if g is not None and k == 4:
                        eng.wait_ge(sg.mixed.sem, sg.mixed.after(g))
                        v.tensor_tensor(self.mixb[:, g.pair], self.mixb[:, g.pair], row("L1_gnn_b2"), ALU.add).then_inc(sg.biased.sem, 1)
                    g = scale
                    if g is not None:
                        eng.wait_ge(sg.rooted.sem, sg.rooted.after(g))
                        v.reciprocal(self.rs[:, g.pair, :], self.sd[:, g.pair, :]).then_inc(sg.inverted.sem, 1)
                    g = mix
                    if g is not None and k == 4:
                        eng.wait_ge(sg.biased.sem, sg.biased.after(g))
                        v.tensor_tensor(feats(g), feats(g), self.mixb[:, g.pair], ALU.add).then_inc(sg.x_new.sem, 1)
                    g = scale
                    if g is not None:
                        eng.wait_ge(sg.inverted.sem, sg.inverted.after(g))
                        r = over4(self.rs[:, g.pair, :])
                        c, f = self.xc[:, g.pair], self.fb[:, g.slot] if k == 6 else None
                        if k < 6:
                            if k in (0, 1):
                                if g.from_(2):
                                    eng.wait_ge(sg.turned.sem, sg.turned.after(g, 2))
                                to = self.hb[:, g.pair]
                            else:
                                if g.from_(UNROLL):
                                    eng.wait_ge(sg.stored.sems[g.slot], sg.stored.after(g, self.stores, 1))
                                to = self.hout[:, g.slot]
                            v.scalar_tensor_tensor(out=to, in0=c, scalar=0.0, in1=r, op0=ALU.max,
                                                   op1=ALU.mult).then_inc(sg.normed.sem, 1)
                        else:
                            v.tensor_tensor(c, c, r, ALU.mult).then_inc(sg.normed.sem, 1)
                    g = norm
                    if g is not None:
                        if k == 0:
                            eng.wait_ge(sg.landed.sems[g.slot], sg.landed.after(g, self.loads))
                            gate(eng, "dve")
                        else:
                            of = sg.with_h if self.apart else {1: sg.mixed, 4: sg.x_new, 5: sg.biased, 6: sg.x_new}[k]
                            eng.wait_ge(of.sem, of.after(g))
                            gate(eng, "dve")
                        src = self.yb[:, g.pair] if k == 6 else feats(g)
                        v.tensor_reduce(self.s1[:, g.pair, :], src, AX_X, ALU.add).then_inc(sg.summed.sem, 1)
                    g = scale
                    if g is not None and k == 6:
                        eng.wait_ge(sg.normed.sem, sg.normed.after(g))
                        v.tensor_tensor(c, c, row("L3_gnn_ln_scale"), ALU.mult).then_inc(sg.scaled.sem, 1)
                    g = norm
                    if g is not None:
                        eng.wait_ge(sg.summed.sem, sg.summed.after(g))
                        if g.from_(2):
                            eng.wait_ge(sg.varied.sem, sg.varied.after(g, 2))
                        v.scalar_tensor_tensor(out=self.xc[:, g.pair], in0=over4(self.s1[:, g.pair, :]), scalar=-1.0 / D, in1=src,
                                               op0=ALU.mult, op1=ALU.add).then_inc(sg.centred.sem, 1)
                    g = scale
                    if g is not None and k == 6:
                        eng.wait_ge(sg.scaled.sem, sg.scaled.after(g))
                        v.tensor_tensor(c, c, row("L3_gnn_ln_offset"), ALU.add).then_inc(sg.offset.sem, 1)
                        eng.wait_ge(sg.offset.sem, sg.offset.after(g))
                        eng.wait_ge(sg.with_h.sem, sg.with_h.after(g))
                        if g.from_(UNROLL):
                            eng.wait_ge(sg.stored.sems[g.slot], sg.stored.after(g, self.stores, 1))
                        v.tensor_tensor(f, c, feats(g), ALU.add).then_inc(sg.final.sem, 1)
                    g = t.at(self.turn + 1) if k == 2 else None
                    if g is not None:
                        eng.wait_ge(sg.turned_sb.sem, sg.turned_sb.after(g))
                        gate(eng, "dve")
                        last = GR if not (g.known and g.g == GROUPS - 1) else N_TRUE - (GROUPS - 1) * GR
                        v.bn_stats(stats[:, bass.ds(g.g, 1), :].rearrange("p o s -> p (o s)"), self.yout[:, g.slot, 0:last]
                                   ).then_inc(sg.stat.sem, 1)
                return step, max(self.evac or 0, self.scale if self.norms or k == 6 else 0, self.turn + 1 if k == 2 else 0)

        class EdgePass:

            def __init__(self, kind, general, sg, qin, banks):
                self.kind, self.general, self.sg, self.qin, self.banks = kind, general, sg, qin, banks
                self.stores = 1
                self.scans = kind == "max" or general
                self.spread = kind in ("max", "mlp") and not general
                self.both = kind in ("max", "mlp") and general
                self.gathers = GT * (2 if self.both else 1)
                self.loads = (4 if self.spread else 0) + self.both + self.scans + (kind == "mlp")
                self.store = {"sum": 2, "max": 3, "mlp": 4}[kind] + 1 if self.scans else 4 if kind == "mlp" else 1

            def bank(self, tensors, g):
                return tensors[g.pair % len(tensors)]

            def buffers(self, tmp, ps):
                k = self.kind
                self.W = P if k == "mlp" else D
                self.sidx = tmp("sidx", [P, UNROLL, GT], I32)
                self.rowsb = tmp("rowsb", [P, UNROLL, GT, self.W])
                if self.both:
                    self.tidx = tmp("tidx", [P, UNROLL, GT], I32)
                    self.trows = tmp("trows", [P, UNROLL, GT, D])
                if self.spread:
                    self.win = tmp("twin", [WP, UNROLL, GT, WK, D])
                    self.relb = tmp("relb", [WP, UNROLL, GR], F16)
                    self.hot = tmp("ehot", [WP, 2, WK, GR])
                if k != "sum" or self.scans:
                    self.s_ps = [ps(f"s_ps{b}", [self.W, GR]) for b in range(self.banks["s"])]
                    self.h_sb = tmp("h_sb", [self.W, 2, GR])
                if k == "mlp":
                    self.t_ps = ps("t_ps", [D, GR])
                    self.t_sb = tmp("t_sb", [D, 2, GR])
                    self.hid_ps = ps("hid_ps", [HID, GR])
                    self.hid = tmp("hid", [HID, 2, GR])
                if self.scans:
                    self.mask = tmp("mask", [D, UNROLL, GR])
                    self.sc = tmp("scan", [D, 2, GR])
                    if k != "sum":
                        self.m_ps = ps("m_ps", [D, GR])
                        self.m_sb = tmp("m_sb", [D, 2, GR])
                if self.scans or k == "mlp":
                    self.o_ps = [ps(f"o_ps{b}", [P, GT, D]) for b in range(self.banks["o"])]
                    self.outb = tmp("eoutb", [P, UNROLL, GT, D])
                else:
                    self.outb = self.rowsb

            def sp(self, eng):
                sg, k = self.sg, self.kind

                def step(t):
                    g = t.at(0)
                    if g is not None:
                        land = sg.landed.sems[g.slot]
                        if self.both:
                            if g.from_(UNROLL):
                                eng.wait_ge(sg.fetched.sems[g.slot], sg.fetched.after(g, self.gathers, 1))
                                gate(eng, "sp")
                            eng.dma_start(self.tidx[:, g.slot, :], a["dst"][1:1 + N].rearrange("(g p j) -> g p j", p=P, j=GT)[bass.ds(g.g, 1)].rearrange("o p j -> (o p) j")).then_inc(land, 16)
                        if k == "mlp":
                            if g.from_(UNROLL):
                                eng.wait_ge(sg.summed_e.sem, sg.summed_e.after(g, UNROLL))
                            gate(eng, "sp")
                            eng.dma_start(self.rowsb[:, g.slot, :, D:P], edgerows(a["edge_attr_64"], g.g)).then_inc(land, 16)
                        if self.scans:
                            if g.from_(UNROLL):
                                eng.wait_ge(sg.scanned.sem, sg.scanned.after(g, UNROLL))
                            gate(eng, "sp")
                            eng.dma_start(self.mask[:, g.slot, :], edgecols(farrow if k == "max" else keeprow, g.g, D)).then_inc(land, 16)
                        if self.spread:
                            if g.from_(UNROLL):
                                eng.wait_ge(sg.summed_e.sem, sg.summed_e.after(g, UNROLL))
                            gate(eng, "sp")
                            for j, s in enumerate(window_starts(eng, firsts, g.g)):
                                eng.dma_start(self.win[:, g.slot, j, :, :], (tabP if k == "max" else self.qin)[bass.ds(s, WIN), :].rearrange(
                                    "(p k) f -> p k f", k=WK)).then_inc(land, 16)
                return step, 0

            def pool(self, eng):
                sg, k = self.sg, self.kind
                srctab = self.qin
                tgttab = tabP if k == "max" else self.qin

                def step(t):
                    g = t.at(0)
                    if g is None:
                        return
                    if g.from_(UNROLL):
                        eng.wait_ge(sg.fetched.sems[g.slot], sg.fetched.after(g, self.gathers, 1))
                        gate(eng, "pool")
                    nc.gpsimd.tensor_copy(self.sidx[:, g.slot, :], srcs[:, bass.ds(g.g * GT, GT)]).then_inc(sg.indexed.sem, 1)
                    eng.wait_ge(sg.indexed.sem, sg.indexed.after(g))
                    if self.both:
                        eng.wait_ge(sg.landed.sems[g.slot], sg.landed.after(g, self.loads))
                    if self.outb is self.rowsb:
                        if g.from_(UNROLL):
                            eng.wait_ge(sg.stored.sems[g.slot], sg.stored.after(g, 1, 1))
                    else:
                        if g.from_(UNROLL):
                            eng.wait_ge(sg.summed_e.sem, sg.summed_e.after(g, UNROLL))
                    gate(eng, "pool")
                    for j in range(GT):
                        nc.gpsimd.indirect_dma_start(self.rowsb[:, g.slot, j, 0:D], None, srctab,
                                                     bass.IndirectOffsetOnAxis(ap=self.sidx[:, g.slot, j:j + 1], axis=0)
                                                     ).then_inc(sg.fetched.sems[g.slot], 16)
                        if self.both:
                            nc.gpsimd.indirect_dma_start(self.trows[:, g.slot, j, :], None, tgttab,
                                                         bass.IndirectOffsetOnAxis(ap=self.tidx[:, g.slot, j:j + 1], axis=0)
                                                         ).then_inc(sg.fetched.sems[g.slot], 16)
                return step, 0

            def targets(self, g, to):
                if self.spread:
                    for j in range(GT):
                        for w in range(WK):
                            mm = nc.tensor.matmul(to[:, bass.ts(j, P)], self.win[:, g.slot, j, w, :], self.hot[:, g.pair, w, bass.ts(j, P)],
                                                  start=j == 0 and w == 0, stop=w == WK - 1, skip_group_check=True)
                else:
                    for j in range(GT):
                        mm = nc.tensor.matmul(to[:, j::GT], self.trows[:, g.slot, j, :], ident, start=j == 0, stop=True,
                                              skip_group_check=True)
                return mm

            def pe(self, eng):
                sg, k = self.sg, self.kind
                if k == "sum" and not self.scans:
                    return None

                def step(t):
                    g = t.at({"sum": 2, "max": 3, "mlp": 4}[k]) if self.scans else None
                    if g is not None:
                        eng.wait_ge(sg.scanned.sem, sg.scanned.after(g))
                        if g.from_(self.banks["o"]):
                            eng.wait_ge(sg.out_ready.sem, sg.out_ready.after(g, self.banks["o"]))
                        gate(eng, "pe")
                        for j in range(GT):
                            mm = nc.tensor.transpose(self.bank(self.o_ps, g)[:, j, :], self.sc[:, g.pair, j::GT], ident[0:D, 0:D])
                        mm.then_inc(sg.turned_e.sem, 1)
                    if k != "sum":
                        g = t.at(2 if k == "mlp" else 1)
                        if g is not None:
                            hid_ready = sg.hid_sb if k == "mlp" else sg.hidden_e
                            hid, w = (self.hid, wm2) if k == "mlp" else (self.h_sb, w2)
                            eng.wait_ge(hid_ready.sem, hid_ready.after(g))
                            if self.scans:
                                if g.from_(1):
                                    eng.wait_ge(sg.msg_sb.sem, sg.msg_sb.after(g, 1))
                                gate(eng, "pe")
                                nc.tensor.matmul(self.m_ps[:], w, hid[:, g.pair, :], start=True, stop=True).then_inc(sg.msg.sem, 1)
                            else:
                                if g.from_(self.banks["o"]):
                                    eng.wait_ge(sg.msg_sb.sem, sg.msg_sb.after(g, self.banks["o"]))
                                gate(eng, "pe")
                                for j in range(GT):
                                    mm = nc.tensor.matmul(self.bank(self.o_ps, g)[:, j, :], hid[:, g.pair, j::GT], w, start=True, stop=True,
                                                          skip_group_check=True)
                                mm.then_inc(sg.msg.sem, 1)
                        g = t.at(1)
                        if g is not None and k == "mlp":
                            eng.wait_ge(sg.hidden_e.sem, sg.hidden_e.after(g))
                            eng.wait_ge(sg.tgt_sb.sem, sg.tgt_sb.after(g))
                            if g.from_(1):
                                eng.wait_ge(sg.hid_sb.sem, sg.hid_sb.after(g, 1))
                            gate(eng, "pe")
                            nc.tensor.matmul(self.hid_ps[:], wmse, self.h_sb[:, g.pair, :], start=True, stop=False)
                            nc.tensor.matmul(self.hid_ps[:], wmt, self.t_sb[:, g.pair, :], start=False, stop=True
                                             ).then_inc(sg.hid_sum.sem, 1)
                    g = t.at(0)
                    if g is not None:
                        eng.wait_ge(sg.fetched.sems[g.slot], sg.fetched.after(g, self.gathers))
                        eng.wait_ge(sg.landed.sems[g.slot], sg.landed.after(g, self.loads))
                        if self.spread:
                            eng.wait_ge(sg.rel_hot.sem, sg.rel_hot.after(g))
                        if g.from_(self.banks["s"]):
                            eng.wait_ge(sg.hidden_e.sem, sg.hidden_e.after(g, self.banks["s"]))
                        if k == "mlp":
                            if g.from_(1):
                                eng.wait_ge(sg.tgt_sb.sem, sg.tgt_sb.after(g, 1))
                        gate(eng, "pe")
                        if k == "max":
                            self.targets(g, self.bank(self.s_ps, g))
                            for j in range(GT):
                                mm = nc.tensor.matmul(self.bank(self.s_ps, g)[:, j::GT], self.rowsb[:, g.slot, j, :], ident,
                                                      start=False, stop=True, skip_group_check=True)
                        else:
                            if k == "mlp":
                                self.targets(g, self.t_ps)
                            for j in range(GT):
                                mm = nc.tensor.transpose(self.bank(self.s_ps, g)[:, j::GT], self.rowsb[:, g.slot, j, :], ident)
                        mm.then_inc(sg.summed_e.sem, 1)
                return step, {"sum": 2, "max": 3, "mlp": 4}[k]

            def act(self, eng):
                sg, k = self.sg, self.kind

                def load_targets(g):
                    if g.from_(UNROLL):
                        eng.wait_ge(sg.rel_hot.sem, sg.rel_hot.after(g, UNROLL))
                    gate(eng, "act")
                    eng.dma_start(self.relb[:, g.slot, :], edgecols(relrow, g.g, WP)).then_inc(sg.targeted.sems[g.slot], 16)

                def results(t):
                    g = t.at(0) if self.spread else None
                    if g is not None:
                        if not g.known:
                            load_targets(Group(g.g + LEAD, g.turn + (g.slot + LEAD) // UNROLL, (g.slot + LEAD) % UNROLL, False))
                        else:
                            for e in range(0 if g.g == 0 else g.g + LEAD, min(g.g + LEAD, GROUPS - 1) + 1):
                                load_targets(Group(e, e // UNROLL, e % UNROLL, True))
                    g = t.at(3) if k == "mlp" and not self.scans else None
                    if g is not None:
                        eng.wait_ge(sg.msg_sb.sem, sg.msg_sb.after(g))
                        nc.scalar.activation(self.outb[:, g.slot], self.outb[:, g.slot], ACT.Relu).then_inc(sg.out_ready.sem, 1)
                    g = t.at({"sum": 2, "max": 3, "mlp": 4}[k]) if self.scans else None
                    if g is not None:
                        eng.wait_ge(sg.turned_e.sem, sg.turned_e.after(g))
                        if g.from_(UNROLL):
                            eng.wait_ge(sg.stored.sems[g.slot], sg.stored.after(g, 1, 1))
                        nc.scalar.copy(self.outb[:, g.slot], self.bank(self.o_ps, g)[:]).then_inc(sg.out_ready.sem, 1)
                    g = t.at(2 if k == "mlp" else 1) if self.scans and k != "sum" else None
                    if g is not None:
                        eng.wait_ge(sg.msg.sem, sg.msg.after(g))
                        if g.from_(2):
                            eng.wait_ge(sg.scanned.sem, sg.scanned.after(g, 2))
                        nc.scalar.activation(self.m_sb[:, g.pair, :], self.m_ps[:], ACT.Relu if k == "mlp" else ACT.Identity,
                                             bias=col("L3_gnn_msg_b2" if k == "mlp" else "L0_gnn_b2")).then_inc(sg.msg_sb.sem, 1)
                    g = t.at(1) if k == "mlp" else None
                    if g is not None:
                        eng.wait_ge(sg.hid_sum.sem, sg.hid_sum.after(g))
                        if g.from_(2):
                            eng.wait_ge(sg.msg.sem, sg.msg.after(g, 2))
                        nc.scalar.activation(self.hid[:, g.pair, :], self.hid_ps[:], ACT.Relu,
                                             bias=col("L3_gnn_msg_b1", HID)).then_inc(sg.hid_sb.sem, 1)

                def copies(t):
                    g = t.at(0) if k != "sum" or self.scans else None
                    if g is not None:
                        eng.wait_ge(sg.summed_e.sem, sg.summed_e.after(g))
                        h = self.h_sb[:, g.pair, :]
                        if k == "max":
                            if g.from_(2):
                                eng.wait_ge(sg.msg.sem, sg.msg.after(g, 2))
                            nc.scalar.activation(h, self.bank(self.s_ps, g)[:], ACT.Relu, bias=col("L0_gnn_b1")).then_inc(sg.hidden_e.sem, 1)
                        elif k == "sum":
                            if g.from_(2):
                                eng.wait_ge(sg.scanned.sem, sg.scanned.after(g, 2))
                            nc.scalar.copy(h, self.bank(self.s_ps, g)[:]).then_inc(sg.hidden_e.sem, 1)
                        else:
                            if g.from_(2):
                                eng.wait_ge(sg.hid_sum.sem, sg.hid_sum.after(g, 2))
                            nc.scalar.copy(self.t_sb[:, g.pair, :], self.t_ps[:]).then_inc(sg.tgt_sb.sem, 1)
                            nc.scalar.copy(h, self.bank(self.s_ps, g)[:]).then_inc(sg.hidden_e.sem, 1)

                def store(t):
                    g = t.at(self.store)
                    if g is not None:
                        if self.outb is self.rowsb:
                            eng.wait_ge(sg.fetched.sems[g.slot], sg.fetched.after(g, self.gathers))
                        else:
                            eng.wait_ge(sg.out_ready.sem, sg.out_ready.after(g))
                        eng.dma_start(edgerows(msgs[0:N, :], g.g)[:, :, 0:D], self.outb[:, g.slot]).then_inc(sg.stored.sems[g.slot], 16)
                return [(results, self.store), (copies, self.store), (store, self.store)]

            def dve(self, eng):
                sg, k, v = self.sg, self.kind, nc.vector
                if k == "sum" and not self.scans:
                    return None

                def step(t):
                    g = t.at(3) if k == "mlp" and not self.scans else None
                    if g is not None:
                        eng.wait_ge(sg.msg.sem, sg.msg.after(g))
                        if g.from_(UNROLL):
                            eng.wait_ge(sg.stored.sems[g.slot], sg.stored.after(g, 1, 1))
                        v.tensor_tensor(self.outb[:, g.slot], self.bank(self.o_ps, g)[:], row("L3_gnn_msg_b2"), ALU.add).then_inc(sg.msg_sb.sem, 1)
                    g = t.at(0) if self.spread else None
                    if g is not None:
                        eng.wait_ge(sg.targeted.sems[g.slot], sg.targeted.after(g, 1))
                        if g.from_(2):
                            eng.wait_ge(sg.summed_e.sem, sg.summed_e.after(g, 2))
                        for w in range(WK):
                            mm = v.tensor_scalar(self.hot[:, g.pair, w, :], self.relb[:, g.slot, :], pcol[0:WP, w:w + 1], None, ALU.is_equal)
                        mm.then_inc(sg.rel_hot.sem, 1)
                    g = t.at({"sum": 1, "max": 2, "mlp": 3}[k]) if self.scans else None
                    if g is not None:
                        of = sg.hidden_e if k == "sum" else sg.msg_sb
                        eng.wait_ge(of.sem, of.after(g))
                        eng.wait_ge(sg.landed.sems[g.slot], sg.landed.after(g, self.loads))
                        if g.from_(1):
                            eng.wait_ge(sg.scanned.sem, sg.scanned.after(g, 1))
                        if g.from_(2):
                            eng.wait_ge(sg.turned_e.sem, sg.turned_e.after(g, 2))
                        if not g.known or g.g > 0:
                            initial = self.sc[:, 1 - g.pair, GR - 1:GR]
                        else:
                            initial = 0.0
                        data = (self.h_sb if k == "sum" else self.m_sb)[:, g.pair, :]
                        ops = (ALU.add, ALU.max) if k == "max" else (ALU.mult, ALU.add)
                        v.tensor_tensor_scan(self.sc[:, g.pair, :], self.mask[:, g.slot, :], data, initial, *ops).then_inc(sg.scanned.sem, 1)
                return step, {"sum": 1, "max": 2, "mlp": 3}[k] if self.scans else 3

        def run(number, fast, general):
            used = {"fast": [fast], "general": [general], "both": [fast, general]}[mode]
            for n, passes in enumerate(used):
                with ExitStack() as memory:
                    for p, _ in passes:
                        p.buffers(lambda name, shape, dt=F32: memory.enter_context(nc.sbuf_tensor(f"r{number}_{n}_{name}", shape, dt))[:],
                                  lambda name, shape: memory.enter_context(nc.psum_tensor(f"r{number}_{n}_{name}", shape, F32)))

            def program(passes, of):
                if not passes:
                    return None

                def emit(eng):
                    parts = [(of(p, eng), lag) for p, lag in passes]
                    parts = [(part, lag) for part, lag in parts if part]
                    if parts and isinstance(parts[0][0], list):
                        parts = [(stages[k], lag) for k in range(3) for stages, lag in parts]
                    if not parts:
                        return

                    def step(t):
                        for (one, _), lag in parts:
                            one(t.later(lag))
                    steps(eng, step, max(own + lag for (_, own), lag in parts))
                return emit

            def stored(passes):
                go = program(passes[::-1], lambda p, e: p.act(e))
                if go is None:
                    return None

                def emit(eng):
                    go(eng)
                    for p, _ in passes:
                        p.sg.stored.wait_all(eng, p.stores, GROUPS)
                return emit

            def both(build_one):
                return build_one(fast), build_one(general)

            if not any(used):
                return
            with nc.Block() as block:
                @block.sync
                def _(sp):
                    either(sp, *both(lambda ps: program(ps, lambda p, e: p.sp(e))))

                @block.gpsimd
                def _(pool):
                    either(pool, *both(lambda ps: program(ps, lambda p, e: p.pool(e))))

                @block.tensor
                def _(pe):
                    either(pe, *both(lambda ps: program(ps[::-1], lambda p, e: p.pe(e))))

                @block.scalar
                def _(act):
                    either(act, *both(stored))

                @block.vector
                def _(dve):
                    either(dve, *both(lambda ps: program(ps, lambda p, e: p.dve(e))))
            for passes in used:
                for p, _ in passes:
                    p.sg.close(p.loads, p.gathers, p.stores)
                    if isinstance(p, NodePass) and p.own:
                        p.sg.close_own()
                    if isinstance(p, EdgePass) and p.spread:
                        p.sg.targeted.close(1, GROUPS)

        def layer(number, edge_kind, node_kind, qin, qout):
            tight = {"agg": 1, "tp": 1, "mp": 1, "s": 1, "o": 1} if edge_kind == "mlp" else \
                {"agg": 2, "tp": 1, "mp": 1, "s": 2, "o": 1} if edge_kind == "max" else WIDE
            fe = fn = ge = gn = None
            if mode != "general":
                fe = EdgePass(edge_kind, False, signals["fast_e"], qin, tight)
                fn = NodePass(node_kind, False, signals["fast_n"], qin, qout, tight, source=fe)
            if mode != "fast":
                ge = EdgePass(edge_kind, True, signals["general_e"], qin, WIDE if edge_kind != "mlp" else dict(WIDE, o=2))
                gn = NodePass(node_kind, True, signals["general_n"], qin, qout, WIDE)
            run(number, [(fe, 0), (fn, AHEAD + fe.store + SLACK)] if fe else [], [(ge, 0)] if ge else [])
            run(number + 1, [], [(gn, 0)] if gn else [])

        def nodes_only(number, kind, qout):
            on = {path: [(NodePass(kind, path == "general", signals[path + "_n"], None, qout, WIDE), 0)]
                  for path in ("fast", "general") if mode in (path, "both")}
            run(number, on.get("fast", []), on.get("general", []))

        def batch_norm():
            chain, rooted = bn_chain, bn_rooted
            with nc.Block() as block:
                @block.vector
                def _(dve):
                    n = [0]

                    def link(ins):
                        n[0] += 1
                        ins.then_inc(chain, 1)
                        dve.wait_ge(chain, n[0])
                    v = nc.vector
                    link(v.bn_aggr(bn[:, 0:2], stats.rearrange("p g s -> p (g s)")))
                    dve.wait_ge(rooted, 1)
                    link(v.reciprocal(bn[:, 3:4], bn[:, 2:3]))
                    link(v.tensor_tensor(bn[:, 4:5], bn[:, 3:4], col("L1_gnn_gamma"), ALU.mult))
                    link(v.tensor_tensor(bn[:, 6:7], bn[:, 4:5], bn[:, 0:1], ALU.mult))
                    link(v.tensor_tensor(bn[:, 5:6], col("L1_gnn_beta"), bn[:, 6:7], ALU.subtract))

                @block.scalar
                def _(act):
                    act.wait_ge(chain, 1)
                    nc.scalar.activation(bn[:, 2:3], bn[:, 1:2], ACT.Sqrt, bias=epsc[0:D, :]).then_inc(rooted, 1)

        SLACK = 5
        WIDE = {"agg": 2, "tp": 2, "mp": 2, "s": 2, "o": 2}
        signals = {}
        for path in ("fast", "general"):
            if mode in (path, "both"):
                signals[path + "_e"], signals[path + "_n"] = EdgeSignals(path + "_e"), NodeSignals(path + "_n")
        first = NodePass(0, False, signals["fast_n" if mode == "fast" else "general_n"], None, tabQ[0], WIDE)
        setup(first)
        first.sg.close(first.loads, first.gathers, first.stores)
        layer(2, "max", 1, tabQ[0], tabQ[1])
        layer(4, "sum", 2, tabQ[1], None)
        batch_norm()
        nodes_only(6, 3, tabQ[0])
        layer(7, "sum", 4, tabQ[0], tabQ[1])
        layer(9, "sum", 5, tabQ[1], tabQ[0])
        layer(11, "mlp", 6, tabQ[0], None)


MODE = "both"
NAMES = ["L0_gnn_W1", "L0_gnn_b1", "L0_gnn_W2", "L0_gnn_b2", "L1_gnn_W1", "L1_gnn_b1", "L1_gnn_gamma",
         "L1_gnn_beta", "L1_gnn_W2", "L1_gnn_b2", "L2_gnn_W", "L2_gnn_b", "L3_gnn_msg_W1", "L3_gnn_msg_b1",
         "L3_gnn_msg_W2", "L3_gnn_msg_b2", "L3_gnn_node_W1", "L3_gnn_node_b1", "L3_gnn_node_W2",
         "L3_gnn_node_b2", "L3_gnn_ln_scale", "L3_gnn_ln_offset"]


def kernel(**inputs):
    import numpy as _np
    import concourse.bacc as _bacc
    from concourse import mybir as _mybir
    from concourse.bass_utils import run_bass_kernel_spmd as _run

    nc = _bacc.Bacc("TRN2", target_bir_lowering=False, num_devices=1)
    arrays = {n: _np.ascontiguousarray(inputs[n]) for n in NAMES}
    more = N - N_TRUE
    for n in ("x", "edge_attr_64"):
        arrays[n] = _np.concatenate([_np.asarray(inputs[n]), _np.zeros((more, D), _np.float32)])
    arrays["src"] = _np.concatenate([_np.asarray(inputs["src"]), _np.zeros((more,), _np.int32)])
    arrays["dst"] = _np.concatenate([_np.full((1,), -1, _np.int32), _np.asarray(inputs["dst"]),
                                     _np.arange(N_TRUE, N + 1, dtype=_np.int32)])
    aps = {n: nc.dram_tensor(f"in_{n}", v.shape, _mybir.dt.from_np(v.dtype), kind="ExternalInput").ap()
           for n, v in arrays.items()}
    out = nc.dram_tensor("out", (N, D), F32, kind="ExternalOutput").ap()
    build(nc, MODE, aps, out)
    r = _run(nc, [{f"in_{n}": v for n, v in arrays.items()}], core_ids=[0])
    return r.results[0]["out"][:N_TRUE]
```
